# Optimizing a Trainium2 kernel written in Bass

```python
import numpy as np
import jax
import jax.numpy as jnp

def _softmax(x, axis=-1):
    return jax.nn.softmax(x, axis=axis)

def _gelu(x):
    return jax.nn.gelu(x, approximate=True)

def _silu(x):
    return jax.nn.silu(x)

def _sigmoid(x):
    return jax.nn.sigmoid(x)

def _layernorm(x, axis=-1, eps=1e-05):
    m = jnp.mean(x, axis=axis, keepdims=True)
    v = jnp.var(x, axis=axis, keepdims=True)
    return (x - m) / jnp.sqrt(v + eps)

def _scatter_add(tgt, idx, src, axis=0):
    return tgt.at[idx].add(src)

def _segment_sum(src, seg, n):
    return jax.ops.segment_sum(src, seg, n)
kernel_name = 'mk_sandwich_d2_jaxref_r8_790483'

def setup_inputs(seed: int=0):
    np.random.seed(seed)
    _w = jnp.asarray

    def _L0_attn_setup():
        import jax, jax.numpy as jnp
        import numpy as np
        HIDDEN = 512
        N_HEADS = 32
        N_KV = 8
        HEAD_DIM = HIDDEN // N_HEADS
        Q_PER_KV = N_HEADS // N_KV
        SEQ = 256
        ROPE_BASE = 1000000.0
        POS_SCALE = 1.0
        SM_SCALE = 1.0 / HEAD_DIM
        BLOCK = 64
        LOCAL_BLOCKS = 16
        VERT_STRIDE = 8

        def _blocksparse_mask(seq_len):
            nb = seq_len // BLOCK
            qb = np.arange(nb)[:, None]
            kb = np.arange(nb)[None, :]
            bmask = (kb <= qb) & ((qb - kb < LOCAL_BLOCKS) | ((kb + 1) % VERT_STRIDE == 0))
            emask = np.kron(bmask, np.ones((BLOCK, BLOCK), dtype=bool))
            i = np.arange(seq_len)
            emask &= i[:, None] >= i[None, :]
            return jnp.asarray(emask)

        def _rope(x, cos, sin):
            x1, x2 = jnp.split(x, 2, axis=-1)
            rot = jnp.concatenate([-x2, x1], axis=-1)
            return x * cos[None, :, None, :] + rot * sin[None, :, None, :]
        key = jax.random.key(seed)
        k1, k2, k3, k4, k5 = jax.random.split(key, 5)
        qkv_out = (N_HEADS + 2 * N_KV) * HEAD_DIM
        return {'hidden_states': jax.random.normal(k1, (1, SEQ, HIDDEN), dtype=jnp.float32), 'w_qkv': jax.random.normal(k2, (qkv_out, HIDDEN), dtype=jnp.float32) * 0.02, 'b_qkv': jnp.zeros((qkv_out,), dtype=jnp.float32), 'w_dense': jax.random.normal(k3, (HIDDEN, HIDDEN), dtype=jnp.float32) * 0.02, 'b_dense': jnp.zeros((HIDDEN,), dtype=jnp.float32)}
    _L0_attn_in = _L0_attn_setup()

    def _L0_ffn_setup():
        import jax, jax.numpy as jnp
        import numpy as np
        K_TOP = 8
        key = jax.random.key(seed)
        k1, k2, k3 = jax.random.split(key, 3)
        B, S, H, E = (4, 512, 512, 64)
        hidden_states = jax.random.normal(k1, (B, S, H), dtype=jnp.float32)
        router_weight = jax.random.normal(k2, (E, H), dtype=jnp.float32)
        router_bias = jnp.zeros((E,), dtype=jnp.float32)
        expert_bias = jax.random.normal(k3, (E, H), dtype=jnp.float32) * 0.1
        return {'hidden_states': hidden_states, 'router_weight': router_weight, 'router_bias': router_bias, 'expert_bias': expert_bias}
    _L0_ffn_in = _L0_ffn_setup()

    def _L1_attn_setup():
        import jax, jax.numpy as jnp
        import numpy as np
        N_HEADS = 32
        N_KV_HEADS = 8
        DIM = 512
        HEAD_DIM = DIM // N_HEADS
        N_REP = N_HEADS // N_KV_HEADS
        ROPE_THETA = 10000.0

        def _apply_rope(x):
            seq = x.shape[2]
            hd = x.shape[-1]
            inv_freq = 1.0 / ROPE_THETA ** (jnp.arange(0, hd, 2, dtype=jnp.float32) / hd)
            angles = jnp.arange(seq, dtype=jnp.float32)[:, None] * inv_freq[None, :]
            cos = jnp.cos(angles)[None, None]
            sin = jnp.sin(angles)[None, None]
            x1 = x[..., 0::2]
            x2 = x[..., 1::2]
            r1 = x1 * cos - x2 * sin
            r2 = x1 * sin + x2 * cos
            return jnp.stack([r1, r2], axis=-1).reshape(x.shape)
        key = jax.random.key(seed)
        k1, k2, k3 = jax.random.split(key, 3)
        bs, seq = (1, 256)
        x = jax.random.normal(k1, (bs, seq, DIM), dtype=jnp.float32)
        w_qkv = jax.random.normal(k2, (DIM, HEAD_DIM * (N_HEADS + 2 * N_KV_HEADS)), dtype=jnp.float32) * 0.02
        w_o = jax.random.normal(k3, (N_HEADS * HEAD_DIM, DIM), dtype=jnp.float32) * 0.02
        return {'x': x, 'w_qkv': w_qkv, 'w_o': w_o}
    _L1_attn_in = _L1_attn_setup()

    def _L1_ffn_setup():
        import jax, jax.numpy as jnp
        import numpy as np
        H = 512
        I = 256
        E = 16
        TOPK = 4
        SI = 256
        key = jax.random.key(seed)
        ks = jax.random.split(key, 9)
        s = 0.02
        return {'hidden_states': jax.random.normal(ks[0], (2, 256, H), dtype=jnp.float32), 'gate_w': jax.random.normal(ks[1], (E, H), dtype=jnp.float32) * s, 'bias': jnp.zeros((E,), dtype=jnp.float32), 'Wg': jax.random.normal(ks[2], (E, I, H), dtype=jnp.float32) * s, 'Wu': jax.random.normal(ks[3], (E, I, H), dtype=jnp.float32) * s, 'Wd': jax.random.normal(ks[4], (E, H, I), dtype=jnp.float32) * s, 'Sg': jax.random.normal(ks[5], (SI, H), dtype=jnp.float32) * s, 'Su': jax.random.normal(ks[6], (SI, H), dtype=jnp.float32) * s, 'Sd': jax.random.normal(ks[7], (H, SI), dtype=jnp.float32) * s}
    _L1_ffn_in = _L1_ffn_setup()
    _d = {'L0_attn_hidden_states': _L0_attn_in['hidden_states'], 'L0_attn_w_qkv': _L0_attn_in['w_qkv'], 'L0_attn_b_qkv': _L0_attn_in['b_qkv'], 'L0_attn_w_dense': _L0_attn_in['w_dense'], 'L0_attn_b_dense': _L0_attn_in['b_dense'], 'L0_ffn_router_weight': _L0_ffn_in['router_weight'], 'L0_ffn_router_bias': _L0_ffn_in['router_bias'], 'L0_ffn_expert_bias': _L0_ffn_in['expert_bias'], 'L1_attn_w_qkv': _L1_attn_in['w_qkv'], 'L1_attn_w_o': _L1_attn_in['w_o'], 'L1_ffn_gate_w': _L1_ffn_in['gate_w'], 'L1_ffn_bias': _L1_ffn_in['bias'], 'L1_ffn_Wg': _L1_ffn_in['Wg'], 'L1_ffn_Wu': _L1_ffn_in['Wu'], 'L1_ffn_Wd': _L1_ffn_in['Wd'], 'L1_ffn_Sg': _L1_ffn_in['Sg'], 'L1_ffn_Su': _L1_ffn_in['Su'], 'L1_ffn_Sd': _L1_ffn_in['Sd']}
    _x0 = _d['L0_attn_hidden_states']
    _d['L0_attn_hidden_states'] = jax.random.normal(jax.random.fold_in(jax.random.key(seed), 1), (1, 1024, 512), dtype=_x0.dtype)
    del _x0
    return _d

def reference(L0_attn_hidden_states, L0_attn_w_qkv, L0_attn_b_qkv, L0_attn_w_dense, L0_attn_b_dense, L0_ffn_router_weight, L0_ffn_router_bias, L0_ffn_expert_bias, L1_attn_w_qkv, L1_attn_w_o, L1_ffn_gate_w, L1_ffn_bias, L1_ffn_Wg, L1_ffn_Wu, L1_ffn_Wd, L1_ffn_Sg, L1_ffn_Su, L1_ffn_Sd):

    def _L0_attn_ref(hidden_states, w_qkv, b_qkv, w_dense, b_dense):
        import jax, jax.numpy as jnp
        import numpy as np
        HIDDEN = 512
        N_HEADS = 32
        N_KV = 8
        HEAD_DIM = HIDDEN // N_HEADS
        Q_PER_KV = N_HEADS // N_KV
        SEQ = 256
        ROPE_BASE = 1000000.0
        POS_SCALE = 1.0
        SM_SCALE = 1.0 / HEAD_DIM
        BLOCK = 64
        LOCAL_BLOCKS = 16
        VERT_STRIDE = 8

        def _blocksparse_mask(seq_len):
            nb = seq_len // BLOCK
            qb = np.arange(nb)[:, None]
            kb = np.arange(nb)[None, :]
            bmask = (kb <= qb) & ((qb - kb < LOCAL_BLOCKS) | ((kb + 1) % VERT_STRIDE == 0))
            emask = np.kron(bmask, np.ones((BLOCK, BLOCK), dtype=bool))
            i = np.arange(seq_len)
            emask &= i[:, None] >= i[None, :]
            return jnp.asarray(emask)

        def _rope(x, cos, sin):
            x1, x2 = jnp.split(x, 2, axis=-1)
            rot = jnp.concatenate([-x2, x1], axis=-1)
            return x * cos[None, :, None, :] + rot * sin[None, :, None, :]
        B, S, _ = hidden_states.shape
        qkv = jnp.einsum('bsh,oh->bso', hidden_states, w_qkv) + b_qkv
        qkv = qkv.reshape(B, S, N_KV, Q_PER_KV + 2, HEAD_DIM)
        q = qkv[:, :, :, :Q_PER_KV].reshape(B, S, N_HEADS, HEAD_DIM)
        k = qkv[:, :, :, Q_PER_KV]
        v = qkv[:, :, :, Q_PER_KV + 1]
        inv_freq = 1.0 / ROPE_BASE ** (jnp.arange(0, HEAD_DIM, 2, dtype=jnp.float32) / HEAD_DIM)
        t = jnp.arange(S, dtype=jnp.float32) * POS_SCALE
        freqs = jnp.outer(t, inv_freq)
        emb = jnp.concatenate([freqs, freqs], axis=-1)
        cos, sin = (jnp.cos(emb), jnp.sin(emb))
        q = _rope(q, cos, sin)
        k = _rope(k, cos, sin)
        k = jnp.repeat(k, Q_PER_KV, axis=2)
        v = jnp.repeat(v, Q_PER_KV, axis=2)
        mask = _blocksparse_mask(S)
        scores = jnp.einsum('bqhd,bkhd->bhqk', q, k) * SM_SCALE
        scores = jnp.where(mask[None, None], scores, jnp.finfo(scores.dtype).min)
        probs = jax.nn.softmax(scores, axis=-1)
        ctx = jnp.einsum('bhqk,bkhd->bqhd', probs, v).reshape(B, S, HIDDEN)
        out = jnp.einsum('bsh,oh->bso', ctx, w_dense) + b_dense
        return out

    def _L0_ffn_ref(hidden_states, router_weight, router_bias, expert_bias):
        import jax, jax.numpy as jnp
        import numpy as np
        K_TOP = 8
        B, S, H = hidden_states.shape
        E = router_weight.shape[0]
        T = B * S
        flat = hidden_states.reshape(T, H)
        logits = jnp.einsum('th,eh->te', flat, router_weight) + router_bias
        scores = jax.nn.softmax(logits, axis=-1)
        topk_w, topk_idx = jax.lax.top_k(scores, K_TOP)
        w_sum = topk_w.sum(axis=-1, keepdims=True)
        w_dense = jnp.zeros((T, E), dtype=scores.dtype).at[jnp.arange(T)[:, None], topk_idx].add(topk_w)
        bias_mix = jnp.einsum('te,eh->th', w_dense, expert_bias)
        out = flat * w_sum + bias_mix
        return out.reshape(B, S, H)

    def _L1_attn_ref(x, w_qkv, w_o):
        import jax, jax.numpy as jnp
        import numpy as np
        N_HEADS = 32
        N_KV_HEADS = 8
        DIM = 512
        HEAD_DIM = DIM // N_HEADS
        N_REP = N_HEADS // N_KV_HEADS
        ROPE_THETA = 10000.0

        def _apply_rope(x):
            seq = x.shape[2]
            hd = x.shape[-1]
            inv_freq = 1.0 / ROPE_THETA ** (jnp.arange(0, hd, 2, dtype=jnp.float32) / hd)
            angles = jnp.arange(seq, dtype=jnp.float32)[:, None] * inv_freq[None, :]
            cos = jnp.cos(angles)[None, None]
            sin = jnp.sin(angles)[None, None]
            x1 = x[..., 0::2]
            x2 = x[..., 1::2]
            r1 = x1 * cos - x2 * sin
            r2 = x1 * sin + x2 * cos
            return jnp.stack([r1, r2], axis=-1).reshape(x.shape)
        bs, seq, _ = x.shape
        qkv = x @ w_qkv
        q_sz = N_HEADS * HEAD_DIM
        kv_sz = N_KV_HEADS * HEAD_DIM
        xq = qkv[..., :q_sz].reshape(bs, seq, N_HEADS, HEAD_DIM).transpose(0, 2, 1, 3)
        xk = qkv[..., q_sz:q_sz + kv_sz].reshape(bs, seq, N_KV_HEADS, HEAD_DIM).transpose(0, 2, 1, 3)
        xv = qkv[..., q_sz + kv_sz:].reshape(bs, seq, N_KV_HEADS, HEAD_DIM).transpose(0, 2, 1, 3)
        xq = _apply_rope(xq)
        xk = _apply_rope(xk)
        keys = jnp.repeat(xk, N_REP, axis=1)
        values = jnp.repeat(xv, N_REP, axis=1)
        scale = 1.0 / jnp.sqrt(jnp.float32(HEAD_DIM))
        scores = jnp.einsum('bhsd,bhtd->bhst', xq, keys) * scale
        causal = jnp.tril(jnp.ones((seq, seq), dtype=bool))[None, None]
        scores = jnp.where(causal, scores, -jnp.inf)
        probs = jax.nn.softmax(scores, axis=-1)
        out = jnp.einsum('bhst,bhtd->bhsd', probs, values)
        out = out.transpose(0, 2, 1, 3).reshape(bs, seq, N_HEADS * HEAD_DIM)
        return out @ w_o

    def _L1_ffn_ref(hidden_states, gate_w, bias, Wg, Wu, Wd, Sg, Su, Sd):
        import jax, jax.numpy as jnp
        import numpy as np
        H = 512
        I = 256
        E = 16
        TOPK = 4
        SI = 256
        orig_shape = hidden_states.shape
        x = hidden_states.reshape(-1, orig_shape[-1])
        scores = jax.nn.sigmoid(x @ gate_w.T) + bias
        topk_w, topk_idx = jax.lax.top_k(scores, TOPK)
        topk_w = topk_w / (jnp.sum(topk_w, axis=-1, keepdims=True) + 1e-20)
        cw = jnp.sum(jax.nn.one_hot(topk_idx, E, dtype=x.dtype) * topk_w[..., None], axis=1)
        g = jnp.einsum('th,eih->eti', x, Wg)
        u = jnp.einsum('th,eih->eti', x, Wu)
        z = jax.nn.silu(g) * u
        zw = z * cw.T[:, :, None]
        out = jnp.einsum('eti,ehi->th', zw, Wd)
        out = out + jax.nn.silu(x @ Sg.T) * (x @ Su.T) @ Sd.T
        return out.reshape(orig_shape)
    x = L0_attn_hidden_states
    x = x + _layernorm(_L0_attn_ref(_layernorm(x, axis=-1), L0_attn_w_qkv, L0_attn_b_qkv, L0_attn_w_dense, L0_attn_b_dense), axis=-1)
    x = x + _layernorm(_L0_ffn_ref(_layernorm(x, axis=-1), L0_ffn_router_weight, L0_ffn_router_bias, L0_ffn_expert_bias), axis=-1)
    x = x + _layernorm(_L1_attn_ref(_layernorm(x, axis=-1), L1_attn_w_qkv, L1_attn_w_o), axis=-1)
    x = x + _layernorm(_L1_ffn_ref(_layernorm(x, axis=-1), L1_ffn_gate_w, L1_ffn_bias, L1_ffn_Wg, L1_ffn_Wu, L1_ffn_Wd, L1_ffn_Sg, L1_ffn_Su, L1_ffn_Sd), axis=-1)
    return x

_drawn_inputs = setup_inputs


def setup_inputs(seed=0):
    import zlib

    import numpy as np

    out = dict(_drawn_inputs(seed))
    spreads = {'L0_attn_b_qkv': (0.0, 0.1),
     'L0_attn_b_dense': (0.0, 0.1),
     'L0_ffn_router_bias': (0.0, 0.1),
     'L1_ffn_bias': (0.0, 0.1)}
    factors = {}
    for name, (base, spread) in spreads.items():
        noise = np.random.default_rng([zlib.crc32(name.encode()), seed]).standard_normal(out[name].shape)
        drawn = base * np.exp(spread * noise) if base else spread * noise
        out[name] = jnp.asarray(drawn.astype(out[name].dtype))
    for name, factor in factors.items():
        out[name] = (out[name] * factor).astype(out[name].dtype)
    return out
```

```python
from contextlib import ExitStack

import numpy as np

import concourse.bass as bass
from concourse import mybir

F32 = mybir.dt.float32
F32R = mybir.dt.float32r
BF16 = mybir.dt.bfloat16
ALU = mybir.AluOpType
ACT = mybir.ActivationFunctionType
AX = mybir.AxisListType

P = 128
S = 1024
H = 512
NB = S // P
KC = H // P
HD = 16
NH, NKV = 32, 8
REP = NH // NKV
QW = NH * HD
KW = NKV * HD
QKV = QW + 2 * KW
QK_HEADS = NH + NKV
SLOTS = 6
STACK = SLOTS * HD
MROWS = 3
VW = 32
E0, TOP0 = 64, 8
E1, TOP1 = 16, 4
I1 = 256
EPS = 1e-5
NEG = -1e30
SCALES = (1.0 / HD, 1.0 / 4.0)


class Buffers:

    def __init__(self, nc, ctx, prefix=""):
        self.nc, self.ctx, self.prefix = nc, ctx, prefix
        self.semaphores = []
        ctx.callback(self.clear)

    def clear(self):
        self.nc.clear_and_free_semaphores(self.semaphores)
        self.nc.all_engine_barrier()

    def sb(self, name, shape, dt=F32):
        return self.ctx.enter_context(self.nc.sbuf_tensor(self.prefix + name, shape, dt))

    def ps(self, name, shape, dt=F32):
        return self.ctx.enter_context(self.nc.psum_tensor(self.prefix + name, shape, dt))

    def sem(self, name):
        self.semaphores.append(self.nc.alloc_semaphore(self.prefix + name))
        return self.semaphores[-1]


def apart(engine):
    engine.nop(nofuse=True)


def one(ap_of_blocks, i):
    return ap_of_blocks[:, bass.ds(i, 1), :].rearrange("p a w -> p (a w)")


def row_phase(nc, name, const, attn, io, after=None, ffn=False, before=None, moe=None):
    x, ident, identb, ones_row, neg_half = (const[k] for k in ("x", "ident", "identb", "ones_row", "neg_half"))
    with ExitStack() as ctx:
        b = Buffers(nc, ctx, name)
        sem = b.sem
        norms = {}

        def norm_set(k):
            norms[k] = dict(
                stats=b.sb(f"st_{k}", [P, 6]), mv=b.sb(f"mv_{k}", [P, 2]), ve=b.sb(f"ve_{k}", [P, 1]),
                rstd=b.sb(f"rstd_{k}", [P, 1]), s_stats=sem(f"s_stats_{k}"), s_mv=sem(f"s_mv_{k}"),
                s_ve=sem(f"s_ve_{k}"), s_rstd=sem(f"s_rstd_{k}"), s_out=sem(f"s_out_{k}"))

        s_load = sem("s_load")
        s_x = sem("s_x")
        n_load = 0
        psT = b.ps("psT", [P, KC, P])
        s_dve = {}
        y = b.sb("y", [P, H])
        if after is not None:
            norm_set("d")
            wd_raw = b.sb("wd_raw", [P, KC, H])
            wd_hi, wd_lo = b.sb("wd_hi", [P, KC, H], F32R), b.sb("wd_lo", [P, KC, H], F32R)
            bd = b.sb("bd", [1, H]) if after == 0 else None
            ctx_raw = b.sb("ctx_raw", [P, KC, P])
            ctx_hi, ctx_lo = b.sb("ctx_hi", [P, KC, P], F32R), b.sb("ctx_lo", [P, KC, P], F32R)
            psD = b.ps("psD", [P, H])
            s_wd_hi, s_wd, s_ctx, s_ctx_hi, s_ctx_lo, s_proj, s_xd = map(
                sem, ("s_wd_hi", "s_wd", "s_ctx", "s_ctx_hi", "s_ctx_lo", "s_proj", "s_xd"))
        if ffn:
            norm_set("f")
            norm_set("g")
            rw = b.sb("rw", [P, KC, E0])
            rb = b.sb("rb", [1, E0])
            eb = b.sb("eb", [E0, H])
            h = b.sb("h", [P, H])
            hT = b.sb("hT", [P, KC, P])
            mx8, top8 = b.sb("mx8", [P, 8]), b.sb("top8", [P, 8])
            nmx, sm, rs, wsum = (b.sb(n, [P, 1]) for n in ("nmx", "sm", "rs", "wsum"))
            pe_, pn, pr, w = (b.sb(n, [P, E0]) for n in ("pe_", "pn", "pr", "w"))
            wT = b.sb("wT", [E0, P])
            o0 = b.sb("o0", [P, H])
            psL = b.ps("psL", [P, P])
            psM = b.ps("psM", [P, H])
            (s_hTp, s_hT, s_logit, s_mx8, s_nmx, s_exp, s_rs, s_pn, s_top8, s_pr, s_w, s_wTp, s_wT, s_mix, s_o0,
             s_xf) = map(sem, ("s_hTp", "s_hT", "s_logit", "s_mx8", "s_nmx", "s_exp", "s_rs", "s_pn", "s_top8",
                               "s_pr", "s_w", "s_wTp", "s_wT", "s_mix", "s_o0", "s_xf"))
        if before is not None:
            norm_set("a")
            wq_raw = b.sb("wq_raw", [P, QKV])
            wq_hi, wq_lo = b.sb("wq_hi", [P, KC, QKV], F32R), b.sb("wq_lo", [P, KC, QKV], F32R)
            bq = b.sb("bq", [1, QKV]) if before == 0 else None
            n_hi, n_lo = b.sb("n_hi", [P, KC, P], F32R), b.sb("n_lo", [P, KC, P], F32R)
            cos, sin = b.sb("cos", [P, NB, HD]), b.sb("sin", [P, NB, HD])
            rc, rs_, qr, r1 = (b.sb(n, [P, QK_HEADS, HD]) for n in ("rc", "rs_", "qr", "r1"))
            stack = b.sb("stack", [P, QK_HEADS, SLOTS, HD], BF16)
            psQ = b.ps("psQ", [P, 1024])
            psS = [b.ps(f"psS{n}", [P, 8, P], BF16) for n in range(2)]
            (s_wq_raw, s_wq_hi, s_wq, s_nTp, s_n_hi, s_n_lo, s_qkv, s_rc, s_qr, s_v, s_sth, s_r1, s_r2, s_stack,
             s_stp, s_ste_act, s_ste_dve) = map(
                sem, ("s_wq_raw", "s_wq_hi", "s_wq", "s_nTp", "s_n_hi", "s_n_lo", "s_qkv", "s_rc", "s_qr", "s_v",
                      "s_sth", "s_r1", "s_r2", "s_stack", "s_stp", "s_ste_act", "s_ste_dve"))
        if moe is not None:
            norm_set("m")
            gw = b.sb("gw", [P, KC, E1])
            gb = b.sb("gb", [P, E1])
            nT = b.sb("nT", [P, KC, P])
            psG = b.ps("psG", [P, E1])
            ge, gd, sg, gm, gc = (b.sb(n, [P, E1]) for n in ("ge", "gd", "sg", "gm", "gc"))
            s20, g20 = b.sb("s20", [P, E1 + 4]), b.sb("g20", [P, E1 + 4])
            g8, rep8 = b.sb("g8", [P, 8]), b.sb("rep8", [P, 8])
            gsum, gden, grec = (b.sb(n, [P, 1]) for n in ("gsum", "gden", "grec"))
            (s_pre, s_mTp, s_mT, s_mhi, s_mlo, s_glog, s_ge, s_gd, s_sg, s_s20, s_g8, s_rep, s_g20, s_gm, s_gc, s_gsum,
             s_gden, s_grec, s_cw) = map(
                sem, ("s_pre", "s_mTp", "s_mT", "s_mhi", "s_mlo", "s_glog", "s_ge", "s_gd", "s_sg", "s_s20", "s_g8",
                      "s_rep", "s_g20", "s_gm", "s_gc", "s_gsum", "s_gden", "s_grec", "s_cw"))

        loads = []
        if after is not None:
            loads += [(wd_raw[:], io[f"wd{after}"])] + ([(bd[:], io["bd"])] if after == 0 else [])
        if ffn:
            loads += [(rw[:], io["rw"]), (rb[:], io["rb"]), (eb[:], io["eb"])]
        if before is not None:
            loads += [(cos[:], io[f"cos{before}"]), (sin[:], io[f"sin{before}"])]
            loads += [(bq[:], io["bq"])] if before == 0 else []
        if moe is not None:
            loads += [(gw[:], io["gw"]), (gb[:], io["gb"])]

        block = ctx.enter_context(nc.Block())

        @block.sync
        def _(sp):
            for dst, src in loads:
                sp.dma_start(dst, src).then_inc(s_load, 16)
            if before == 0:
                sp.dma_start(x[:], io["x"]).then_inc(s_x, 16)
            if before is not None:
                for k in range(KC):
                    if k:
                        sp.wait_ge(s_wq, k)
                    sp.dma_start(wq_raw[:], io[f"wq{before}"][:, k, :]).then_inc(s_wq_raw, 16)
            if after is not None:
                with sp.Fori(0, NB) as i:
                    sp.dma_start(ctx_raw[:], io["ctx_read"][:, :, bass.ds(i * P, P)]).then_inc(s_ctx, 16)
                    sp.wait_ge(s_ctx_lo, i + 1)
                    apart(sp)

        @block.scalar
        def _(act):
            act.wait_ge(s_load, 16 * len(loads))
            if after is not None:
                nc.scalar.copy(wd_hi[:], wd_raw[:]).then_inc(s_wd_hi, 1)
            if before is not None:
                for k in range(KC):
                    act.wait_ge(s_wq_raw, 16 * (k + 1))
                    nc.scalar.copy(wq_hi[:, k, :], wq_raw[:]).then_inc(s_wq_hi, 1)
            with act.Fori(0, NB) as i:
                if after is not None:
                    act.wait_ge(s_ctx, 16 * i + 16)
                    nc.scalar.copy(ctx_hi[:], ctx_raw[:]).then_inc(s_ctx_hi, 1)
                if ffn:
                    act.wait_ge(s_hTp, i + 1)
                    nc.scalar.copy(hT[:], psT[:]).then_inc(s_hT, 1)
                    act.wait_ge(s_nmx, i + 1)
                    nc.scalar.activation(pe_[:], psL[:, 0:E0], ACT.Exp, bias=nmx[:, 0:1],
                                         accum_out=sm[:, 0:1]).then_inc(s_exp, 1)
                    act.wait_ge(s_wTp, i + 1)
                    nc.scalar.copy(wT[:], psL[0:E0, :]).then_inc(s_wT, 1)
                if before is not None:
                    act.wait_ge(s_nTp, i + 1)
                    nc.scalar.copy(n_hi[:], psT[:]).then_inc(s_n_hi, 1)
                    act.wait_ge(s_qkv, i + 1)
                    v_out = attn["v"][:, bass.ds(i, 1), :, 0:HD].rearrange("p a g d -> p (a g) d")
                    act.wait_ge(s_qr, i + 1)
                    nc.scalar.copy(v_out, psQ[:, QW + KW:QKV].rearrange("p (g d) -> p g d", d=HD)).then_inc(s_v, 1)
                    nc.scalar.copy(stack[:, 0:NH, 0:3, :],
                                   qr[:, 0:NH, :].unsqueeze(2).to_broadcast([P, NH, 3, HD])).then_inc(s_sth, 1)
                    nc.scalar.copy(stack[:, NH:, 0, :], qr[:, NH:, :]).then_inc(s_sth, 1)
                    nc.scalar.copy(stack[:, NH:, 4:6, :],
                                   qr[:, NH:, :].unsqueeze(2).to_broadcast([P, NKV, 2, HD])).then_inc(s_sth, 1)
                    act.wait_ge(s_r1, i + 1)
                    nc.scalar.copy(stack[:, 0:NH, 3:5, :],
                                   r1[:, 0:NH, :].unsqueeze(2).to_broadcast([P, NH, 2, HD])).then_inc(s_sth, 1)
                    nc.scalar.copy(stack[:, NH:, 2:4, :],
                                   r1[:, NH:, :].unsqueeze(2).to_broadcast([P, NKV, 2, HD])).then_inc(s_sth, 1)
                    act.wait_ge(s_r2, i + 1)
                    nc.scalar.copy(stack[:, 0:NH, 5, :], qr[:, 0:NH, :]).then_inc(s_stack, 1)
                    nc.scalar.copy(stack[:, NH:, 1, :], qr[:, NH:, :]).then_inc(s_stack, 1)
                    for u in range(1, QK_HEADS // 8, 2):
                        act.wait_ge(s_stp, i * (QK_HEADS // 8) + u + 1)
                        nc.scalar.copy(attn["q"][0:STACK, 8 * u:8 * u + 8, bass.ds(i * P, P)],
                                       psS[u % 2][0:STACK, :, :]).then_inc(s_ste_act, 1)
                if moe is not None:
                    act.wait_ge(s_mTp, i + 1)
                    nc.scalar.copy(nT[:], psT[:]).then_inc(s_mT, 1)
                    act.wait_ge(s_mT, i + 1)
                    nc.scalar.copy(moe["hi"][:, :, bass.ds(i * P, P)], nT[:]).then_inc(s_mhi, 1)
                    act.wait_ge(s_glog, i + 1)
                    nc.scalar.activation(ge[:], psG[:], ACT.Exp, scale=-1.0).then_inc(s_ge, 1)

        @block.gpsimd
        def _(pool):
            def rstd(k, i):
                n = norms[k]
                pool.wait_ge(n["s_mv"], i + 1)
                apart(pool)
                nc.gpsimd.tensor_scalar(n["ve"][:], n["mv"][:, 1:2], EPS, 1.0, ALU.add, ALU.mult).then_inc(n["s_ve"], 1)
                pool.wait_ge(n["s_ve"], i + 1)
                nc.gpsimd.tensor_tensor(n["rstd"][:], n["ve"][:], neg_half[:], ALU.pow).then_inc(n["s_rstd"], 1)

            if before is not None:
                nc.gpsimd.memset(attn["v"][:], 1.0).then_inc(s_v, 1)
            if moe is not None:
                nc.gpsimd.memset(s20[:, E1:], NEG).then_inc(s_pre, 1)
                nc.gpsimd.memset(rep8[:, TOP1:], NEG).then_inc(s_pre, 1)
            with pool.Fori(0, NB) as i:
                for k in [k for k in "dfgam" if k in norms]:
                    rstd(k, i)

        @block.vector
        def _(dve):
            def stats(k, src, i):
                n = norms[k]
                apart(dve)
                nc.vector.bn_stats(n["stats"][:], src).then_inc(n["s_stats"], 1)
                dve.wait_ge(n["s_stats"], i + 1)
                apart(dve)
                nc.vector.bn_aggr(n["mv"][:], n["stats"][:]).then_inc(n["s_mv"], 1)

            def apply(k, out, src, i):
                n = norms[k]
                dve.wait_ge(n["s_rstd"], i + 1)
                nc.vector.tensor_scalar(out, src, n["mv"][:, 0:1], n["rstd"][:, 0:1], ALU.subtract,
                                        ALU.mult).then_inc(n["s_out"], 1)

            if after is not None:
                dve.wait_ge(s_load, 16 * len(loads))
                dve.wait_ge(s_wd_hi, 1)
                nc.vector.tensor_tensor(wd_lo[:], wd_raw[:], wd_hi[:].bitcast(F32), ALU.subtract).then_inc(s_wd, 1)
            if before is not None:
                for k in range(KC):
                    dve.wait_ge(s_wq_hi, k + 1)
                    nc.vector.tensor_tensor(wq_lo[:, k, :], wq_raw[:], wq_hi[:, k, :].bitcast(F32),
                                            ALU.subtract).then_inc(s_wq, 1)
            if before == 0:
                dve.wait_ge(s_x, 16)
            if ffn or before is not None:
                dve.wait_ge(s_load, 16 * len(loads))
            if before is not None:
                dve.wait_ge(s_v, 1)
            if moe is not None:
                dve.wait_ge(s_load, 16 * len(loads))
                dve.wait_ge(s_pre, 2)
            with dve.Fori(0, NB) as i:
                xi = one(x, i)
                if after is not None:
                    dve.wait_ge(s_ctx_hi, i + 1)
                    nc.vector.tensor_tensor(ctx_lo[:], ctx_raw[:], ctx_hi[:].bitcast(F32),
                                            ALU.subtract).then_inc(s_ctx_lo, 1)
                    dve.wait_ge(s_proj, i + 1)
                    stats("d", psD[:], i)
                    apply("d", y[:], psD[:], i)
                    dve.wait_ge(norms["d"]["s_out"], i + 1)
                    nc.vector.tensor_tensor(xi, xi, y[:], ALU.add).then_inc(s_xd, 1)
                    dve.wait_ge(s_xd, i + 1)
                if ffn:
                    stats("f", xi, i)
                    apply("f", h[:], xi, i)
                    dve.wait_ge(s_logit, i + 1)
                    apart(dve)
                    nc.vector.max(mx8[:], psL[:, 0:E0]).then_inc(s_mx8, 1)
                    dve.wait_ge(s_mx8, i + 1)
                    nc.vector.tensor_scalar(nmx[:], mx8[:, 0:1], -1.0, None, ALU.mult).then_inc(s_nmx, 1)
                    dve.wait_ge(s_exp, i + 1)
                    nc.vector.reciprocal(rs[:], sm[:]).then_inc(s_rs, 1)
                    dve.wait_ge(s_rs, i + 1)
                    nc.vector.tensor_scalar(pn[:], pe_[:], rs[:, 0:1], None, ALU.mult).then_inc(s_pn, 1)
                    dve.wait_ge(s_pn, i + 1)
                    apart(dve)
                    nc.vector.max(top8[:], pn[:]).then_inc(s_top8, 1)
                    dve.wait_ge(s_top8, i + 1)
                    apart(dve)
                    nc.vector.match_replace(pr[:], top8[:], pn[:], 0.0).then_inc(s_pr, 1)
                    nc.vector.reduce_sum(wsum[:], top8[:], AX.X).then_inc(s_pr, 1)
                    dve.wait_ge(s_pr, 2 * i + 2)
                    nc.vector.tensor_tensor(w[:], pn[:], pr[:], ALU.subtract).then_inc(s_w, 1)
                    dve.wait_ge(s_mix, i + 1)
                    nc.vector.scalar_tensor_tensor(out=o0[:], in0=h[:], scalar=wsum[:, 0:1], in1=psM[:],
                                                   op0=ALU.mult, op1=ALU.add).then_inc(s_o0, 1)
                    dve.wait_ge(s_o0, i + 1)
                    stats("g", o0[:], i)
                    apply("g", y[:], o0[:], i)
                    dve.wait_ge(norms["g"]["s_out"], i + 1)
                    nc.vector.tensor_tensor(xi, xi, y[:], ALU.add).then_inc(s_xf, 1)
                    dve.wait_ge(s_xf, i + 1)
                if before is not None:
                    stats("a", xi, i)
                    apply("a", y[:], xi, i)
                    dve.wait_ge(s_n_hi, i + 1)
                    nc.vector.tensor_tensor(n_lo[:], psT[:], n_hi[:].bitcast(F32), ALU.subtract).then_inc(s_n_lo, 1)
                    dve.wait_ge(s_qkv, i + 1)
                    qk = psQ[:, 0:QW + KW].rearrange("p (h d) -> p h d", d=HD)
                    ci = cos[:, bass.ds(i, 1), :].to_broadcast([P, QK_HEADS, HD])
                    nc.vector.tensor_tensor(rc[:], qk, ci, ALU.mult).then_inc(s_rc, 1)
                    for half in range(2):
                        lo, hi = half * HD // 2, (half + 1) * HD // 2
                        si = sin[:, bass.ds(i, 1), lo:hi].to_broadcast([P, QK_HEADS, HD // 2])
                        nc.vector.tensor_tensor(rs_[:, :, lo:hi], qk[:, :, HD // 2 - lo:HD - lo], si,
                                                ALU.mult).then_inc(s_rc, 1)
                    dve.wait_ge(s_rc, 3 * i + 3)
                    nc.vector.tensor_tensor(qr[:], rc[:], rs_[:], ALU.add).then_inc(s_qr, 1)
                    dve.wait_ge(s_sth, 5 * i + 3)
                    nc.vector.tensor_tensor(r1[:], qr[:], stack[:, :, 0, :], ALU.subtract).then_inc(s_r1, 1)
                    dve.wait_ge(s_sth, 5 * i + 5)
                    nc.vector.tensor_tensor(qr[:], r1[:], stack[:, :, 3, :], ALU.subtract).then_inc(s_r2, 1)
                    for u in range(0, QK_HEADS // 8, 2):
                        dve.wait_ge(s_stp, i * (QK_HEADS // 8) + u + 1)
                        dst = attn["q"] if u < NH // 8 else attn["k"]
                        h0 = 8 * u if u < NH // 8 else 0
                        nc.vector.tensor_copy(dst[0:STACK, h0:h0 + 8, bass.ds(i * P, P)],
                                              psS[u % 2][0:STACK, :, :]).then_inc(s_ste_dve, 1)
                if moe is not None:
                    stats("m", xi, i)
                    apply("m", y[:], xi, i)
                    dve.wait_ge(s_mhi, i + 1)
                    nc.vector.tensor_tensor(moe["lo"][:, :, bass.ds(i * P, P)], nT[:],
                                            moe["hi"][:, :, bass.ds(i * P, P)].bitcast(F32),
                                            ALU.subtract).then_inc(s_mlo, 1)
                    dve.wait_ge(s_ge, i + 1)
                    nc.vector.tensor_scalar(gd[:], ge[:], 1.0, None, ALU.add).then_inc(s_gd, 1)
                    dve.wait_ge(s_gd, i + 1)
                    nc.vector.reciprocal(sg[:], gd[:]).then_inc(s_sg, 1)
                    dve.wait_ge(s_sg, i + 1)
                    nc.vector.tensor_tensor(s20[:, 0:E1], sg[:], gb[:], ALU.add).then_inc(s_s20, 1)
                    dve.wait_ge(s_s20, i + 1)
                    apart(dve)
                    nc.vector.max(g8[:], s20[:]).then_inc(s_g8, 1)
                    dve.wait_ge(s_g8, i + 1)
                    nc.vector.tensor_copy(rep8[:, 0:TOP1], g8[:, 0:TOP1]).then_inc(s_rep, 1)
                    dve.wait_ge(s_rep, i + 1)
                    apart(dve)
                    nc.vector.match_replace(g20[:], rep8[:], s20[:], -3e38).then_inc(s_g20, 1)
                    nc.vector.reduce_sum(gsum[:], g8[:, 0:TOP1], AX.X).then_inc(s_gsum, 1)
                    dve.wait_ge(s_g20, i + 1)
                    nc.vector.tensor_scalar(gm[:], g20[:, 0:E1], -2e38, None, ALU.is_le).then_inc(s_gm, 1)
                    dve.wait_ge(s_gm, i + 1)
                    nc.vector.tensor_tensor(gc[:], gm[:], s20[:, 0:E1], ALU.mult).then_inc(s_gc, 1)
                    dve.wait_ge(s_gsum, i + 1)
                    nc.vector.tensor_scalar(gden[:], gsum[:], 1e-20, None, ALU.add).then_inc(s_gden, 1)
                    dve.wait_ge(s_gden, i + 1)
                    nc.vector.reciprocal(grec[:], gden[:]).then_inc(s_grec, 1)
                    dve.wait_ge(s_grec, i + 1)
                    dve.wait_ge(s_gc, i + 1)
                    nc.vector.tensor_scalar(one(moe["cw"], i), gc[:], grec[:, 0:1], None, ALU.mult).then_inc(s_cw, 1)

        @block.tensor
        def _(pe):
            def split_product(out, a_hi, a_lo, w_hi, w_lo, chunks, open_group=True):
                for k in range(chunks):
                    for m, (a, wt) in enumerate(((a_hi, w_hi), (a_hi, w_lo), (a_lo, w_hi))):
                        last = nc.tensor.matmul(out, a[:, k, :], wt[:, k, :], start=open_group and k == 0 and m == 0,
                                                stop=(k == chunks - 1 and m == 2))
                return last

            pe.wait_ge(s_load, 16 * len(loads))
            if after is not None:
                pe.wait_ge(s_wd, 1)
            if before is not None:
                pe.wait_ge(s_wq, KC)
            with pe.Fori(0, NB) as i:
                if after is not None:
                    pe.wait_ge(s_ctx_lo, i + 1)
                    if after == 0:
                        nc.tensor.matmul(psD[:], ones_row[0:1, :], bd[:], start=True, stop=False)
                    split_product(psD[:], ctx_hi, ctx_lo, wd_hi, wd_lo, KC, after != 0).then_inc(s_proj, 1)
                if ffn:
                    pe.wait_ge(norms["f"]["s_out"], i + 1)
                    for k in range(KC):
                        last = nc.tensor.transpose(psT[:, k, :], h[:, k * P:(k + 1) * P], ident[:])
                    last.then_inc(s_hTp, 1)
                    pe.wait_ge(s_hT, i + 1)
                    nc.tensor.matmul(psL[:, 0:E0], ones_row[0:1, :], rb[:], start=True, stop=False)
                    for k in range(KC):
                        last = nc.tensor.matmul(psL[:, 0:E0], hT[:, k, :], rw[:, k, :], start=False,
                                                stop=(k == KC - 1))
                    last.then_inc(s_logit, 1)
                    pe.wait_ge(s_w, i + 1)
                    apart(pe)
                    nc.tensor.transpose(psL[0:E0, :], w[:], ident[:]).then_inc(s_wTp, 1)
                    pe.wait_ge(s_wT, i + 1)
                    nc.tensor.matmul(psM[:], wT[:], eb[:], start=True, stop=True).then_inc(s_mix, 1)
                if before is not None:
                    pe.wait_ge(norms["a"]["s_out"], i + 1)
                    for k in range(KC):
                        last = nc.tensor.transpose(psT[:, k, :], y[:, k * P:(k + 1) * P], ident[:])
                    last.then_inc(s_nTp, 1)
                    pe.wait_ge(s_n_lo, i + 1)
                    for c0, c1 in ((0, QW), (QW, QKV)):
                        if before == 0:
                            nc.tensor.matmul(psQ[:, c0:c1], ones_row[0:1, :], bq[:, c0:c1], start=True, stop=False)
                        last = split_product(psQ[:, c0:c1], n_hi, n_lo, wq_hi[:, :, c0:c1], wq_lo[:, :, c0:c1], KC,
                                             before != 0)
                    last.then_inc(s_qkv, 1)
                    pe.wait_ge(s_stack, 2 * i + 2)
                    for u in range(QK_HEADS // 8):
                        if u >= 2:
                            if u % 2:
                                pe.wait_ge(s_ste_act, 2 * i + u // 2)
                            else:
                                pe.wait_ge(s_ste_dve, 3 * i + u // 2)
                        for j in range(8):
                            last = nc.tensor.transpose(psS[u % 2][0:STACK, j, :],
                                                       stack[:, 8 * u + j, :, :].rearrange("p s d -> p (s d)"),
                                                       identb[:])
                        last.then_inc(s_stp, 1)
                    pe.wait_ge(s_ste_dve, 3 * i + 3)
                    pe.wait_ge(s_ste_act, 2 * i + 2)
                if moe is not None:
                    pe.wait_ge(norms["m"]["s_out"], i + 1)
                    for k in range(KC):
                        last = nc.tensor.transpose(psT[:, k, :], y[:, k * P:(k + 1) * P], ident[:])
                    last.then_inc(s_mTp, 1)
                    pe.wait_ge(s_mT, i + 1)
                    for k in range(KC):
                        last = nc.tensor.matmul(psG[:], nT[:, k, :], gw[:, k, :], start=(k == 0), stop=(k == KC - 1))
                    last.then_inc(s_glog, 1)
                    pe.wait_ge(s_mlo, i + 1)


STEPS = []
for _c in range(S // 512):
    _q0 = 512 * _c
    for _kb in range(0, 4 * _c, 2):
        STEPS.append((_c, [(_kb, _q0, 512, 0), (_kb + 1, _q0, 512, 512)]))
    _d = 4 * _c
    STEPS.append((_c, [(_d, _q0, 512, 0), (_d + 1, _q0 + 128, 384, 512), (_d + 3, _q0 + 384, 128, 896)]))
    STEPS.append((_c, [(_d + 2, _q0 + 256, 256, 0)]))
N_STEPS = len(STEPS)
UNITS = [(qb, k0, min(512, (qb + 1) * P - k0), k0 // 512) for qb in range(NB) for k0 in range(0, (qb + 1) * P, 512)]
N_UNITS = REP * len(UNITS)
UNITS_WITH_STEP = [12, 4, 12, 12, 8, 0]
assert sum(UNITS_WITH_STEP) == N_UNITS and len(UNITS_WITH_STEP) == N_STEPS
P_BUFS = 3
assert N_STEPS % P_BUFS == 0


def attention_phase(nc, name, layer, const, attn, io):
    scale = SCALES[layer]
    identb, mask = const["identb"], const["mask"]
    q, k, v = attn["q"], attn["k"], attn["v"]
    with ExitStack() as ctx:
        b = Buffers(nc, ctx, name)
        sem = b.sem
        vg = b.sb("vg", [P, NB, VW])
        pt = [b.sb(f"pt{n}", [P, REP, 1024]) for n in range(P_BUFS)]
        mraw = b.sb("mraw", [P, REP * NB, 2])
        nm, m_r1, m_r2 = (b.sb(n, [P, REP * NB]) for n in ("nm", "m_r1", "m_r2"))
        m3 = b.sb("m3", [P, MROWS, REP * NB], BF16)
        mT = b.sb("mT", [MROWS * REP * NB, P], BF16)
        ob = b.sb("ob", [P, 512])
        den, rec, cx = b.sb("den", [P, 512]), b.sb("rec", [P, 512]), b.sb("cx", [P, 512])
        psU = [b.ps(f"psU{n}", [P, 512]) for n in range(2)]
        psE = [b.ps(f"psE{n}", [P, 1024]) for n in range(2)]
        psO = b.ps("psO", [P, 512])
        psX = b.ps("psX", [MROWS * REP * NB, P], BF16)
        (s_pre, s_vg, s_unit, s_max, s_nm, s_m, s_m3, s_mTp, s_mT, s_mrow, s_sc, s_p, s_causal, s_pv, s_ob, s_den,
         s_rec, s_cx, s_out) = map(
            sem, ("s_pre", "s_vg", "s_unit", "s_max", "s_nm", "s_m", "s_m3", "s_mTp", "s_mT", "s_mrow", "s_sc", "s_p",
                  "s_causal", "s_pv", "s_ob", "s_den", "s_rec", "s_cx", "s_out"))
        block = ctx.enter_context(nc.Block())
        N_EXP = REP * N_STEPS
        DIAG = [n for n, (c, tiles) in enumerate(STEPS) if tiles[0][0] >= 4 * c]

        def over_groups(eng, body):
            body(0, None)
            with eng.Fori(0, NKV - 1) as g:
                body(g + 1, g)
            body(None, NKV - 1)

        @block.sync
        def _(sp):
            def body(gm, g):
                if g is not None:
                    for c in range(2):
                        sp.wait_ge(s_cx, 2 * g + c + 1)
                        apart(sp)
                        for j in range(REP):
                            sp.dma_start(io["ctx_write"][bass.ds(g * (REP * HD) + j * HD, HD), c * 512:(c + 1) * 512],
                                         cx[32 * j:32 * j + HD, :]).then_inc(s_out, 16)
                if gm is not None:
                    sp.wait_ge(s_mT, gm + 1)
                    apart(sp)
                    sp.dma_start(q[STACK:STACK + MROWS, bass.ds(gm * REP, REP), :], mT[:]).then_inc(s_mrow, 16)

            over_groups(sp, body)
            sp.wait_ge(s_out, 16 * 2 * REP * NKV)

        @block.gpsimd
        def _(pool):
            def body(gm, g):
                if g is not None:
                    apart(pool)
                    nc.gpsimd.tensor_copy(vg[:], v[:, :, bass.ds(g, 1), :].rearrange("p b a w -> p b (a w)")
                                          ).then_inc(s_vg, 1)
                    for n in DIAG:
                        pool.wait_ge(s_p, REP * (N_STEPS * g + n + 1))
                        t = pt[n % P_BUFS]
                        spots = [t[:, :, 0:1024].rearrange("p h (a w) -> p h a w", w=512)[:, :, :, 0:P], t[:, :, 896:1024]]
                        if len(STEPS[n][1]) == 1:
                            spots = [t[:, :, 0:P]]
                        for spot in spots:
                            rows = [[0, w] for w in spot.shape[1:-1]]
                            apart(pool)
                            last = nc.gpsimd.affine_select(out=spot, in_=spot, compare_op=ALU.is_ge, fill=0.0, base=0,
                                                           pattern=rows + [[1, P]], channel_multiplier=-1)
                            last.then_inc(s_causal, 1)
                if gm is not None:
                    pool.wait_ge(s_nm, gm + 1)
                    apart(pool)
                    nc.gpsimd.tensor_copy(m3[:, 0, :], nm[:]).then_inc(s_m, 1)
                    pool.wait_ge(s_m, 4 * gm + 1)
                    nc.gpsimd.tensor_tensor(m_r1[:], nm[:], m3[:, 0, :], ALU.subtract).then_inc(s_m, 1)
                    pool.wait_ge(s_m, 4 * gm + 2)
                    apart(pool)
                    nc.gpsimd.tensor_copy(m3[:, 1, :], m_r1[:]).then_inc(s_m, 1)
                    pool.wait_ge(s_m, 4 * gm + 3)
                    nc.gpsimd.tensor_tensor(m_r2[:], m_r1[:], m3[:, 1, :], ALU.subtract).then_inc(s_m, 1)
                    pool.wait_ge(s_m, 4 * gm + 4)
                    apart(pool)
                    nc.gpsimd.tensor_copy(m3[:, 2, :], m_r2[:]).then_inc(s_m3, 1)
                if g is not None:
                    pool.wait_ge(s_pv, N_STEPS * (g + 1))

            over_groups(pool, body)

        @block.scalar
        def _(act):
            def body(gm, g):
                if g is not None:
                    for n, (c, tiles) in enumerate(STEPS):
                        width = max(col + w for _, _, w, col in tiles)
                        for j in range(REP):
                            u = REP * n + j
                            act.wait_ge(s_sc, N_EXP * g + u + 1)
                            if j == 0 and n >= P_BUFS:
                                act.wait_ge(s_pv, N_STEPS * g + n - P_BUFS + 1)
                            nc.scalar.activation(pt[n % P_BUFS][:, j, 0:width], psE[u % 2][:, 0:width], ACT.Exp,
                                                 scale=scale).then_inc(s_p, 1)
                        if n == 3:
                            act.wait_ge(s_pv, N_STEPS * g + 2)
                            nc.scalar.copy(ob[:], psO[:]).then_inc(s_ob, 1)
                    act.wait_ge(s_pv, N_STEPS * (g + 1))
                    act.wait_ge(s_cx, 2 * g + 1)
                    nc.scalar.copy(ob[:], psO[:]).then_inc(s_ob, 1)
                if gm is not None:
                    act.wait_ge(s_mTp, gm + 1)
                    nc.scalar.copy(mT[:], psX[:]).then_inc(s_mT, 1)
                if g is not None:
                    act.wait_ge(s_cx, 2 * g + 2)

            over_groups(act, body)

        @block.vector
        def _(dve):
            def normalise(g, c):
                dve.wait_ge(s_ob, 2 * g + c + 1)
                apart(dve)
                nc.vector.stream_shuffle(den[:], ob[:], [HD] * 32).then_inc(s_den, 1)
                dve.wait_ge(s_den, 2 * g + c + 1)
                nc.vector.reciprocal(rec[:], den[:]).then_inc(s_rec, 1)
                dve.wait_ge(s_rec, 2 * g + c + 1)
                if c == 1:
                    dve.wait_ge(s_out, 16 * REP * (2 * g + 1))
                nc.vector.tensor_tensor(cx[:], ob[:], rec[:], ALU.mult).then_inc(s_cx, 1)

            def maxima(gm, units):
                for u in units:
                    qb, k0, nk, slot = UNITS[u % len(UNITS)]
                    dve.wait_ge(s_unit, N_UNITS * gm + u + 1)
                    nc.vector.tensor_reduce(mraw[:, (u // len(UNITS)) * NB + qb, slot:slot + 1], psU[u % 2][:, 0:nk],
                                            AX.X, ALU.max).then_inc(s_max, 1)

            def body(gm, g):
                at = 0
                for n in range(N_STEPS):
                    if gm is not None:
                        maxima(gm, range(at, at + UNITS_WITH_STEP[n]))
                        at += UNITS_WITH_STEP[n]
                    if n == N_STEPS - 2 and gm is not None:
                        dve.wait_ge(s_max, N_UNITS * (gm + 1))
                        nc.vector.tensor_reduce(nm[:], mraw[:], AX.X, ALU.max, negate=True).then_inc(s_nm, 1)
                        dve.wait_ge(s_nm, gm + 1)
                    if n == N_STEPS - 2 and g is not None:
                        normalise(g, 0)
                if g is not None:
                    normalise(g, 1)
                    dve.wait_ge(s_out, 16 * REP * (2 * g + 2))

            nc.vector.memset(mraw[:], -3e38).then_inc(s_pre, 1)
            dve.wait_ge(s_pre, 1)
            over_groups(dve, body)

        @block.tensor
        def _(pe):
            def unit(gm, u):
                j, (qb, k0, nk, _) = u // len(UNITS), UNITS[u % len(UNITS)]
                if isinstance(gm, int) and gm == 0:
                    if u >= 2:
                        pe.wait_ge(s_max, u - 1)
                else:
                    pe.wait_ge(s_max, N_UNITS * gm + u - 1)
                out = psU[u % 2]
                diagonal = k0 + nk == (qb + 1) * P
                last = nc.tensor.matmul(out[:, 0:nk], head(gm, j, qb * P, P), keys(gm, k0, nk), start=True,
                                        stop=not diagonal)
                if diagonal:
                    last = nc.tensor.matmul(out[:, nk - P:nk], identb[:], mask[:], start=False, stop=True)
                last.then_inc(s_unit, 1)

            def head(g, j, q0, n, rows=STACK):
                return q[0:rows, bass.ds(g * REP + j, 1), q0:q0 + n].rearrange("p a w -> p (a w)")

            def keys(g, k0, n, rows=STACK):
                return k[0:rows, bass.ds(g, 1), k0:k0 + n].rearrange("p a w -> p (a w)")

            def scores(g, n, j):
                u = REP * n + j
                if isinstance(g, int) or u >= 2:
                    pe.wait_ge(s_p, N_EXP * g + u - 1)
                for kb, q0, w, col in STEPS[n][1]:
                    last = nc.tensor.matmul(psE[u % 2][:, col:col + w], keys(g, kb * P, P, STACK + MROWS),
                                            head(g, j, q0, w, STACK + MROWS), start=True, stop=True)
                last.then_inc(s_sc, 1)

            def values(g, n):
                c, tiles = STEPS[n]
                if n == 0:
                    pe.wait_ge(s_vg, g + 1)
                pe.wait_ge(s_p, REP * (N_STEPS * g + n + 1))
                if n in DIAG:
                    done = sum(2 if len(STEPS[m][1]) > 1 else 1 for m in DIAG if m <= n)
                    per = sum(2 if len(STEPS[m][1]) > 1 else 1 for m in DIAG)
                    pe.wait_ge(s_causal, per * g + done)
                if n == 2:
                    pe.wait_ge(s_ob, 2 * g + 1)
                for kb, q0, w, col in tiles:
                    for j in range(REP):
                        last = nc.tensor.matmul(psO[32 * j:32 * j + 32, q0 - 512 * c:q0 - 512 * c + w], vg[:, kb, :],
                                                pt[n % P_BUFS][:, j, col:col + w], start=(kb == 0),
                                                stop=(kb == 4 * c + 2))
                last.then_inc(s_pv, 1)

            def body(gm, g):
                at = 0
                for n in range(N_STEPS):
                    per = UNITS_WITH_STEP[n] if gm is not None else 0
                    if g is not None and n == 0:
                        pe.wait_ge(s_mrow, 16 * g + 16)
                    for j in range(REP):
                        if g is not None:
                            scores(g, n, j)
                        if gm is not None:
                            for u in range(at + per * j // REP, at + per * (j + 1) // REP):
                                unit(gm, u)
                    at += per
                    if g is not None and n >= 1:
                        values(g, n - 1)
                if gm is not None:
                    pe.wait_ge(s_m3, gm + 1)
                    nc.tensor.transpose(psX[:], m3[:].rearrange("p a n -> p (a n)"), identb[:]).then_inc(s_mTp, 1)
                if g is not None:
                    values(g, N_STEPS - 1)
                    pe.wait_ge(s_ob, 2 * g + 2)

            over_groups(pe, body)


def moe_phase(nc, name, const, moe, io, out):
    x, ident, neg_half = const["x"], const["ident"], const["neg_half"]
    PAIRS = E1 // 2
    with ExitStack() as ctx:
        b = Buffers(nc, ctx, name)
        sem = b.sem
        raw_gu = [b.sb(f"raw_gu{n}", [P, KC, 2 * I1]) for n in range(2)]
        raw_dn = [b.sb(f"raw_dn{n}", [P, 2, H]) for n in range(2)]
        gu_hi = [b.sb(f"gu_hi{n}", [P, KC, 2 * I1], F32R) for n in range(2)]
        gu_lo = [b.sb(f"gu_lo{n}", [P, KC, 2 * I1], F32R) for n in range(2)]
        dn_hi = [b.sb(f"dn_hi{n}", [P, 2, H], F32R) for n in range(2)]
        dn_lo = [b.sb(f"dn_lo{n}", [P, 2, H], F32R) for n in range(2)]
        yacc = b.sb("yacc", [P, NB, H])
        sil = [b.sb(f"sil{n}", [P, I1]) for n in range(2)]
        z = [b.sb(f"z{n}", [P, I1]) for n in range(2)]
        z_hi = [b.sb(f"z_hi{n}", [P, 2, P], F32R) for n in range(2)]
        z_lo = [b.sb(f"z_lo{n}", [P, 2, P], F32R) for n in range(2)]
        stats, mv, ve, rstd = b.sb("stats", [P, 6]), b.sb("mv", [P, 2]), b.sb("ve", [P, 1]), b.sb("rstd", [P, 1])
        yn = b.sb("yn", [P, H])
        psG = [b.ps(f"psG{n}", [P, 2 * I1]) for n in range(2)]
        psZ = [b.ps(f"psZ{n}", [P, 2, P]) for n in range(2)]
        psY = [b.ps(f"psY{n}", [P, H]) for n in range(2)]
        s_w = [sem("s_w0"), sem("s_w1")]
        (s_cw1, s_y0, s_whi, s_wlo, s_gu, s_sil, s_z, s_zTp, s_zhi, s_zlo, s_y, s_acc, s_st, s_mv, s_ve, s_rstd, s_yn,
         s_fin, s_store) = map(
            sem, ("s_cw1", "s_y0", "s_whi", "s_wlo", "s_gu", "s_sil", "s_z", "s_zTp", "s_zhi", "s_zlo", "s_y", "s_acc",
                  "s_st", "s_mv", "s_ve", "s_rstd", "s_yn", "s_fin", "s_store"))
        block = ctx.enter_context(nc.Block())
        N_E = E1 + 1

        def over_experts(eng, body):
            body(0, 0, 0)
            body(1, 1, 0)
            with eng.Fori(1, PAIRS) as pair:
                body(2 * pair, 0, pair)
                body(2 * pair + 1, 1, pair)
            body(E1, 0, PAIRS)

        @block.sync
        def _(sp):
            def body(e, n, pair):
                if not (isinstance(e, int) and e < 2):
                    sp.wait_ge(s_wlo, 2 * e - 2)
                apart(sp)
                sp.dma_start(raw_gu[n][:], io["gu"][bass.ds(e, 1)].rearrange("a p k n -> p (a k) n")).then_inc(s_w[n], 16)
                sp.dma_start(raw_dn[n][:], io["dn"][bass.ds(e, 1)].rearrange("a p k n -> p (a k) n")).then_inc(s_w[n], 16)

            over_experts(sp, body)
            with sp.Fori(0, NB) as i:
                sp.wait_ge(s_fin, i + 1)
                apart(sp)
                sp.dma_start(out[:, bass.ds(i, 1), :], x[:, bass.ds(i, 1), :]).then_inc(s_store, 16)
            sp.wait_ge(s_store, 16 * NB)

        @block.gpsimd
        def _(pool):
            nc.gpsimd.memset(moe["cw"][:, :, E1:], 1.0).then_inc(s_cw1, 1)
            nc.gpsimd.memset(yacc[:], 0.0).then_inc(s_y0, 1)
            with pool.Fori(0, NB) as i:
                pool.wait_ge(s_mv, i + 1)
                apart(pool)
                nc.gpsimd.tensor_scalar(ve[:], mv[:, 1:2], EPS, 1.0, ALU.add, ALU.mult).then_inc(s_ve, 1)
                pool.wait_ge(s_ve, i + 1)
                nc.gpsimd.tensor_tensor(rstd[:], ve[:], neg_half[:], ALU.pow).then_inc(s_rstd, 1)

        @block.scalar
        def _(act):
            def split(e, n, pair):
                act.wait_ge(s_w[n], 32 * pair + 32)
                if not (isinstance(e, int) and e < 2):
                    act.wait_ge(s_y, NB * e - NB)
                nc.scalar.copy(gu_hi[n][:], raw_gu[n][:]).then_inc(s_whi, 1)
                nc.scalar.copy(dn_hi[n][:], raw_dn[n][:]).then_inc(s_whi, 1)

            def body(e, n, prefetch=True):
                for t in range(NB):
                    u = NB * e + t
                    act.wait_ge(s_gu, u + 1)
                    nc.scalar.activation(sil[t % 2][:], psG[t % 2][:, 0:I1], ACT.Silu).then_inc(s_sil, 1)
                    act.wait_ge(s_zTp, u + 1)
                    nc.scalar.copy(z_hi[t % 2][:], psZ[t % 2][:]).then_inc(s_zhi, 1)

            def step(e, n, pair):
                split(e, n, pair)
                body(e, n)
            over_experts(act, step)

        @block.vector
        def _(dve):
            dve.wait_ge(s_y0, 1)
            dve.wait_ge(s_cw1, 1)

            def step(e, n, pair):
                dve.wait_ge(s_whi, 2 * e + 1)
                nc.vector.tensor_tensor(gu_lo[n][:], raw_gu[n][:], gu_hi[n][:].bitcast(F32),
                                        ALU.subtract).then_inc(s_wlo, 1)
                dve.wait_ge(s_whi, 2 * e + 2)
                nc.vector.tensor_tensor(dn_lo[n][:], raw_dn[n][:], dn_hi[n][:].bitcast(F32),
                                        ALU.subtract).then_inc(s_wlo, 1)
                for t in range(NB):
                    u = NB * e + t
                    dve.wait_ge(s_sil, u + 1)
                    nc.vector.scalar_tensor_tensor(
                        out=z[t % 2][:], in0=sil[t % 2][:], scalar=moe["cw"][:, t, bass.ds(e, 1)],
                        in1=psG[t % 2][:, I1:], op0=ALU.mult, op1=ALU.mult).then_inc(s_z, 1)
                    dve.wait_ge(s_zhi, u + 1)
                    nc.vector.tensor_tensor(z_lo[t % 2][:], psZ[t % 2][:], z_hi[t % 2][:].bitcast(F32),
                                            ALU.subtract).then_inc(s_zlo, 1)
                    dve.wait_ge(s_y, u + 1)
                    nc.vector.tensor_tensor(yacc[:, t, :], yacc[:, t, :], psY[t % 2][:], ALU.add).then_inc(s_acc, 1)
            over_experts(dve, step)
            with dve.Fori(0, NB) as i:
                yi, xi = one(yacc, i), one(x, i)
                dve.wait_ge(s_acc, NB * N_E)
                apart(dve)
                nc.vector.bn_stats(stats[:], yi).then_inc(s_st, 1)
                dve.wait_ge(s_st, i + 1)
                apart(dve)
                nc.vector.bn_aggr(mv[:], stats[:]).then_inc(s_mv, 1)
                dve.wait_ge(s_rstd, i + 1)
                nc.vector.tensor_scalar(yn[:], yi, mv[:, 0:1], rstd[:, 0:1], ALU.subtract, ALU.mult).then_inc(s_yn, 1)
                dve.wait_ge(s_yn, i + 1)
                nc.vector.tensor_tensor(xi, xi, yn[:], ALU.add).then_inc(s_fin, 1)
                dve.wait_ge(s_fin, i + 1)

        @block.tensor
        def _(pe):
            def up(e, n, t):
                u = NB * e + t
                if not (isinstance(e, int) and e == 0 and t < 2):
                    pe.wait_ge(s_z, u - 1)
                for k in range(KC):
                    for m, (a, wt) in enumerate(((moe["hi"], gu_hi[n]), (moe["hi"], gu_lo[n]), (moe["lo"], gu_hi[n]))):
                        last = nc.tensor.matmul(psG[t % 2][:], a[:, k, t * P:(t + 1) * P], wt[:, k, :],
                                                start=(k == 0 and m == 0), stop=(k == KC - 1 and m == 2))
                last.then_inc(s_gu, 1)

            def down(e, n, t):
                u = NB * e + t
                pe.wait_ge(s_z, u + 1)
                for k in range(2):
                    last = nc.tensor.transpose(psZ[t % 2][:, k, :], z[t % 2][:, k * P:(k + 1) * P], ident[:])
                last.then_inc(s_zTp, 1)
                pe.wait_ge(s_zlo, u + 1)
                if not (isinstance(e, int) and e == 0 and t < 2):
                    pe.wait_ge(s_acc, u - 1)
                for k in range(2):
                    for m, (a, wt) in enumerate(((z_hi[t % 2], dn_hi[n]), (z_hi[t % 2], dn_lo[n]), (z_lo[t % 2], dn_hi[n]))):
                        last = nc.tensor.matmul(psY[t % 2][:], a[:, k, :], wt[:, k, :], start=(k == 0 and m == 0),
                                                stop=(k == 1 and m == 2))
                last.then_inc(s_y, 1)

            def step(e, n, pair):
                pe.wait_ge(s_wlo, 2 * e + 2)
                up(e, n, 0)
                for t in range(NB):
                    if t + 1 < NB:
                        up(e, n, t + 1)
                    down(e, n, t)
            over_experts(pe, step)


def sandwich(nc, io, out):
    with ExitStack() as ctx:
        b = Buffers(nc, ctx)
        const = {
            "x": b.sb("x", [P, NB, H]), "ident": b.sb("ident", [P, P]), "identb": b.sb("identb", [P, P], BF16),
            "mask": b.sb("mask", [P, P], BF16), "ones_row": b.sb("ones_row", [1, P]),
            "neg_half": b.sb("neg_half", [P, 1]),
        }
        s_base, s_const, s_kones = b.sem("s_base"), b.sem("s_const"), b.sem("s_kones")
        io["ctx_write"] = io["ctx"].rearrange("(h r) t -> (h r) t", r=HD)
        io["ctx_read"] = io["ctx"].rearrange("(k p) t -> p k t", p=P)
        with ExitStack() as attn_ctx:
            a = Buffers(nc, attn_ctx)
            attn = {"q": a.sb("q", [STACK + MROWS, NH, S], BF16), "k": a.sb("k", [STACK + MROWS, NKV, S], BF16),
                    "v": a.sb("v", [P, NB, NKV, VW])}
            with nc.Block() as block:
                @block.gpsimd
                def _(pool):
                    nc.gpsimd.memset(const["ident"][:], 0.0).then_inc(s_base, 1)
                    nc.gpsimd.memset(const["identb"][:], 0.0).then_inc(s_base, 1)
                    nc.gpsimd.memset(const["mask"][:], 0.0).then_inc(s_base, 1)
                    nc.gpsimd.memset(const["ones_row"][:], 1.0).then_inc(s_const, 1)
                    nc.gpsimd.memset(const["neg_half"][:], -0.5).then_inc(s_const, 1)
                    pool.wait_ge(s_base, 3)
                    for m in ("ident", "identb"):
                        nc.gpsimd.affine_select(out=const[m][:], in_=const[m][:], compare_op=ALU.not_equal, fill=1.0,
                                                base=0, pattern=[[-1, P]], channel_multiplier=1).then_inc(s_const, 1)
                    nc.gpsimd.affine_select(out=const["mask"][:], in_=const["mask"][:], compare_op=ALU.is_ge, fill=NEG,
                                            base=0, pattern=[[-1, P]], channel_multiplier=1).then_inc(s_const, 1)
                    pool.wait_ge(s_const, 5)

                @block.vector
                def _(dve):
                    nc.vector.memset(attn["k"][STACK:, :, :], 1.0).then_inc(s_kones, 1)
                    dve.wait_ge(s_kones, 1)
            row_phase(nc, "a0_", const, attn, io, before=0)
            attention_phase(nc, "b0_", 0, const, attn, io)
            row_phase(nc, "c0_", const, attn, io, after=0, ffn=True, before=1)
            attention_phase(nc, "b1_", 1, const, attn, io)
        m = Buffers(nc, ctx)
        moe = {"hi": m.sb("m_hi", [P, KC, S], F32R), "lo": m.sb("m_lo", [P, KC, S], F32R),
               "cw": m.sb("cw", [P, NB, E1 + 1])}

        cw16 = {"hi": moe["hi"], "lo": moe["lo"], "cw": moe["cw"][:, :, 0:E1]}
        row_phase(nc, "c1_", const, None, io, after=1, moe=cw16)
        moe_phase(nc, "m_", const, moe, io, out)


def rope_tables(base, interleaved=False):
    half = np.arange(0, HD, 2, dtype=np.float32) / np.float32(HD)
    inv_freq = (np.float32(1.0) / np.power(np.float32(base), half)).astype(np.float32)
    angle = (np.arange(S, dtype=np.float32)[:, None] * inv_freq[None, :]).astype(np.float32)
    cos, sin = np.cos(angle), np.sin(angle)
    tables = np.concatenate([cos, cos], 1), np.concatenate([-sin, sin], 1)
    return [np.ascontiguousarray(t.astype(np.float32).reshape(NB, P, HD).transpose(1, 0, 2)) for t in tables]


def by_chunk(w):
    return np.ascontiguousarray(w.reshape(-1, P, w.shape[1]).transpose(1, 0, 2))


def kernel(**inputs):
    import concourse.bacc as _bacc
    from concourse.bass_utils import run_bass_kernel_spmd as _run

    a = {k: np.asarray(v) for k, v in inputs.items()}

    def regroup(w):
        g = w.reshape((NKV, REP + 2, HD) + w.shape[1:])
        return np.concatenate([g[:, :REP].reshape((QW,) + w.shape[1:]), g[:, REP].reshape((KW,) + w.shape[1:]),
                               g[:, REP + 1].reshape((KW,) + w.shape[1:])], 0)

    halves = np.concatenate([np.arange(0, HD, 2), np.arange(1, HD, 2)])
    qk_order = (np.arange(QK_HEADS)[:, None] * HD + halves[None, :]).reshape(-1)
    order1 = np.concatenate([qk_order, np.arange(QW + KW, QKV)])
    cos0, sin0 = rope_tables(1000000.0)
    cos1, sin1 = rope_tables(10000.0)
    gates = np.concatenate([a["L1_ffn_Wg"], a["L1_ffn_Sg"][None]], 0)
    ups = np.concatenate([a["L1_ffn_Wu"], a["L1_ffn_Su"][None]], 0)
    downs = np.concatenate([a["L1_ffn_Wd"], a["L1_ffn_Sd"][None]], 0)
    gu = np.concatenate([gates, ups], 1).transpose(0, 2, 1)
    dn = downs.transpose(0, 2, 1)
    arrays = {
        "x": a["L0_attn_hidden_states"].reshape(NB, P, H).transpose(1, 0, 2),
        "wq0": by_chunk(regroup(a["L0_attn_w_qkv"]).T),
        "bq": regroup(a["L0_attn_b_qkv"])[None],
        "wd0": by_chunk(a["L0_attn_w_dense"].T),
        "bd": a["L0_attn_b_dense"][None],
        "rw": by_chunk(a["L0_ffn_router_weight"].T),
        "rb": a["L0_ffn_router_bias"][None],
        "eb": a["L0_ffn_expert_bias"],
        "wq1": by_chunk(a["L1_attn_w_qkv"][:, order1]),
        "wd1": by_chunk(a["L1_attn_w_o"]),
        "gw": by_chunk(a["L1_ffn_gate_w"].T),
        "gb": np.broadcast_to(a["L1_ffn_bias"][None], (P, E1)),
        "gu": gu.reshape(E1 + 1, KC, P, 2 * I1).transpose(0, 2, 1, 3),
        "dn": dn.reshape(E1 + 1, 2, P, H).transpose(0, 2, 1, 3),
        "cos0": cos0, "sin0": sin0, "cos1": cos1, "sin1": sin1,
    }
    arrays = {k: np.ascontiguousarray(v) for k, v in arrays.items()}
    nc = _bacc.Bacc("TRN2", target_bir_lowering=False, num_devices=1)
    io = {k: nc.dram_tensor(f"in_{k}", v.shape, mybir.dt.from_np(v.dtype), kind="ExternalInput").ap()
          for k, v in arrays.items()}
    io["ctx"] = nc.dram_tensor("ctx_scratch", [QW, S], F32).ap()
    out = nc.dram_tensor("out_0", [P, NB, H], F32, kind="ExternalOutput").ap()
    sandwich(nc, io, out)
    r = _run(nc, [{f"in_{k}": v for k, v in arrays.items()}], core_ids=[0])
    return r.results[0]["out_0"].transpose(1, 0, 2).reshape(1, S, H)
```

```python
from contextlib import ExitStack

import numpy as np

import concourse.bass as bass
from concourse import mybir

F32 = mybir.dt.float32
F32R = mybir.dt.float32r
BF16 = mybir.dt.bfloat16
ALU = mybir.AluOpType
ACT = mybir.ActivationFunctionType
AX = mybir.AxisListType

P = 128
S = 1024
H = 512
NB = S // P
KC = H // P
HD = 16
NH, NKV = 32, 8
REP = NH // NKV
QW = NH * HD
KW = NKV * HD
QKV = QW + 2 * KW
QK_HEADS = NH + NKV
SLOTS = 6
STACK = SLOTS * HD
MROWS = 3
VW = 32
E0, TOP0 = 64, 8
E1, TOP1 = 16, 4
I1 = 256
EPS = 1e-5
NEG = -1e30
SCALES = (1.0 / HD, 1.0 / 4.0)


class Buffers:

    def __init__(self, nc, ctx, prefix=""):
        self.nc, self.ctx, self.prefix = nc, ctx, prefix
        self.semaphores = []
        ctx.callback(self.clear)

    def clear(self):
        self.nc.clear_and_free_semaphores(self.semaphores)
        self.nc.all_engine_barrier()

    def sb(self, name, shape, dt=F32):
        return self.ctx.enter_context(self.nc.sbuf_tensor(self.prefix + name, shape, dt))

    def ps(self, name, shape, dt=F32):
        return self.ctx.enter_context(self.nc.psum_tensor(self.prefix + name, shape, dt))

    def sem(self, name):
        self.semaphores.append(self.nc.alloc_semaphore(self.prefix + name))
        return self.semaphores[-1]


def apart(engine):
    engine.nop(nofuse=True)


def one(ap_of_blocks, i):
    return ap_of_blocks[:, bass.ds(i, 1), :].rearrange("p a w -> p (a w)")


def stage_plan(*names):
    return [(stage, lag) for lag, stage in enumerate(names)][::-1]


def in_turns(plan, stages):
    for turn in range(NB + len(plan) - 1):
        for stage, lag in plan:
            if stage in stages and 0 <= turn - lag < NB:
                stages[stage](turn - lag)


def row_phase(nc, name, const, attn, io, after=None, ffn=False, before=None, moe=None):
    x, ident, identb, ones_row, neg_half = (const[k] for k in ("x", "ident", "identb", "ones_row", "neg_half"))
    with ExitStack() as ctx:
        b = Buffers(nc, ctx, name)
        sem = b.sem
        plan = stage_plan(*(
            (["d_project", "d_stats", "d_add"] if after is not None else []) +
            (["f_apply", "f_logits", "f_choose", "f_mix", "g_add"] if ffn else []) +
            (["first_stats"] if after is None else []) +
            (["a_apply", "a_project", "a_rope", "a_middle", "a_low"] if before is not None else []) +
            (["m_apply", "m_logits", "m_choose"] if moe is not None else [])))
        next_norm = {"d_add": "f" if ffn else "m", "g_add": "a", "first_stats": "a"}
        kinds = [k for k, used in (("d", after is not None), ("f", ffn), ("g", ffn), ("a", before is not None),
                                   ("m", moe is not None)) if used]
        norms = {k: dict(stats=b.sb(f"st_{k}", [P, NB, 6]), mv=b.sb(f"mv_{k}", [P, NB, 2]),
                         ve=b.sb(f"ve_{k}", [P, NB, 1]), rstd=b.sb(f"rstd_{k}", [P, NB, 1]),
                         s_stats=sem(f"s_stats_{k}"), s_mv=sem(f"s_mv_{k}"), s_ve=sem(f"s_ve_{k}"),
                         s_rstd=sem(f"s_rstd_{k}"), s_out=sem(f"s_out_{k}")) for k in kinds}

        s_load = sem("s_load")
        s_x = sem("s_x")
        s_sum = sem("s_sum")
        yt = {k: b.sb(f"yt_{k}", [P, H]) for k in kinds if k in "fam"}
        yT = b.sb("yT", [P, KC, P]) if ffn or moe is not None else None
        if after is not None or before is not None:
            w_raw = [b.sb(f"w_raw{n}", [P, QKV]) for n in range(2)]
            s_w_raw = [sem(f"s_w_raw{n}") for n in range(2)]
            s_w_hi, s_w_lo = sem("s_w_hi"), sem("s_w_lo")
        splits = []
        if after is not None:
            wd_hi, wd_lo = b.sb("wd_hi", [P, KC, H], F32R), b.sb("wd_lo", [P, KC, H], F32R)
            splits += [(io[f"wd{after}"][:, k, :], wd_hi[:, k, :], wd_lo[:, k, :]) for k in range(KC)]
            bd = b.sb("bd", [1, H]) if after == 0 else None
            ctx_hi, ctx_lo = b.sb("ctx_hi", [P, KC, P], F32R), b.sb("ctx_lo", [P, KC, P], F32R)
            ctx_raw = [b.sb(f"ctx_raw{n}", [P, KC, P]) for n in range(2)]
            yd = b.sb("yd", [P, H])
            psD = b.ps("psD", [P, H])
            s_ctx = [sem("s_ctx0"), sem("s_ctx1")]
            s_ctx_hi, s_ctx_lo, s_proj, s_yd = map(sem, ("s_ctx_hi", "s_ctx_lo", "s_proj", "s_yd"))
        if ffn:
            rw, rb, eb = b.sb("rw", [P, KC, E0]), b.sb("rb", [1, E0]), b.sb("eb", [E0, H])
            mx8, top8 = b.sb("mx8", [P, 8]), b.sb("top8", [P, 8])
            nmx, sm, rs, wsum = (b.sb(n, [P, NB, 1]) for n in ("nmx", "sm", "rs", "wsum"))
            ex, pn, pr, w = (b.sb(n, [P, E0]) for n in ("ex", "pn", "pr", "w"))
            wT = b.sb("wT", [E0, P])
            rw_scale = b.sb("rw_scale", [P, NB, 1])
            o0 = b.sb("o0", [P, H])
            psL = b.ps("psL", [P, P])
            psM = b.ps("psM", [P, H])
            (s_hTp, s_hT, s_logit, s_mx8, s_nmx, s_exp, s_rs, s_pn, s_top8, s_pr, s_wsum, s_w, s_wTp, s_wT, s_mix,
             s_scale, s_h2, s_o0) = map(
                sem, ("s_hTp", "s_hT", "s_logit", "s_mx8", "s_nmx", "s_exp", "s_rs", "s_pn", "s_top8", "s_pr",
                      "s_wsum", "s_w", "s_wTp", "s_wT", "s_mix", "s_scale", "s_h2", "s_o0"))
        if before is not None:
            wq_hi, wq_lo = b.sb("wq_hi", [P, KC, QKV], F32R), b.sb("wq_lo", [P, KC, QKV], F32R)
            splits += [(io[f"wq{before}"][:, k, :], wq_hi[:, k, :], wq_lo[:, k, :]) for k in range(KC)]
            bq = b.sb("bq", [1, QKV]) if before == 0 else None
            n_hi = b.sb("n_hi", [P, KC, P], F32R)
            n_lo = b.sb("n_lo", [P, KC, P], F32R)
            cos, sin = b.sb("cos", [P, NB, HD]), b.sb("sin", [P, NB, HD])
            rc, rs_, qr, r1 = (b.sb(n, [P, QK_HEADS, HD]) for n in ("rc", "rs_", "qr", "r1"))
            r2 = rc
            stack = [b.sb(f"stack{n}", [P, QK_HEADS, SLOTS, HD], BF16) for n in range(2)]
            psQ = b.ps("psQ", [P, 1024])
            psS = [b.ps(f"psS{n}", [P, 8, P], BF16) for n in range(2)]
            (s_nTp, s_n_hi, s_n_lo, s_qkv, s_rc, s_qr, s_v, s_high, s_r1, s_mid, s_r2, s_low,
             s_stp, s_ste_act, s_ste_dve) = map(
                sem, ("s_nTp", "s_n_hi", "s_n_lo", "s_qkv", "s_rc", "s_qr", "s_v", "s_high", "s_r1",
                      "s_mid", "s_r2", "s_low", "s_stp", "s_ste_act", "s_ste_dve"))
        if before is not None or moe is not None:
            psT = b.ps("psT", [P, KC, P])
        if moe is not None:
            gw, gb = b.sb("gw", [P, KC, E1]), b.sb("gb", [P, E1])
            psG = b.ps("psG", [P, E1])
            ge, gd, sg, gm, gc = (b.sb(n, [P, E1]) for n in ("ge", "gd", "sg", "gm", "gc"))
            s20, g20 = b.sb("s20", [P, E1 + 4]), b.sb("g20", [P, E1 + 4])
            g8, rep8 = b.sb("g8", [P, 8]), b.sb("rep8", [P, 8])
            gsum, gden, grec = (b.sb(n, [P, NB, 1]) for n in ("gsum", "gden", "grec"))
            (s_pre, s_mTp, s_mT, s_mhi, s_mlo, s_glog, s_ge, s_gd, s_sg, s_s20, s_g8, s_rep, s_g20, s_gm, s_gc, s_gsum,
             s_gden, s_grec, s_cw) = map(
                sem, ("s_pre", "s_mTp", "s_mT", "s_mhi", "s_mlo", "s_glog", "s_ge", "s_gd", "s_sg", "s_s20", "s_g8",
                      "s_rep", "s_g20", "s_gm", "s_gc", "s_gsum", "s_gden", "s_grec", "s_cw"))

        loads = []
        if after == 0:
            loads += [(bd[:], io["bd"])]
        if ffn:
            loads += [(rw[:], io["rw"]), (rb[:], io["rb"]), (eb[:], io["eb"])]
        if before is not None:
            loads += [(cos[:], io[f"cos{before}"]), (sin[:], io[f"sin{before}"])]
            loads += [(bq[:], io["bq"])] if before == 0 else []
        if moe is not None:
            loads += [(gw[:], io["gw"]), (gb[:], io["gb"])]

        sums = []
        in_turns(plan, {s: (lambda i, s=s: sums.append((s, i))) for s in ("d_add", "g_add")})

        def sums_after(stage, i):
            return sums.index((stage, i)) + 1

        block = ctx.enter_context(nc.Block())

        @block.sync
        def _(sp):
            if after is None:
                sp.dma_start(x[:], io["x"]).then_inc(s_x, 16)
            for n, (src, _, _) in enumerate(splits):
                if n >= 2:
                    sp.wait_ge(s_w_lo, n - 1)
                sp.dma_start(w_raw[n % 2][:, 0:src.shape[-1]], src).then_inc(s_w_raw[n % 2], 16)
                if n == 1:
                    for dst, a in loads:
                        sp.dma_start(dst, a).then_inc(s_load, 16)
            if after is not None:
                for i in range(NB):
                    if i >= 2:
                        sp.wait_ge(s_ctx_lo, i - 1)
                    sp.dma_start(ctx_raw[i % 2][:], io["ctx_read"][:, :, i * P:(i + 1) * P]).then_inc(s_ctx[i % 2], 16)

        @block.scalar
        def _(act):
            for n, (src, hi, _) in enumerate(splits):
                act.wait_ge(s_w_raw[n % 2], 16 * (n // 2 + 1))
                nc.scalar.copy(hi, w_raw[n % 2][:, 0:src.shape[-1]]).then_inc(s_w_hi, 1)

            def d_project(i):
                act.wait_ge(s_ctx[i % 2], 16 * (i // 2 + 1))
                if i >= 1:
                    act.wait_ge(s_proj, i)
                nc.scalar.copy(ctx_hi[:], ctx_raw[i % 2][:]).then_inc(s_ctx_hi, 1)

            def d_stats(i):
                act.wait_ge(s_proj, i + 1)
                if i >= 1:
                    act.wait_ge(s_sum, sums_after("d_add", i - 1))
                nc.scalar.copy(yd[:], psD[:]).then_inc(s_yd, 1)

            def f_apply(i):
                act.wait_ge(s_hTp, i + 1)
                if i >= 1:
                    act.wait_ge(s_logit, i)
                nc.scalar.copy(yT[:], psM[:].rearrange("p (k t) -> p k t", t=P)).then_inc(s_hT, 1)

            def f_logits(i):
                act.wait_ge(s_nmx, i + 1)
                if i >= 1:
                    act.wait_ge(s_pn, i)
                nc.scalar.activation(ex[:], psL[:, 0:E0], ACT.Exp, bias=nmx[:, i, :],
                                     accum_out=sm[:, i, :]).then_inc(s_exp, 1)

            def f_choose(i):
                act.wait_ge(s_wTp, i + 1)
                if i >= 1:
                    act.wait_ge(s_mix, i)
                nc.scalar.copy(wT[:], psL[0:E0, :]).then_inc(s_wT, 1)

            def a_apply(i):
                act.wait_ge(s_nTp, i + 1)
                if i >= 1:
                    act.wait_ge(s_qkv, i)
                    act.wait_ge(s_n_lo, i)
                nc.scalar.copy(n_hi[:], psT[:]).then_inc(s_n_hi, 1)

            def a_rope(i):
                act.wait_ge(s_rc, 3 * i + 3)
                nc.scalar.copy(attn["v"][:, i, :, :],
                               psQ[:, QW + KW:QKV].rearrange("p (g d) -> p g d", d=HD)).then_inc(s_v, 1)
                act.wait_ge(s_qr, i + 1)
                if i >= 2:
                    act.wait_ge(s_stp, (i - 1) * (QK_HEADS // 8))
                st = stack[i % 2]
                nc.scalar.copy(st[:, NH:, 0, :], qr[:, NH:, :]).then_inc(s_high, 1)
                nc.scalar.copy(st[:, 0:NH, 0:3, :],
                               qr[:, 0:NH, :].unsqueeze(2).to_broadcast([P, NH, 3, HD])).then_inc(s_high, 1)
                nc.scalar.copy(st[:, NH:, 4:6, :],
                               qr[:, NH:, :].unsqueeze(2).to_broadcast([P, NKV, 2, HD])).then_inc(s_high, 1)

            def a_middle(i):
                act.wait_ge(s_r1, i + 1)
                st = stack[i % 2]
                nc.scalar.copy(st[:, 0:NH, 3:5, :],
                               r1[:, 0:NH, :].unsqueeze(2).to_broadcast([P, NH, 2, HD])).then_inc(s_mid, 1)
                nc.scalar.copy(st[:, NH:, 2:4, :],
                               r1[:, NH:, :].unsqueeze(2).to_broadcast([P, NKV, 2, HD])).then_inc(s_mid, 1)

            def a_low(i):
                act.wait_ge(s_r2, i + 1)
                st = stack[i % 2]
                nc.scalar.copy(st[:, 0:NH, 5, :], r2[:, 0:NH, :]).then_inc(s_low, 1)
                nc.scalar.copy(st[:, NH:, 1, :], r2[:, NH:, :]).then_inc(s_low, 1)
                for u in range(1, QK_HEADS // 8, 2):
                    act.wait_ge(s_stp, i * (QK_HEADS // 8) + u + 1)
                    nc.scalar.copy(attn["q"][0:STACK, 8 * u:8 * u + 8, i * P:(i + 1) * P],
                                   psS[u % 2][0:STACK, :, :]).then_inc(s_ste_act, 1)

            def m_apply(i):
                act.wait_ge(s_mTp, i + 1)
                if i >= 1:
                    act.wait_ge(s_glog, i)
                    act.wait_ge(s_mlo, i)
                    act.wait_ge(s_mhi, i)
                nc.scalar.copy(yT[:], psT[:]).then_inc(s_mT, 1)

            def m_logits(i):
                act.wait_ge(s_mT, i + 1)
                nc.scalar.copy(moe["hi"][:, :, i * P:(i + 1) * P], yT[:]).then_inc(s_mhi, 1)
                act.wait_ge(s_glog, i + 1)
                if i >= 1:
                    act.wait_ge(s_gd, i)
                nc.scalar.activation(ge[:], psG[:], ACT.Exp, scale=-1.0).then_inc(s_ge, 1)

            in_turns(plan, dict(d_project=d_project, d_stats=d_stats, f_apply=f_apply, f_logits=f_logits,
                                f_choose=f_choose, a_apply=a_apply, a_rope=a_rope, a_middle=a_middle, a_low=a_low,
                                m_apply=m_apply, m_logits=m_logits))

        @block.gpsimd
        def _(pool):
            def rstd(k, i):
                n = norms[k]
                pool.wait_ge(n["s_mv"], i + 1)
                nc.gpsimd.tensor_scalar(n["ve"][:, i, :], n["mv"][:, i, 1:2], EPS, 1.0, ALU.add,
                                        ALU.mult).then_inc(n["s_ve"], 1)
                pool.wait_ge(n["s_ve"], i + 1)
                nc.gpsimd.tensor_tensor(n["rstd"][:, i, :], n["ve"][:, i, :], neg_half[:],
                                        ALU.pow).then_inc(n["s_rstd"], 1)

            if moe is not None:
                nc.gpsimd.memset(s20[:, E1:], NEG).then_inc(s_pre, 1)
                nc.gpsimd.memset(rep8[:, TOP1:], NEG).then_inc(s_pre, 1)
            stages = {s: (lambda i, k=k: rstd(k, i)) for s, k in next_norm.items()}
            stages["d_stats"] = lambda i: rstd("d", i)
            stages["f_mix"] = lambda i: rstd("g", i)
            in_turns(plan, stages)

        @block.vector
        def _(dve):
            def stats(k, src, i):
                n = norms[k]
                nc.vector.bn_stats(n["stats"][:, i, :], src).then_inc(n["s_stats"], 1)
                dve.wait_ge(n["s_stats"], i + 1)
                nc.vector.bn_aggr(n["mv"][:, i, :], n["stats"][:, i, :]).then_inc(n["s_mv"], 1)

            def apply(k, out, src, i):
                n = norms[k]
                dve.wait_ge(n["s_rstd"], i + 1)
                nc.vector.tensor_scalar(out, src, n["mv"][:, i, 0:1], n["rstd"][:, i, :], ALU.subtract,
                                        ALU.mult).then_inc(n["s_out"], 1)

            for n, (src, hi, lo) in enumerate(splits):
                dve.wait_ge(s_w_hi, n + 1)
                nc.vector.tensor_tensor(lo, w_raw[n % 2][:, 0:src.shape[-1]], hi.bitcast(F32),
                                        ALU.subtract).then_inc(s_w_lo, 1)
            dve.wait_ge(s_load, 16 * len(loads))
            if after is None:
                dve.wait_ge(s_x, 16)
            if moe is not None:
                dve.wait_ge(s_pre, 2)

            def d_project(i):
                dve.wait_ge(s_ctx_hi, i + 1)
                nc.vector.tensor_tensor(ctx_lo[:], ctx_raw[i % 2][:], ctx_hi[:].bitcast(F32),
                                        ALU.subtract).then_inc(s_ctx_lo, 1)

            def d_stats(i):
                dve.wait_ge(s_yd, i + 1)
                stats("d", yd[:], i)

            def add(k, y, i, stage):
                dve.wait_ge(norms[k]["s_out"], i + 1)
                nc.vector.tensor_tensor(x[:, i, :], x[:, i, :], y, ALU.add).then_inc(s_sum, 1)
                dve.wait_ge(s_sum, sums_after(stage, i))
                stats(next_norm[stage], x[:, i, :], i)

            def d_add(i):
                apply("d", yd[:], yd[:], i)
                add("d", yd[:], i, "d_add")

            def f_apply(i):
                if i >= 1:
                    dve.wait_ge(s_hTp, i)
                apply("f", yt["f"][:], x[:, i, :], i)

            def f_logits(i):
                dve.wait_ge(s_logit, i + 1)
                nc.vector.max(mx8[:], psL[:, 0:E0]).then_inc(s_mx8, 1)
                dve.wait_ge(s_mx8, i + 1)
                nc.vector.tensor_scalar(nmx[:, i, :], mx8[:, 0:1], -1.0, None, ALU.mult).then_inc(s_nmx, 1)

            def f_choose(i):
                dve.wait_ge(s_exp, i + 1)
                nc.vector.reciprocal(rs[:, i, :], sm[:, i, :]).then_inc(s_rs, 1)
                dve.wait_ge(s_rs, i + 1)
                nc.vector.tensor_scalar(pn[:], ex[:], rs[:, i, :], None, ALU.mult).then_inc(s_pn, 1)
                dve.wait_ge(s_pn, i + 1)
                nc.vector.max(top8[:], pn[:]).then_inc(s_top8, 1)
                dve.wait_ge(s_top8, i + 1)
                nc.vector.match_replace(pr[:], top8[:], pn[:], 0.0).then_inc(s_pr, 1)
                nc.vector.reduce_sum(wsum[:, i, :], top8[:], AX.X).then_inc(s_wsum, 1)
                dve.wait_ge(s_pr, i + 1)
                if i >= 1:
                    dve.wait_ge(s_wTp, i)
                nc.vector.tensor_tensor(w[:], pn[:], pr[:], ALU.subtract).then_inc(s_w, 1)

            def f_mix(i):
                n = norms["f"]
                dve.wait_ge(s_wsum, i + 1)
                nc.vector.tensor_tensor(rw_scale[:, i, :], n["rstd"][:, i, :], wsum[:, i, :],
                                        ALU.mult).then_inc(s_scale, 1)
                dve.wait_ge(s_scale, i + 1)
                if i >= 1:
                    dve.wait_ge(s_sum, sums_after("g_add", i - 1))
                nc.vector.tensor_scalar(o0[:], x[:, i, :], n["mv"][:, i, 0:1], rw_scale[:, i, :], ALU.subtract,
                                        ALU.mult).then_inc(s_h2, 1)
                dve.wait_ge(s_h2, i + 1)
                dve.wait_ge(s_mix, i + 1)
                nc.vector.tensor_tensor(o0[:], psM[:], o0[:], ALU.add).then_inc(s_o0, 1)
                dve.wait_ge(s_o0, i + 1)
                stats("g", o0[:], i)

            def g_add(i):
                apply("g", o0[:], o0[:], i)
                add("g", o0[:], i, "g_add")

            def first_stats(i):
                stats("a", x[:, i, :], i)

            def a_apply(i):
                if i >= 1:
                    dve.wait_ge(s_nTp, i)
                apply("a", yt["a"][:], x[:, i, :], i)

            def a_project(i):
                dve.wait_ge(s_n_hi, i + 1)
                if i >= 1:
                    dve.wait_ge(s_qkv, i)
                nc.vector.tensor_tensor(n_lo[:], psT[:], n_hi[:].bitcast(F32), ALU.subtract).then_inc(s_n_lo, 1)

            def a_rope(i):
                dve.wait_ge(s_qkv, i + 1)
                qk = psQ[:, 0:QW + KW].rearrange("p (h d) -> p h d", d=HD)
                if i >= 1:
                    dve.wait_ge(s_qr, i)
                if i >= 2:
                    dve.wait_ge(s_low, 2 * i - 2)
                for half in range(2):
                    lo, hi = half * HD // 2, (half + 1) * HD // 2
                    nc.vector.tensor_tensor(rs_[:, :, lo:hi], qk[:, :, HD // 2 - lo:HD - lo],
                                            sin[:, i:i + 1, lo:hi].to_broadcast([P, QK_HEADS, HD // 2]),
                                            ALU.mult).then_inc(s_rc, 1)
                nc.vector.tensor_tensor(rc[:], qk, cos[:, i:i + 1, :].to_broadcast([P, QK_HEADS, HD]),
                                        ALU.mult).then_inc(s_rc, 1)
                dve.wait_ge(s_rc, 3 * i + 3)
                if i >= 1:
                    dve.wait_ge(s_high, 3 * i)
                    dve.wait_ge(s_r1, i)
                nc.vector.tensor_tensor(qr[:], rc[:], rs_[:], ALU.add).then_inc(s_qr, 1)

            def a_middle(i):
                dve.wait_ge(s_high, 3 * i + 3)
                if i >= 1:
                    dve.wait_ge(s_mid, 2 * i)
                    dve.wait_ge(s_r2, i)
                nc.vector.tensor_tensor(r1[:], qr[:], stack[i % 2][:, :, 0, :], ALU.subtract).then_inc(s_r1, 1)

            def a_low(i):
                dve.wait_ge(s_mid, 2 * i + 2)
                dve.wait_ge(s_qr, min(NB, i + 2))
                nc.vector.tensor_tensor(r2[:], r1[:], stack[i % 2][:, :, 3, :], ALU.subtract).then_inc(s_r2, 1)
                for u in range(0, QK_HEADS // 8, 2):
                    dve.wait_ge(s_stp, i * (QK_HEADS // 8) + u + 1)
                    dst = attn["q"] if u < NH // 8 else attn["k"]
                    h0 = 8 * u if u < NH // 8 else 0
                    nc.vector.tensor_copy(dst[0:STACK, h0:h0 + 8, i * P:(i + 1) * P],
                                          psS[u % 2][0:STACK, :, :]).then_inc(s_ste_dve, 1)

            def m_apply(i):
                if i >= 1:
                    dve.wait_ge(s_mTp, i)
                apply("m", yt["m"][:], x[:, i, :], i)

            def m_logits(i):
                dve.wait_ge(s_mhi, i + 1)
                nc.vector.tensor_tensor(moe["lo"][:, :, i * P:(i + 1) * P], yT[:],
                                        moe["hi"][:, :, i * P:(i + 1) * P].bitcast(F32),
                                        ALU.subtract).then_inc(s_mlo, 1)

            def m_choose(i):
                dve.wait_ge(s_ge, i + 1)
                nc.vector.tensor_scalar(gd[:], ge[:], 1.0, None, ALU.add).then_inc(s_gd, 1)
                dve.wait_ge(s_gd, i + 1)
                nc.vector.reciprocal(sg[:], gd[:]).then_inc(s_sg, 1)
                dve.wait_ge(s_sg, i + 1)
                nc.vector.tensor_tensor(s20[:, 0:E1], sg[:], gb[:], ALU.add).then_inc(s_s20, 1)
                dve.wait_ge(s_s20, i + 1)
                nc.vector.max(g8[:], s20[:]).then_inc(s_g8, 1)
                dve.wait_ge(s_g8, i + 1)
                nc.vector.tensor_copy(rep8[:, 0:TOP1], g8[:, 0:TOP1]).then_inc(s_rep, 1)
                nc.vector.reduce_sum(gsum[:, i, :], g8[:, 0:TOP1], AX.X).then_inc(s_gsum, 1)
                dve.wait_ge(s_rep, i + 1)
                nc.vector.match_replace(g20[:], rep8[:], s20[:], -3e38).then_inc(s_g20, 1)
                dve.wait_ge(s_gsum, i + 1)
                nc.vector.tensor_scalar(gden[:, i, :], gsum[:, i, :], 1e-20, None, ALU.add).then_inc(s_gden, 1)
                dve.wait_ge(s_g20, i + 1)
                nc.vector.tensor_scalar(gm[:], g20[:, 0:E1], -2e38, None, ALU.is_le).then_inc(s_gm, 1)
                dve.wait_ge(s_gden, i + 1)
                nc.vector.reciprocal(grec[:, i, :], gden[:, i, :]).then_inc(s_grec, 1)
                dve.wait_ge(s_gm, i + 1)
                nc.vector.tensor_tensor(gc[:], gm[:], s20[:, 0:E1], ALU.mult).then_inc(s_gc, 1)
                dve.wait_ge(s_grec, i + 1)
                dve.wait_ge(s_gc, i + 1)
                nc.vector.tensor_scalar(moe["cw"][:, i, :], gc[:], grec[:, i, :], None, ALU.mult).then_inc(s_cw, 1)

            in_turns(plan, dict(d_project=d_project, d_stats=d_stats, d_add=d_add, f_apply=f_apply, f_logits=f_logits,
                                f_choose=f_choose, f_mix=f_mix, g_add=g_add, first_stats=first_stats, a_apply=a_apply,
                                a_project=a_project, a_rope=a_rope, a_middle=a_middle, a_low=a_low, m_apply=m_apply,
                                m_logits=m_logits, m_choose=m_choose))

        @block.tensor
        def _(pe):
            def split_product(out, a_hi, a_lo, w_hi, w_lo, chunks, open_group=True):
                for k in range(chunks):
                    for m, (a, wt) in enumerate(((a_hi, w_hi), (a_hi, w_lo), (a_lo, w_hi))):
                        last = nc.tensor.matmul(out, a[:, k, :], wt[:, k, :], start=open_group and k == 0 and m == 0,
                                                stop=(k == chunks - 1 and m == 2))
                return last

            def transposed(out, src, signal):
                for k in range(KC):
                    last = nc.tensor.transpose(out[:, k, :], src[:, k * P:(k + 1) * P], ident[:])
                last.then_inc(signal, 1)

            pe.wait_ge(s_load, 16 * len(loads))

            def d_project(i):
                if i == 0:
                    pe.wait_ge(s_w_lo, KC)
                pe.wait_ge(s_ctx_lo, i + 1)
                if i >= 1:
                    pe.wait_ge(s_yd, i)
                if after == 0:
                    nc.tensor.matmul(psD[:], ones_row[0:1, :], bd[:], start=True, stop=False)
                split_product(psD[:], ctx_hi, ctx_lo, wd_hi, wd_lo, KC, after != 0).then_inc(s_proj, 1)

            def f_apply(i):
                pe.wait_ge(norms["f"]["s_out"], i + 1)
                done = i - 3
                if done >= 0:
                    pe.wait_ge(s_o0, min(NB, done + 1))
                transposed(psM[:].rearrange("p (k t) -> p k t", t=P), yt["f"], s_hTp)

            def f_logits(i):
                pe.wait_ge(s_hT, i + 1)
                if i >= 1:
                    pe.wait_ge(s_wT, i)
                nc.tensor.matmul(psL[:, 0:E0], ones_row[0:1, :], rb[:], start=True, stop=False)
                for k in range(KC):
                    last = nc.tensor.matmul(psL[:, 0:E0], yT[:, k, :], rw[:, k, :], start=False,
                                            stop=(k == KC - 1))
                last.then_inc(s_logit, 1)

            def f_choose(i):
                pe.wait_ge(s_w, i + 1)
                nc.tensor.transpose(psL[0:E0, :], w[:], ident[:]).then_inc(s_wTp, 1)

            def f_mix(i):
                pe.wait_ge(s_wT, i + 1)
                pe.wait_ge(s_hT, min(NB, i + 3))
                nc.tensor.matmul(psM[:], wT[:], eb[:], start=True, stop=True).then_inc(s_mix, 1)

            def a_apply(i):
                pe.wait_ge(norms["a"]["s_out"], i + 1)
                if i >= 1:
                    pe.wait_ge(s_n_lo, i)
                transposed(psT, yt["a"], s_nTp)

            def a_project(i):
                if i == 0:
                    pe.wait_ge(s_w_lo, len(splits))
                pe.wait_ge(s_n_lo, i + 1)
                if i >= 1:
                    pe.wait_ge(s_v, i)
                for c0, c1 in ((0, QW), (QW, QKV)):
                    if before == 0:
                        nc.tensor.matmul(psQ[:, c0:c1], ones_row[0:1, :], bq[:, c0:c1], start=True, stop=False)
                    last = split_product(psQ[:, c0:c1], n_hi, n_lo, wq_hi[:, :, c0:c1], wq_lo[:, :, c0:c1], KC,
                                         before != 0)
                last.then_inc(s_qkv, 1)

            def a_low(i):
                pe.wait_ge(s_low, 2 * i + 2)
                for u in range(QK_HEADS // 8):
                    if u == 0 and i >= 1:
                        pe.wait_ge(s_ste_dve, 3 * i)
                    elif u == 1 and i >= 1:
                        pe.wait_ge(s_ste_act, 2 * i)
                    elif u >= 2 and u % 2:
                        pe.wait_ge(s_ste_act, 2 * i + u // 2)
                    elif u >= 2:
                        pe.wait_ge(s_ste_dve, 3 * i + u // 2)
                    for j in range(8):
                        last = nc.tensor.transpose(psS[u % 2][0:STACK, j, :],
                                                   stack[i % 2][:, 8 * u + j, :, :].rearrange("p s d -> p (s d)"),
                                                   identb[:])
                    last.then_inc(s_stp, 1)

            def m_apply(i):
                pe.wait_ge(norms["m"]["s_out"], i + 1)
                if i >= 1:
                    pe.wait_ge(s_mT, i)
                transposed(psT, yt["m"], s_mTp)

            def m_logits(i):
                pe.wait_ge(s_mT, i + 1)
                if i >= 1:
                    pe.wait_ge(s_ge, i)
                for k in range(KC):
                    last = nc.tensor.matmul(psG[:], yT[:, k, :], gw[:, k, :], start=(k == 0), stop=(k == KC - 1))
                last.then_inc(s_glog, 1)

            in_turns(plan, dict(d_project=d_project, f_apply=f_apply, f_logits=f_logits, f_choose=f_choose,
                                f_mix=f_mix, a_apply=a_apply, a_project=a_project, a_low=a_low, m_apply=m_apply,
                                m_logits=m_logits))


STEPS = []
for _c in range(S // 512):
    _q0 = 512 * _c
    for _kb in range(0, 4 * _c, 2):
        STEPS.append((_c, [(_kb, _q0, 512, 0), (_kb + 1, _q0, 512, 512)]))
    _d = 4 * _c
    STEPS.append((_c, [(_d, _q0, 512, 0), (_d + 1, _q0 + 128, 384, 512), (_d + 3, _q0 + 384, 128, 896)]))
    STEPS.append((_c, [(_d + 2, _q0 + 256, 256, 0)]))
N_STEPS = len(STEPS)
UNITS = [(qb, k0, min(512, (qb + 1) * P - k0), k0 // 512) for qb in range(NB) for k0 in range(0, (qb + 1) * P, 512)]
N_UNITS = REP * len(UNITS)
UNITS_WITH_STEP = [12, 4, 12, 12, 8, 0]
assert sum(UNITS_WITH_STEP) == N_UNITS and len(UNITS_WITH_STEP) == N_STEPS
P_BUFS = 3
assert N_STEPS % P_BUFS == 0


def attention_phase(nc, name, layer, const, attn, io):
    scale = SCALES[layer]
    identb, mask = const["identb"], const["mask"]
    q, k, v = attn["q"], attn["k"], attn["v"]
    with ExitStack() as ctx:
        b = Buffers(nc, ctx, name)
        sem = b.sem
        vg = b.sb("vg", [P, NB, VW])
        pt = [b.sb(f"pt{n}", [P, REP, 1024]) for n in range(P_BUFS)]
        mraw = b.sb("mraw", [P, REP * NB, 2])
        nm, m_r1, m_r2 = (b.sb(n, [P, REP * NB]) for n in ("nm", "m_r1", "m_r2"))
        m3 = b.sb("m3", [P, MROWS, REP * NB], BF16)
        mT = b.sb("mT", [MROWS * REP * NB, P], BF16)
        ob = b.sb("ob", [P, 512])
        den, rec, cx = b.sb("den", [P, 512]), b.sb("rec", [P, 512]), b.sb("cx", [P, 512])
        psU = [b.ps(f"psU{n}", [P, 512]) for n in range(2)]
        psE = [b.ps(f"psE{n}", [P, 1024]) for n in range(2)]
        psO = b.ps("psO", [P, 512])
        psX = b.ps("psX", [MROWS * REP * NB, P], BF16)
        (s_ones, s_pre, s_vg, s_unit, s_max, s_nm, s_m, s_m3, s_mTp, s_mT, s_mrow, s_sc, s_p, s_causal, s_pv, s_ob, s_den,
         s_rec, s_cx, s_out) = map(
            sem, ("s_ones", "s_pre", "s_vg", "s_unit", "s_max", "s_nm", "s_m", "s_m3", "s_mTp", "s_mT", "s_mrow", "s_sc", "s_p",
                  "s_causal", "s_pv", "s_ob", "s_den", "s_rec", "s_cx", "s_out"))
        block = ctx.enter_context(nc.Block())
        N_EXP = REP * N_STEPS
        DIAG = [n for n, (c, tiles) in enumerate(STEPS) if tiles[0][0] >= 4 * c]

        def over_groups(eng, body):
            body(0, None)
            with eng.Fori(0, NKV - 1) as g:
                body(g + 1, g)
            body(None, NKV - 1)

        @block.sync
        def _(sp):
            def body(gm, g):
                if g is not None:
                    for c in range(2):
                        sp.wait_ge(s_cx, 2 * g + c + 1)
                        apart(sp)
                        for j in range(REP):
                            sp.dma_start(io["ctx_write"][bass.ds(g * (REP * HD) + j * HD, HD), c * 512:(c + 1) * 512],
                                         cx[32 * j:32 * j + HD, :]).then_inc(s_out, 16)
                if gm is not None:
                    sp.wait_ge(s_mT, gm + 1)
                    apart(sp)
                    sp.dma_start(q[STACK:STACK + MROWS, bass.ds(gm * REP, REP), :], mT[:]).then_inc(s_mrow, 16)

            over_groups(sp, body)
            sp.wait_ge(s_out, 16 * 2 * REP * NKV)

        @block.gpsimd
        def _(pool):
            def body(gm, g):
                if g is not None:
                    apart(pool)
                    nc.gpsimd.tensor_copy(vg[:, :, 0:HD], v[:, :, bass.ds(g, 1), :].rearrange("p b a w -> p b (a w)")
                                          ).then_inc(s_vg, 1)
                    for n in DIAG:
                        pool.wait_ge(s_p, REP * (N_STEPS * g + n + 1))
                        t = pt[n % P_BUFS]
                        spots = [t[:, :, 0:1024].rearrange("p h (a w) -> p h a w", w=512)[:, :, :, 0:P], t[:, :, 896:1024]]
                        if len(STEPS[n][1]) == 1:
                            spots = [t[:, :, 0:P]]
                        for spot in spots:
                            rows = [[0, w] for w in spot.shape[1:-1]]
                            apart(pool)
                            last = nc.gpsimd.affine_select(out=spot, in_=spot, compare_op=ALU.is_ge, fill=0.0, base=0,
                                                           pattern=rows + [[1, P]], channel_multiplier=-1)
                            last.then_inc(s_causal, 1)
                if gm is not None:
                    pool.wait_ge(s_nm, gm + 1)
                    apart(pool)
                    nc.gpsimd.tensor_copy(m3[:, 0, :], nm[:]).then_inc(s_m, 1)
                    pool.wait_ge(s_m, 4 * gm + 1)
                    nc.gpsimd.tensor_tensor(m_r1[:], nm[:], m3[:, 0, :], ALU.subtract).then_inc(s_m, 1)
                    pool.wait_ge(s_m, 4 * gm + 2)
                    apart(pool)
                    nc.gpsimd.tensor_copy(m3[:, 1, :], m_r1[:]).then_inc(s_m, 1)
                    pool.wait_ge(s_m, 4 * gm + 3)
                    nc.gpsimd.tensor_tensor(m_r2[:], m_r1[:], m3[:, 1, :], ALU.subtract).then_inc(s_m, 1)
                    pool.wait_ge(s_m, 4 * gm + 4)
                    apart(pool)
                    nc.gpsimd.tensor_copy(m3[:, 2, :], m_r2[:]).then_inc(s_m3, 1)
                if g is not None:
                    pool.wait_ge(s_pv, N_STEPS * (g + 1))

            nc.gpsimd.memset(vg[:], 1.0).then_inc(s_ones, 1)
            pool.wait_ge(s_ones, 1)
            over_groups(pool, body)

        @block.scalar
        def _(act):
            def body(gm, g):
                if g is not None:
                    for n, (c, tiles) in enumerate(STEPS):
                        width = max(col + w for _, _, w, col in tiles)
                        for j in range(REP):
                            u = REP * n + j
                            act.wait_ge(s_sc, N_EXP * g + u + 1)
                            if j == 0 and n >= P_BUFS:
                                act.wait_ge(s_pv, N_STEPS * g + n - P_BUFS + 1)
                            nc.scalar.activation(pt[n % P_BUFS][:, j, 0:width], psE[u % 2][:, 0:width], ACT.Exp,
                                                 scale=scale).then_inc(s_p, 1)
                        if n == 3:
                            act.wait_ge(s_pv, N_STEPS * g + 2)
                            nc.scalar.copy(ob[:], psO[:]).then_inc(s_ob, 1)
                    act.wait_ge(s_pv, N_STEPS * (g + 1))
                    act.wait_ge(s_cx, 2 * g + 1)
                    nc.scalar.copy(ob[:], psO[:]).then_inc(s_ob, 1)
                if gm is not None:
                    act.wait_ge(s_mTp, gm + 1)
                    nc.scalar.copy(mT[:], psX[:]).then_inc(s_mT, 1)
                if g is not None:
                    act.wait_ge(s_cx, 2 * g + 2)

            over_groups(act, body)

        @block.vector
        def _(dve):
            def normalise(g, c):
                dve.wait_ge(s_ob, 2 * g + c + 1)
                apart(dve)
                nc.vector.stream_shuffle(den[:], ob[:], [HD] * 32).then_inc(s_den, 1)
                dve.wait_ge(s_den, 2 * g + c + 1)
                nc.vector.reciprocal(rec[:], den[:]).then_inc(s_rec, 1)
                dve.wait_ge(s_rec, 2 * g + c + 1)
                if c == 1:
                    dve.wait_ge(s_out, 16 * REP * (2 * g + 1))
                nc.vector.tensor_tensor(cx[:], ob[:], rec[:], ALU.mult).then_inc(s_cx, 1)

            def maxima(gm, units):
                for u in units:
                    qb, k0, nk, slot = UNITS[u % len(UNITS)]
                    dve.wait_ge(s_unit, N_UNITS * gm + u + 1)
                    nc.vector.tensor_reduce(mraw[:, (u // len(UNITS)) * NB + qb, slot:slot + 1], psU[u % 2][:, 0:nk],
                                            AX.X, ALU.max).then_inc(s_max, 1)

            def body(gm, g):
                at = 0
                for n in range(N_STEPS):
                    if gm is not None:
                        maxima(gm, range(at, at + UNITS_WITH_STEP[n]))
                        at += UNITS_WITH_STEP[n]
                    if n == N_STEPS - 2 and gm is not None:
                        dve.wait_ge(s_max, N_UNITS * (gm + 1))
                        nc.vector.tensor_reduce(nm[:], mraw[:], AX.X, ALU.max, negate=True).then_inc(s_nm, 1)
                        dve.wait_ge(s_nm, gm + 1)
                    if n == N_STEPS - 2 and g is not None:
                        normalise(g, 0)
                if g is not None:
                    normalise(g, 1)
                    dve.wait_ge(s_out, 16 * REP * (2 * g + 2))

            nc.vector.memset(mraw[:], -3e38).then_inc(s_pre, 1)
            dve.wait_ge(s_pre, 1)
            over_groups(dve, body)

        @block.tensor
        def _(pe):
            def unit(gm, u):
                j, (qb, k0, nk, _) = u // len(UNITS), UNITS[u % len(UNITS)]
                if isinstance(gm, int) and gm == 0:
                    if u >= 2:
                        pe.wait_ge(s_max, u - 1)
                else:
                    pe.wait_ge(s_max, N_UNITS * gm + u - 1)
                out = psU[u % 2]
                diagonal = k0 + nk == (qb + 1) * P
                last = nc.tensor.matmul(out[:, 0:nk], head(gm, j, qb * P, P), keys(gm, k0, nk), start=True,
                                        stop=not diagonal)
                if diagonal:
                    last = nc.tensor.matmul(out[:, nk - P:nk], identb[:], mask[:], start=False, stop=True)
                last.then_inc(s_unit, 1)

            def head(g, j, q0, n, rows=STACK):
                return q[0:rows, bass.ds(g * REP + j, 1), q0:q0 + n].rearrange("p a w -> p (a w)")

            def keys(g, k0, n, rows=STACK):
                return k[0:rows, bass.ds(g, 1), k0:k0 + n].rearrange("p a w -> p (a w)")

            def scores(g, n, j):
                u = REP * n + j
                if isinstance(g, int) or u >= 2:
                    pe.wait_ge(s_p, N_EXP * g + u - 1)
                for kb, q0, w, col in STEPS[n][1]:
                    last = nc.tensor.matmul(psE[u % 2][:, col:col + w], keys(g, kb * P, P, STACK + MROWS),
                                            head(g, j, q0, w, STACK + MROWS), start=True, stop=True)
                last.then_inc(s_sc, 1)

            def values(g, n):
                c, tiles = STEPS[n]
                if n == 0:
                    pe.wait_ge(s_vg, g + 1)
                pe.wait_ge(s_p, REP * (N_STEPS * g + n + 1))
                if n in DIAG:
                    done = sum(2 if len(STEPS[m][1]) > 1 else 1 for m in DIAG if m <= n)
                    per = sum(2 if len(STEPS[m][1]) > 1 else 1 for m in DIAG)
                    pe.wait_ge(s_causal, per * g + done)
                if n == 2:
                    pe.wait_ge(s_ob, 2 * g + 1)
                for kb, q0, w, col in tiles:
                    for j in range(REP):
                        last = nc.tensor.matmul(psO[32 * j:32 * j + 32, q0 - 512 * c:q0 - 512 * c + w], vg[:, kb, :],
                                                pt[n % P_BUFS][:, j, col:col + w], start=(kb == 0),
                                                stop=(kb == 4 * c + 2))
                last.then_inc(s_pv, 1)

            def body(gm, g):
                at = 0
                for n in range(N_STEPS):
                    per = UNITS_WITH_STEP[n] if gm is not None else 0
                    if g is not None and n == 0:
                        pe.wait_ge(s_mrow, 16 * g + 16)
                    for j in range(REP):
                        if g is not None:
                            scores(g, n, j)
                        if gm is not None:
                            for u in range(at + per * j // REP, at + per * (j + 1) // REP):
                                unit(gm, u)
                    at += per
                    if g is not None and n >= 1:
                        values(g, n - 1)
                if gm is not None:
                    pe.wait_ge(s_m3, gm + 1)
                    nc.tensor.transpose(psX[:], m3[:].rearrange("p a n -> p (a n)"), identb[:]).then_inc(s_mTp, 1)
                if g is not None:
                    values(g, N_STEPS - 1)
                    pe.wait_ge(s_ob, 2 * g + 2)

            over_groups(pe, body)


def moe_phase(nc, name, const, moe, io, out):
    x, ident, neg_half = const["x"], const["ident"], const["neg_half"]
    PAIRS = E1 // 2
    with ExitStack() as ctx:
        b = Buffers(nc, ctx, name)
        sem = b.sem
        raw_gu = [b.sb(f"raw_gu{n}", [P, KC, 2 * I1]) for n in range(2)]
        raw_dn = [b.sb(f"raw_dn{n}", [P, 2, H]) for n in range(2)]
        gu_hi = [b.sb(f"gu_hi{n}", [P, KC, 2 * I1], F32R) for n in range(2)]
        gu_lo = [b.sb(f"gu_lo{n}", [P, KC, 2 * I1], F32R) for n in range(2)]
        dn_hi = [b.sb(f"dn_hi{n}", [P, 2, H], F32R) for n in range(2)]
        dn_lo = [b.sb(f"dn_lo{n}", [P, 2, H], F32R) for n in range(2)]
        chunks = [[(raw_gu[n][:, k, :], gu_hi[n][:, k, :], gu_lo[n][:, k, :]) for k in range(KC)] +
                  [(raw_dn[n][:, k, :], dn_hi[n][:, k, :], dn_lo[n][:, k, :]) for k in range(2)] for n in range(2)]
        N_CH = len(chunks[0])
        yacc = b.sb("yacc", [P, NB, H])
        sil = [b.sb(f"sil{n}", [P, I1]) for n in range(2)]
        z = [b.sb(f"z{n}", [P, I1]) for n in range(2)]
        z_hi = [b.sb(f"z_hi{n}", [P, 2, P], F32R) for n in range(2)]
        z_lo = [b.sb(f"z_lo{n}", [P, 2, P], F32R) for n in range(2)]
        stats, mv = b.sb("stats", [P, NB, 6]), b.sb("mv", [P, NB, 2])
        ve, rstd = b.sb("ve", [P, NB, 1]), b.sb("rstd", [P, NB, 1])
        psG = [b.ps(f"psG{n}", [P, 2 * I1]) for n in range(2)]
        psZ = [b.ps(f"psZ{n}", [P, 2, P]) for n in range(2)]
        psY = [b.ps(f"psY{n}", [P, H]) for n in range(2)]
        s_w = [sem("s_w0"), sem("s_w1")]
        (s_cw1, s_y0, s_whi, s_wlo, s_gu, s_sil, s_z, s_zTp, s_zhi, s_zlo, s_y, s_acc, s_st, s_mv, s_ve, s_rstd, s_yn,
         s_fin, s_store) = map(
            sem, ("s_cw1", "s_y0", "s_whi", "s_wlo", "s_gu", "s_sil", "s_z", "s_zTp", "s_zhi", "s_zlo", "s_y", "s_acc",
                  "s_st", "s_mv", "s_ve", "s_rstd", "s_yn", "s_fin", "s_store"))
        block = ctx.enter_context(nc.Block())
        N_E = E1 + 1
        LAST = NB * N_E - 1

        def over_experts(eng, body):
            body(0, 0)
            body(1, 1)
            with eng.Fori(1, PAIRS) as pair:
                body(2 * pair, 0)
                body(2 * pair + 1, 1)
            body(E1, 0)

        def exists(u):
            return not isinstance(u, int) or u >= 0

        @block.sync
        def _(sp):
            def body(e, n):
                if not (isinstance(e, int) and e < 2):
                    sp.wait_ge(s_wlo, N_CH * e - N_CH)
                apart(sp)
                sp.dma_start(raw_gu[n][:], io["gu"][bass.ds(e, 1)].rearrange("a p k n -> p (a k) n")).then_inc(s_w[n], 16)
                sp.dma_start(raw_dn[n][:], io["dn"][bass.ds(e, 1)].rearrange("a p k n -> p (a k) n")).then_inc(s_w[n], 16)

            over_experts(sp, body)
            for i in range(NB):
                sp.wait_ge(s_fin, i + 1)
                sp.dma_start(out[:, i, :], x[:, i, :]).then_inc(s_store, 16)
            sp.wait_ge(s_store, 16 * NB)

        @block.gpsimd
        def _(pool):
            nc.gpsimd.memset(moe["cw"][:, :, E1:], 1.0).then_inc(s_cw1, 1)
            nc.gpsimd.memset(yacc[:], 0.0).then_inc(s_y0, 1)
            for i in range(NB):
                pool.wait_ge(s_mv, i + 1)
                nc.gpsimd.tensor_scalar(ve[:, i, :], mv[:, i, 1:2], EPS, 1.0, ALU.add, ALU.mult).then_inc(s_ve, 1)
                pool.wait_ge(s_ve, i + 1)
                nc.gpsimd.tensor_tensor(rstd[:, i, :], ve[:, i, :], neg_half[:], ALU.pow).then_inc(s_rstd, 1)

        @block.scalar
        def _(act):
            def split(pair, n, c):
                if c == 0:
                    act.wait_ge(s_w[n], 32 * pair + 32)
                src, hi, _ = chunks[n][c]
                nc.scalar.copy(hi, src).then_inc(s_whi, 1)

            def high_z(u, buf):
                act.wait_ge(s_zTp, u + 1)
                nc.scalar.copy(z_hi[buf][:], psZ[buf][:]).then_inc(s_zhi, 1)

            def body(e, n, pair):
                for t in range(NB):
                    u = NB * e + t
                    act.wait_ge(s_gu, u + 1)
                    nc.scalar.activation(sil[t % 2][:], psG[t % 2][:, 0:I1], ACT.Silu).then_inc(s_sil, 1)
                    if exists(u - 1):
                        high_z(u - 1, (t - 1) % 2)
                    if t < N_CH and not (isinstance(e, int) and e == E1):
                        split(pair + n, 1 - n, t)

            for c in range(N_CH):
                split(0, 0, c)
            body(0, 0, 0)
            body(1, 1, 0)
            with act.Fori(1, PAIRS) as pair:
                body(2 * pair, 0, pair)
                body(2 * pair + 1, 1, pair)
            body(E1, 0, PAIRS)
            high_z(LAST, 1)

        @block.vector
        def _(dve):
            def split(e, n, c):
                dve.wait_ge(s_whi, N_CH * e + c + 1)
                src, hi, lo = chunks[n][c]
                nc.vector.tensor_tensor(lo, src, hi.bitcast(F32), ALU.subtract).then_inc(s_wlo, 1)

            def low_z(u, buf):
                dve.wait_ge(s_zhi, u + 1)
                nc.vector.tensor_tensor(z_lo[buf][:], psZ[buf][:], z_hi[buf][:].bitcast(F32),
                                        ALU.subtract).then_inc(s_zlo, 1)

            def accumulate(u, t):
                dve.wait_ge(s_y, u + 1)
                nc.vector.tensor_tensor(yacc[:, t, :], yacc[:, t, :], psY[t % 2][:], ALU.add).then_inc(s_acc, 1)

            def final_stats(t):
                dve.wait_ge(s_acc, NB * E1 + t + 1)
                nc.vector.bn_stats(stats[:, t, :], yacc[:, t, :]).then_inc(s_st, 1)
                dve.wait_ge(s_st, t + 1)
                nc.vector.bn_aggr(mv[:, t, :], stats[:, t, :]).then_inc(s_mv, 1)

            def final_add(t):
                dve.wait_ge(s_rstd, t + 1)
                nc.vector.tensor_scalar(yacc[:, t, :], yacc[:, t, :], mv[:, t, 0:1], rstd[:, t, :], ALU.subtract,
                                        ALU.mult).then_inc(s_yn, 1)
                dve.wait_ge(s_yn, t + 1)
                nc.vector.tensor_tensor(x[:, t, :], x[:, t, :], yacc[:, t, :], ALU.add).then_inc(s_fin, 1)

            def body(e, n):
                for t in range(NB):
                    u = NB * e + t
                    dve.wait_ge(s_sil, u + 1)
                    nc.vector.scalar_tensor_tensor(
                        out=z[t % 2][:], in0=sil[t % 2][:], scalar=moe["cw"][:, t, bass.ds(e, 1)],
                        in1=psG[t % 2][:, I1:], op0=ALU.mult, op1=ALU.mult).then_inc(s_z, 1)
                    if exists(u - 1):
                        low_z(u - 1, (t - 1) % 2)
                    if exists(u - 2):
                        accumulate(u - 2, (t - 2) % NB)
                    if isinstance(e, int) and e == E1:
                        if t >= 3:
                            final_stats(t - 3)
                        if t >= 4:
                            final_add(t - 4)
                    elif t < N_CH:
                        split(e + 1, 1 - n, t)

            dve.wait_ge(s_y0, 1)
            dve.wait_ge(s_cw1, 1)
            for c in range(N_CH):
                split(0, 0, c)
            over_experts(dve, body)
            low_z(LAST, 1)
            accumulate(LAST - 1, NB - 2)
            final_stats(NB - 3)
            final_add(NB - 4)
            accumulate(LAST, NB - 1)
            final_stats(NB - 2)
            final_stats(NB - 1)
            for t in range(NB - 3, NB):
                final_add(t)
            dve.wait_ge(s_fin, NB)

        @block.tensor
        def _(pe):
            def up(e, n, t):
                u = NB * e + t
                if not (isinstance(e, int) and e == 0 and t < 2):
                    pe.wait_ge(s_z, u - 1)
                for k in range(KC):
                    for m, (a, wt) in enumerate(((moe["hi"], gu_hi[n]), (moe["hi"], gu_lo[n]), (moe["lo"], gu_hi[n]))):
                        last = nc.tensor.matmul(psG[t % 2][:], a[:, k, t * P:(t + 1) * P], wt[:, k, :],
                                                start=(k == 0 and m == 0), stop=(k == KC - 1 and m == 2))
                last.then_inc(s_gu, 1)

            def turn_z(u, buf):
                pe.wait_ge(s_z, u + 1)
                for k in range(2):
                    last = nc.tensor.transpose(psZ[buf][:, k, :], z[buf][:, k * P:(k + 1) * P], ident[:])
                last.then_inc(s_zTp, 1)

            def down(u, n, buf):
                pe.wait_ge(s_zlo, u + 1)
                if exists(u - 2):
                    pe.wait_ge(s_acc, u - 1)
                for k in range(2):
                    for m, (a, wt) in enumerate(((z_hi[buf], dn_hi[n]), (z_hi[buf], dn_lo[n]), (z_lo[buf], dn_hi[n]))):
                        last = nc.tensor.matmul(psY[buf][:], a[:, k, :], wt[:, k, :], start=(k == 0 and m == 0),
                                                stop=(k == 1 and m == 2))
                last.then_inc(s_y, 1)

            def body(e, n):
                pe.wait_ge(s_wlo, N_CH * e + N_CH)
                for t in range(NB):
                    u = NB * e + t
                    up(e, n, t)
                    if exists(u - 1):
                        turn_z(u - 1, (t - 1) % 2)
                    if exists(u - 2):
                        down(u - 2, n if t >= 2 else 1 - n, t % 2)

            over_experts(pe, body)
            turn_z(LAST, 1)
            down(LAST - 1, 0, 0)
            down(LAST, 0, 1)


def sandwich(nc, io, out):
    with ExitStack() as ctx:
        b = Buffers(nc, ctx)
        const = {
            "x": b.sb("x", [P, NB, H]), "ident": b.sb("ident", [P, P]), "identb": b.sb("identb", [P, P], BF16),
            "mask": b.sb("mask", [P, P], BF16), "ones_row": b.sb("ones_row", [1, P]),
            "neg_half": b.sb("neg_half", [P, 1]),
        }
        s_base, s_const, s_kones = b.sem("s_base"), b.sem("s_const"), b.sem("s_kones")
        io["ctx_write"] = io["ctx"].rearrange("(h r) t -> (h r) t", r=HD)
        io["ctx_read"] = io["ctx"].rearrange("(k p) t -> p k t", p=P)
        with ExitStack() as attn_ctx:
            a = Buffers(nc, attn_ctx)
            attn = {"q": a.sb("q", [STACK + MROWS, NH, S], BF16), "k": a.sb("k", [STACK + MROWS, NKV, S], BF16),
                    "v": a.sb("v", [P, NB, NKV, HD])}
            with nc.Block() as block:
                @block.gpsimd
                def _(pool):
                    nc.gpsimd.memset(const["ident"][:], 0.0).then_inc(s_base, 1)
                    nc.gpsimd.memset(const["identb"][:], 0.0).then_inc(s_base, 1)
                    nc.gpsimd.memset(const["mask"][:], 0.0).then_inc(s_base, 1)
                    nc.gpsimd.memset(const["ones_row"][:], 1.0).then_inc(s_const, 1)
                    nc.gpsimd.memset(const["neg_half"][:], -0.5).then_inc(s_const, 1)
                    pool.wait_ge(s_base, 3)
                    for m in ("ident", "identb"):
                        nc.gpsimd.affine_select(out=const[m][:], in_=const[m][:], compare_op=ALU.not_equal, fill=1.0,
                                                base=0, pattern=[[-1, P]], channel_multiplier=1).then_inc(s_const, 1)
                    nc.gpsimd.affine_select(out=const["mask"][:], in_=const["mask"][:], compare_op=ALU.is_ge, fill=NEG,
                                            base=0, pattern=[[-1, P]], channel_multiplier=1).then_inc(s_const, 1)
                    pool.wait_ge(s_const, 5)

                @block.vector
                def _(dve):
                    nc.vector.memset(attn["k"][STACK:, :, :], 1.0).then_inc(s_kones, 1)
                    dve.wait_ge(s_kones, 1)
            row_phase(nc, "a0_", const, attn, io, before=0)
            attention_phase(nc, "b0_", 0, const, attn, io)
            row_phase(nc, "c0_", const, attn, io, after=0, ffn=True, before=1)
            attention_phase(nc, "b1_", 1, const, attn, io)
        m = Buffers(nc, ctx)
        moe = {"hi": m.sb("m_hi", [P, KC, S], F32R), "lo": m.sb("m_lo", [P, KC, S], F32R),
               "cw": m.sb("cw", [P, NB, E1 + 1])}
        cw16 = {"hi": moe["hi"], "lo": moe["lo"], "cw": moe["cw"][:, :, 0:E1]}
        row_phase(nc, "c1_", const, None, io, after=1, moe=cw16)
        moe_phase(nc, "m_", const, moe, io, out)


def rope_tables(base, interleaved=False):
    half = np.arange(0, HD, 2, dtype=np.float32) / np.float32(HD)
    inv_freq = (np.float32(1.0) / np.power(np.float32(base), half)).astype(np.float32)
    angle = (np.arange(S, dtype=np.float32)[:, None] * inv_freq[None, :]).astype(np.float32)
    cos, sin = np.cos(angle), np.sin(angle)
    tables = np.concatenate([cos, cos], 1), np.concatenate([-sin, sin], 1)
    return [np.ascontiguousarray(t.astype(np.float32).reshape(NB, P, HD).transpose(1, 0, 2)) for t in tables]


def by_chunk(w):
    return np.ascontiguousarray(w.reshape(-1, P, w.shape[1]).transpose(1, 0, 2))


def kernel(**inputs):
    import concourse.bacc as _bacc
    from concourse.bass_utils import run_bass_kernel_spmd as _run

    a = {k: np.asarray(v) for k, v in inputs.items()}

    def regroup(w):
        g = w.reshape((NKV, REP + 2, HD) + w.shape[1:])
        return np.concatenate([g[:, :REP].reshape((QW,) + w.shape[1:]), g[:, REP].reshape((KW,) + w.shape[1:]),
                               g[:, REP + 1].reshape((KW,) + w.shape[1:])], 0)

    halves = np.concatenate([np.arange(0, HD, 2), np.arange(1, HD, 2)])
    qk_order = (np.arange(QK_HEADS)[:, None] * HD + halves[None, :]).reshape(-1)
    order1 = np.concatenate([qk_order, np.arange(QW + KW, QKV)])
    cos0, sin0 = rope_tables(1000000.0)
    cos1, sin1 = rope_tables(10000.0)
    gates = np.concatenate([a["L1_ffn_Wg"], a["L1_ffn_Sg"][None]], 0)
    ups = np.concatenate([a["L1_ffn_Wu"], a["L1_ffn_Su"][None]], 0)
    downs = np.concatenate([a["L1_ffn_Wd"], a["L1_ffn_Sd"][None]], 0)
    gu = np.concatenate([gates, ups], 1).transpose(0, 2, 1)
    dn = downs.transpose(0, 2, 1)
    arrays = {
        "x": a["L0_attn_hidden_states"].reshape(NB, P, H).transpose(1, 0, 2),
        "wq0": by_chunk(regroup(a["L0_attn_w_qkv"]).T),
        "bq": regroup(a["L0_attn_b_qkv"])[None],
        "wd0": by_chunk(a["L0_attn_w_dense"].T),
        "bd": a["L0_attn_b_dense"][None],
        "rw": by_chunk(a["L0_ffn_router_weight"].T),
        "rb": a["L0_ffn_router_bias"][None],
        "eb": a["L0_ffn_expert_bias"],
        "wq1": by_chunk(a["L1_attn_w_qkv"][:, order1]),
        "wd1": by_chunk(a["L1_attn_w_o"]),
        "gw": by_chunk(a["L1_ffn_gate_w"].T),
        "gb": np.broadcast_to(a["L1_ffn_bias"][None], (P, E1)),
        "gu": gu.reshape(E1 + 1, KC, P, 2 * I1).transpose(0, 2, 1, 3),
        "dn": dn.reshape(E1 + 1, 2, P, H).transpose(0, 2, 1, 3),
        "cos0": cos0, "sin0": sin0, "cos1": cos1, "sin1": sin1,
    }
    arrays = {k: np.ascontiguousarray(v) for k, v in arrays.items()}
    nc = _bacc.Bacc("TRN2", target_bir_lowering=False, num_devices=1)
    io = {k: nc.dram_tensor(f"in_{k}", v.shape, mybir.dt.from_np(v.dtype), kind="ExternalInput").ap()
          for k, v in arrays.items()}
    io["ctx"] = nc.dram_tensor("ctx_scratch", [QW, S], F32).ap()
    out = nc.dram_tensor("out_0", [P, NB, H], F32, kind="ExternalOutput").ap()
    sandwich(nc, io, out)
    r = _run(nc, [{f"in_{k}": v for k, v in arrays.items()}], core_ids=[0])
    return r.results[0]["out_0"].transpose(1, 0, 2).reshape(1, S, H)
```

```python
from contextlib import ExitStack

import numpy as np

import concourse.bass as bass
from concourse import mybir

F32 = mybir.dt.float32
F32R = mybir.dt.float32r
BF16 = mybir.dt.bfloat16
I32 = mybir.dt.int32
ALU = mybir.AluOpType
ACT = mybir.ActivationFunctionType
AX = mybir.AxisListType

P = 128
S = 1024
H = 512
NB = S // P
KC = H // P
HD = 16
NH, NKV = 32, 8
REP = NH // NKV
QW = NH * HD
KW = NKV * HD
QKV = QW + 2 * KW
QK_HEADS = NH + NKV
SLOTS = 6
STACK = SLOTS * HD
MROWS = 3
VW = 32
E0, TOP0 = 64, 8
E1, TOP1 = 16, 4
I1 = 256
WIDE = 256
N_SHARED = S // WIDE
SLOT_ROWS = E1 * S + WIDE
MAX_TILES = -(-(TOP1 * S // WIDE + E1 - 1) // 2) * 2
MIN_ROUNDS = TOP1 * S // WIDE // 2
EPS = 1e-5
NEG = -1e30
SCALES = (1.0 / HD, 1.0 / 4.0)


class Buffers:

    def __init__(self, nc, ctx, prefix=""):
        self.nc, self.ctx, self.prefix = nc, ctx, prefix
        self.semaphores = []
        ctx.callback(self.clear)

    def clear(self):
        self.nc.clear_and_free_semaphores(self.semaphores)
        self.nc.all_engine_barrier()

    def sb(self, name, shape, dt=F32):
        return self.ctx.enter_context(self.nc.sbuf_tensor(self.prefix + name, shape, dt))

    def ps(self, name, shape, dt=F32):
        return self.ctx.enter_context(self.nc.psum_tensor(self.prefix + name, shape, dt))

    def sem(self, name):
        self.semaphores.append(self.nc.alloc_semaphore(self.prefix + name))
        return self.semaphores[-1]


def apart(engine):
    engine.nop(nofuse=True)


def one(ap_of_blocks, i):
    return ap_of_blocks[:, bass.ds(i, 1), :].rearrange("p a w -> p (a w)")


class Plan:

    def __init__(self, pace, hops):
        self.pace, self.hops = pace, hops

    def slot(self, hop, i):
        return self.pace * i + self.hops.index(hop)

    def run(self, parts, chunks=(), oldest_first=True):
        for slot in range(self.pace * (NB - 1) + len(self.hops)):
            for at, work in chunks:
                if at == slot:
                    work()
            for i in range(NB) if oldest_first else reversed(range(NB)):
                hop = slot - self.pace * i
                if 0 <= hop < len(self.hops) and self.hops[hop] in parts:
                    parts[self.hops[hop]](i)

    def before(self, hop, i, other):
        return sum((self.slot(other, j), j) < (self.slot(hop, i), i) for j in range(NB))


D_HOPS = ["d_divide", "d_high", "d_low", "d_project", "d_project2", "d_stats", "d_rstd", "d_apply", "d_add"]
F_HOPS = ["f_rstd", "f_apply", "f_turn", "f_take", "f_logits", "f_max", "f_exp", "f_choose", "f_turn_w",
          "f_mix", "f_sum", "g_rstd", "g_apply", "g_add"]
A_HOPS = ["a_rstd", "a_apply", "a_turn", "a_high", "a_low", "a_project", "a_project2", "a_rope", "s_high", "s_rest", "s_middle",
          "s_rest2", "s_low", "s_turn01", "s_take01", "s_turn23", "s_take23", "s_take_k"]
M_HOPS = ["m_rstd", "m_apply", "m_turn", "m_take", "m_logits", "m_exp", "m_choose", "m_count", "m_slot", "m_scatter"]


def row_phase(nc, name, const, attn, io, after=None, ffn=False, before=None, moe=None):
    x, ident, identb, ones_row, neg_half = (const[k] for k in ("x", "ident", "identb", "ones_row", "neg_half"))
    with ExitStack() as ctx:
        b = Buffers(nc, ctx, name)
        sem = b.sem
        hops = ((D_HOPS if after is not None else []) + (F_HOPS if ffn else []) +
                (["first_stats"] if after is None else []) + (A_HOPS if before is not None else []) +
                (M_HOPS if moe is not None else []))
        plan = Plan(4, hops)
        next_norm = {"d_add": "f" if ffn else "m", "g_add": "a", "first_stats": "a"}
        kinds = [k for k, used in (("d", after is not None), ("f", ffn), ("g", ffn), ("a", before is not None),
                                   ("m", moe is not None)) if used]
        norms = {k: dict(stats=b.sb(f"st_{k}", [P, NB, 6]), mv=b.sb(f"mv_{k}", [P, NB, 2]),
                         rstd=b.sb(f"rstd_{k}", [P, NB, 1]),
                         shift=b.sb(f"shift_{k}", [P, NB, 1]), s_shift=sem(f"s_shift_{k}"),
                         s_stats=sem(f"s_stats_{k}"), s_mv=sem(f"s_mv_{k}"), s_ve=sem(f"s_ve_{k}"),
                         s_rstd=sem(f"s_rstd_{k}"), s_out=sem(f"s_out_{k}")) for k in kinds}

        s_load = sem("s_load")
        s_x = [sem(f"s_x{i}") for i in range(NB)] if after is None else None
        s_sum = sem("s_sum")
        yt = {k: b.sb(f"yt_{k}", [P, H]) for k in kinds if k in "fam"}
        yT = b.sb("yT", [P, KC, P]) if ffn or moe is not None else None
        if after is not None or before is not None:
            w_raw = [b.sb(f"w_raw{n}", [P, QKV]) for n in range(2)]
            s_w_raw = [sem(f"s_w_raw{n}") for n in range(2)]
            s_w_hi, s_w_lo = sem("s_w_hi"), sem("s_w_lo")
        splits = []
        if after is not None:
            wd_hi, wd_lo = b.sb("wd_hi", [P, KC, H], F32R), b.sb("wd_lo", [P, KC, H], F32R)
            splits += [(io[f"wd{after}"][:, k, :], wd_hi[:, k, :], wd_lo[:, k, :]) for k in range(KC)]
            bd = b.sb("bd", [1, H]) if after == 0 else None
            ctx_hi, ctx_lo = b.sb("ctx_hi", [P, KC, P], F32R), b.sb("ctx_lo", [P, KC, P], F32R)
            ctx_raw = [b.sb(f"ctx_raw{n}", [P, KC, P]) for n in range(2)]
            inv = [b.sb(f"inv{n}", [P, KC, P]) for n in range(2)]
            yd = b.sb("yd", [P, H])
            den, rden = yd[:, 0:NH * S // P], yd[:, NH * S // P:2 * NH * S // P]
            psD = b.ps("psD", [P, H])
            s_ctx = [sem("s_ctx0"), sem("s_ctx1")]
            s_inv = [sem("s_inv0"), sem("s_inv1")]
            s_den, s_rden, s_rden_out, s_ctx_n, s_ctx_hi, s_ctx_lo, s_proj = map(
                sem, ("s_den", "s_rden", "s_rden_out", "s_ctx_n", "s_ctx_hi", "s_ctx_lo", "s_proj"))
        if ffn:
            rw, rb, eb = b.sb("rw", [P, KC, E0]), b.sb("rb", [1, E0]), b.sb("eb", [E0, H])
            mx8, top8 = b.sb("mx8", [P, 8]), b.sb("top8", [P, 8])
            nmx, sm, rs, wsum = (b.sb(n, [P, NB, 1]) for n in ("nmx", "sm", "rs", "wsum"))
            ex, pn, pr, w = (b.sb(n, [P, E0]) for n in ("ex", "pn", "pr", "w"))
            wT = b.sb("wT", [E0, P])
            rw_scale = b.sb("rw_scale", [P, NB, 1])
            o0 = b.sb("o0", [P, H])
            psL = b.ps("psL", [P, P])
            psM = b.ps("psM", [P, H])
            (s_hTp, s_hT, s_logit, s_mx8, s_nmx, s_exp, s_rs, s_pn, s_top8, s_pr, s_wsum, s_w, s_wTp, s_wT, s_mix,
             s_scale, s_h2, s_o0) = map(
                sem, ("s_hTp", "s_hT", "s_logit", "s_mx8", "s_nmx", "s_exp", "s_rs", "s_pn", "s_top8", "s_pr",
                      "s_wsum", "s_w", "s_wTp", "s_wT", "s_mix", "s_scale", "s_h2", "s_o0"))
        if before is not None:
            wq_hi, wq_lo = b.sb("wq_hi", [P, KC, QKV], F32R), b.sb("wq_lo", [P, KC, QKV], F32R)
            splits += [(io[f"wq{before}"][:, k, :], wq_hi[:, k, :], wq_lo[:, k, :]) for k in range(KC)]
            bq = b.sb("bq", [1, QKV]) if before == 0 else None
            n_hi = b.sb("n_hi", [P, KC, P], F32R)
            n_lo = b.sb("n_lo", [P, KC, P], F32R)
            cos, sin = b.sb("cos", [P, NB, HD]), b.sb("sin", [P, NB, HD])
            rc, rs_, qr, rest = (b.sb(n, [P, QK_HEADS, HD]) for n in ("rc", "rs_", "qr", "rest"))
            stack = [b.sb(f"stack{n}", [P, QK_HEADS, SLOTS, HD], BF16) for n in range(2)]
            psQ = b.ps("psQ", [P, 1024])
            psS = [b.ps(f"psS{n}", [P, 8, P], BF16) for n in range(2)]
            psK = (psD if after is not None else b.ps("psK", [P, H]))[:].bitcast(BF16).rearrange("p (h t) -> p h t", t=P)
            s_kones = sem("s_kones")
            (s_nTp, s_n_hi, s_n_lo, s_qkv, s_rc, s_qr, s_v, s_high, s_r1, s_mid, s_r2, s_low,
             s_stp, s_ste_act, s_ste_dve) = map(
                sem, ("s_nTp", "s_n_hi", "s_n_lo", "s_qkv", "s_rc", "s_qr", "s_v", "s_high", "s_r1",
                      "s_mid", "s_r2", "s_low", "s_stp", "s_ste_act", "s_ste_dve"))
        if before is not None or moe is not None:
            psT = b.ps("psT", [P, KC, P])
        if moe is not None:
            gw, gb = b.sb("gw", [P, KC, E1]), b.sb("gb", [P, E1])
            psG = b.ps("psG", [P, E1])
            ge, gd, sg, gc = (b.sb(n, [P, E1]) for n in ("ge", "gd", "sg", "gc"))
            gm, cw = b.sb("gm", [P, NB, E1]), b.sb("cw", [P, NB, E1])
            tri, ebase = b.sb("tri", [P, P]), b.sb("ebase", [P, E1])
            rows_of = moe["rows_of"]
            unused = b.sb("unused", [P, SLOT_ROWS // P, 2], I32)
            place, chosen = b.sb("place", [P, E1]), b.sb("chosen", [P, E1])
            picked = b.sb("picked", [P, TOP1, E1])
            slot8 = b.sb("slot8", [P, NB, 8])
            psP = b.ps("psP", [P, E1])
            s_counts, s_pos, s_place, s_chosen, s_slot8, s_slot, s_wk, s_tab, s_rows = map(
                sem, ("s_counts", "s_pos", "s_place", "s_chosen", "s_slot8", "s_slot", "s_wk", "s_tab", "s_rows"))
            s20, g20 = b.sb("s20", [P, E1 + 4]), b.sb("g20", [P, E1 + 4])
            g8, rep8 = b.sb("g8", [P, 8]), b.sb("rep8", [P, 8])
            gsum, gden, grec = (b.sb(n, [P, NB, 1]) for n in ("gsum", "gden", "grec"))
            (s_pre, s_mTp, s_mT, s_mhi, s_mlo, s_glog, s_ge, s_gd, s_sg, s_s20, s_g8, s_rep, s_g20, s_gm, s_gc, s_gsum,
             s_gden, s_grec, s_cw) = map(
                sem, ("s_pre", "s_mTp", "s_mT", "s_mhi", "s_mlo", "s_glog", "s_ge", "s_gd", "s_sg", "s_s20", "s_g8",
                      "s_rep", "s_g20", "s_gm", "s_gc", "s_gsum", "s_gden", "s_grec", "s_cw"))

        loads = []
        if after == 0:
            loads += [(bd[:], io["bd"])]
        if ffn:
            loads += [(rw[:], io["rw"]), (rb[:], io["rb"]), (eb[:], io["eb"])]
        if before is not None:
            loads += [(cos[:], io[f"cos{before}"]), (sin[:], io[f"sin{before}"])]
            loads += [(bq[:], io["bq"])] if before == 0 else []
        if moe is not None:
            loads += [(gw[:], io["gw"]), (gb[:], io["gb"]), (tri[:], io["tri"]), (ebase[:], io["ebase"]),
                      (rows_of[:], io["rows_of"])]

        sums = []
        plan.run({h: (lambda i, h=h: sums.append((h, i))) for h in ("d_add", "g_add")})

        n_first = KC if after is not None else 0
        split_slot = [-1] * n_first + [(3 + 4 * k if after is not None else k) for k in range(len(splits) - n_first)]
        assert before is None or max(split_slot) + 1 < plan.slot("a_project", 0)

        def sums_after(stage, i):
            return sums.index((stage, i)) + 1

        block = ctx.enter_context(nc.Block())

        @block.sync
        def _(sp):
            def weights(n):
                if n >= 2:
                    sp.wait_ge(s_w_lo, n - 1)
                src = splits[n][0]
                sp.dma_start(w_raw[n % 2][:, 0:src.shape[-1]], src).then_inc(s_w_raw[n % 2], 16)

            def attended(i):
                if i >= 2:
                    sp.wait_ge(s_ctx_lo, i - 1)
                for k in range(KC):
                    heads = slice(k * (NH // KC), (k + 1) * (NH // KC))
                    src = io["rden"][heads, i * P:(i + 1) * P].unsqueeze(1).to_broadcast([NH // KC, HD, P])
                    sp.dma_start(inv[i % 2][:, k, :], src).then_inc(s_inv[i % 2], 16)
                sp.dma_start(ctx_raw[i % 2][:], io["ctx_read"][:, :, i * P:(i + 1) * P]).then_inc(s_ctx[i % 2], 16)

            if after is None:
                for n in range(2):
                    sp.dma_start(x[:, n, :], io["x"][:, n, :]).then_inc(s_x[n], 16)
                    weights(n)
                for dst, a in loads:
                    sp.dma_start(dst, a).then_inc(s_load, 16)
                for n in range(2, NB):
                    sp.dma_start(x[:, n, :], io["x"][:, n, :]).then_inc(s_x[n], 16)
                for n in range(2, len(splits)):
                    weights(n)
            else:
                sp.dma_start(den, io["den_spread"]).then_inc(s_den, 16)
                for n in range(n_first):
                    weights(n)
                    if n == 1:
                        sp.wait_ge(s_rden, 1)
                        sp.dma_start(io["rden_spread"], rden).then_inc(s_rden_out, 16)
                for dst, a in loads:
                    sp.dma_start(dst, a).then_inc(s_load, 16)
                sp.wait_ge(s_rden_out, 16)
                attended(0)
                attended(1)
                for n in range(n_first, min(len(splits), n_first + 2)):
                    weights(n)
                def normalised(i):
                    sp.wait_ge(norms["m"]["s_out"], i + 1)
                    sp.dma_start(io["rows"][i * P:(i + 1) * P, :], yt["m"][:]).then_inc(s_rows, 16)

                if moe is not None:
                    sp.wait_ge(s_pre, 4)
                    sp.dma_start(io["slots"].rearrange("(p n) a -> p n a", p=P), unused[:]).then_inc(s_tab, 16)
                for i in range(2, NB):
                    attended(i)
                    if n_first + i < len(splits):
                        weights(n_first + i)
                    if moe is not None and i >= 4:
                        normalised(i - 4)
                if moe is not None:
                    for i in range(NB - 4, NB):
                        normalised(i)
                    sp.wait_ge(s_rows, 16 * NB)

        @block.scalar
        def _(act):
            def split(n):
                src, hi, _ = splits[n]
                act.wait_ge(s_w_raw[n % 2], 16 * (n // 2 + 1))
                nc.scalar.copy(hi, w_raw[n % 2][:, 0:src.shape[-1]]).then_inc(s_w_hi, 1)

            def d_high(i):
                act.wait_ge(s_ctx_n, i + 1)
                if i >= 1:
                    act.wait_ge(s_proj, i)
                nc.scalar.copy(ctx_hi[:], ctx_raw[i % 2][:]).then_inc(s_ctx_hi, 1)

            def apply(k, out, src, i):
                n = norms[k]
                act.wait_ge(n["s_shift"], i + 1)
                nc.scalar.activation(out, src, ACT.Identity, bias=n["shift"][:, i, :],
                                     scale=n["rstd"][:, i, :]).then_inc(n["s_out"], 1)

            def d_apply(i):
                if i >= 1:
                    act.wait_ge(s_sum, sums_after("d_add", i - 1))
                apply("d", yd[:], psD[:], i)

            def f_apply(i):
                if i >= 1:
                    act.wait_ge(s_hTp, i)
                apply("f", yt["f"][:], x[:, i, :], i)

            def a_apply(i):
                if i >= 1:
                    act.wait_ge(s_nTp, i)
                apply("a", yt["a"][:], x[:, i, :], i)

            def m_apply(i):
                if i >= 1:
                    act.wait_ge(s_mTp, i)
                    act.wait_ge(s_rows, 16 * i)
                apply("m", yt["m"][:], x[:, i, :], i)

            def f_take(i):
                act.wait_ge(s_hTp, i + 1)
                if i >= 1:
                    act.wait_ge(s_logit, i)
                nc.scalar.copy(yT[:], psT[:]).then_inc(s_hT, 1)

            def f_exp(i):
                act.wait_ge(s_nmx, i + 1)
                if i >= 1:
                    act.wait_ge(s_pn, i)
                nc.scalar.activation(ex[:], psL[:, 0:E0], ACT.Exp, bias=nmx[:, i, :],
                                     accum_out=sm[:, i, :]).then_inc(s_exp, 1)

            def f_take_w(i):
                act.wait_ge(s_wTp, i + 1)
                if i >= 1:
                    act.wait_ge(s_mix, i)
                nc.scalar.copy(wT[:], psM[0:E0, 0:P]).then_inc(s_wT, 1)

            def a_high(i):
                act.wait_ge(s_nTp, i + 1)
                if i >= 1:
                    act.wait_ge(s_qkv, i)
                    act.wait_ge(s_n_lo, i)
                nc.scalar.copy(n_hi[:], psT[:]).then_inc(s_n_hi, 1)

            def s_high_(i):
                act.wait_ge(s_rc, 3 * i + 3)
                nc.scalar.copy(attn["v"][:, i, :, :],
                               psQ[:, QW + KW:QKV].rearrange("p (g d) -> p g d", d=HD)).then_inc(s_v, 1)
                act.wait_ge(s_qr, i + 1)
                if i >= 2:
                    act.wait_ge(s_stp, (i - 1) * (QK_HEADS // 8))
                st = stack[i % 2]
                nc.scalar.copy(st[:, NH:, 0, :], qr[:, NH:, :]).then_inc(s_high, 1)
                nc.scalar.copy(st[:, 0:NH, 0:3, :],
                               qr[:, 0:NH, :].unsqueeze(2).to_broadcast([P, NH, 3, HD])).then_inc(s_high, 1)
                nc.scalar.copy(st[:, NH:, 4:6, :],
                               qr[:, NH:, :].unsqueeze(2).to_broadcast([P, NKV, 2, HD])).then_inc(s_high, 1)

            def s_middle(i):
                act.wait_ge(s_r1, i + 1)
                st = stack[i % 2]
                nc.scalar.copy(st[:, 0:NH, 3:5, :],
                               rest[:, 0:NH, :].unsqueeze(2).to_broadcast([P, NH, 2, HD])).then_inc(s_mid, 1)
                nc.scalar.copy(st[:, NH:, 2:4, :],
                               rest[:, NH:, :].unsqueeze(2).to_broadcast([P, NKV, 2, HD])).then_inc(s_mid, 1)

            def s_low_(i):
                act.wait_ge(s_r2, i + 1)
                st = stack[i % 2]
                nc.scalar.copy(st[:, 0:NH, 5, :], rest[:, 0:NH, :]).then_inc(s_low, 1)
                nc.scalar.copy(st[:, NH:, 1, :], rest[:, NH:, :]).then_inc(s_low, 1)

            def take(i, u):
                act.wait_ge(s_stp, i * (QK_HEADS // 8) + u + 1)
                nc.scalar.copy(attn["q"][0:STACK, 8 * u:8 * u + 8, i * P:(i + 1) * P],
                               psS[u % 2][0:STACK, :, :]).then_inc(s_ste_act, 1)

            def m_take(i):
                act.wait_ge(s_mTp, i + 1)
                if i >= 1:
                    act.wait_ge(s_glog, i)
                    act.wait_ge(s_mlo, i)
                    act.wait_ge(s_mhi, i)
                nc.scalar.copy(yT[:], psT[:]).then_inc(s_mT, 1)

            def m_high(i):
                act.wait_ge(s_mT, i + 1)
                nc.scalar.copy(moe["hi"][:, :, i * P:(i + 1) * P], yT[:]).then_inc(s_mhi, 1)

            def m_exp(i):
                act.wait_ge(s_glog, i + 1)
                if i >= 1:
                    act.wait_ge(s_gd, i)
                nc.scalar.activation(ge[:], psG[:], ACT.Exp, scale=-1.0).then_inc(s_ge, 1)

            for n in range(n_first):
                split(n)
            plan.run(dict(d_high=d_high, d_apply=d_apply, f_apply=f_apply, g_apply=lambda i: apply("g", o0[:], o0[:], i),
                          a_apply=a_apply, m_apply=m_apply, f_take=f_take, f_exp=f_exp, f_turn_w=f_take_w, a_high=a_high,
                          s_high=s_high_, s_middle=s_middle, s_low=s_low_, s_take01=lambda i: take(i, 1),
                          s_take23=lambda i: take(i, 3), m_take=m_take, m_logits=m_high, m_exp=m_exp),
                     [(split_slot[n], lambda n=n: split(n)) for n in range(n_first, len(splits))])

        @block.gpsimd
        def _(pool):
            def rstd(k, i):
                n = norms[k]
                pool.wait_ge(n["s_mv"], i + 1)
                nc.gpsimd.tensor_scalar(n["rstd"][:, i, :], n["mv"][:, i, 1:2], EPS, 1.0, ALU.add,
                                        ALU.mult).then_inc(n["s_ve"], 1)
                pool.wait_ge(n["s_ve"], i + 1)
                nc.gpsimd.tensor_tensor(n["rstd"][:, i, :], n["rstd"][:, i, :], neg_half[:],
                                        ALU.pow).then_inc(n["s_rstd"], 1)
                pool.wait_ge(n["s_rstd"], i + 1)
                nc.gpsimd.tensor_scalar(n["shift"][:, i, :], n["mv"][:, i, 0:1], n["rstd"][:, i, :], -1.0, ALU.mult,
                                        ALU.mult).then_inc(n["s_shift"], 1)

            if moe is not None:
                nc.gpsimd.memset(s20[:, E1:], NEG).then_inc(s_pre, 1)
                nc.gpsimd.memset(rep8[:, TOP1:], NEG).then_inc(s_pre, 1)
                nc.gpsimd.memset(unused[:, :, 0:1], 0).then_inc(s_pre, 1)
                nc.gpsimd.memset(unused[:, :, 1:2], TOP1 * S).then_inc(s_pre, 1)
                nc.gpsimd.memset(moe["counts"][:, 0, :], 0.0).then_inc(s_pre, 1)
                nc.gpsimd.memset(moe["ones"][:], 1.0).then_inc(s_pre, 1)

            def m_scatter(i):
                if i == 0:
                    pool.wait_ge(s_tab, 16)
                pool.wait_ge(s_slot, i + 1)
                for k in range(TOP1):
                    at = moe["slot"][:, TOP1 * i + k:TOP1 * i + k + 1]
                    nc.gpsimd.indirect_dma_start(io["slots"], bass.IndirectOffsetOnAxis(ap=at, axis=0),
                                                 rows_of[:, TOP1 * i + k, :], None).then_inc(moe["s_scattered"], 16)

            parts = {f"{k}_rstd": (lambda i, k=k: rstd(k, i)) for k in kinds}
            plan.run(dict(parts, m_scatter=m_scatter), oldest_first=False)
            if before == 0:
                pool.wait_ge(norms["a"]["s_shift"], NB)
                nc.gpsimd.memset(attn["k"][STACK:, :, :], 1.0).then_inc(s_kones, 1)
                pool.wait_ge(s_kones, 1)

        @block.vector
        def _(dve):
            def split(n):
                src, hi, lo = splits[n]
                dve.wait_ge(s_w_hi, n + 1)
                nc.vector.tensor_tensor(lo, w_raw[n % 2][:, 0:src.shape[-1]], hi.bitcast(F32),
                                        ALU.subtract).then_inc(s_w_lo, 1)

            def stats(k, src, i):
                n = norms[k]
                nc.vector.bn_stats(n["stats"][:, i, :], src).then_inc(n["s_stats"], 1)
                dve.wait_ge(n["s_stats"], i + 1)
                nc.vector.bn_aggr(n["mv"][:, i, :], n["stats"][:, i, :]).then_inc(n["s_mv"], 1)

            def d_divide(i):
                dve.wait_ge(s_ctx[i % 2], 16 * (i // 2 + 1))
                dve.wait_ge(s_inv[i % 2], 16 * KC * (i // 2 + 1))
                nc.vector.tensor_tensor(ctx_raw[i % 2][:], ctx_raw[i % 2][:], inv[i % 2][:],
                                        ALU.mult).then_inc(s_ctx_n, 1)

            def d_low(i):
                dve.wait_ge(s_ctx_hi, i + 1)
                nc.vector.tensor_tensor(ctx_lo[:], ctx_raw[i % 2][:], ctx_hi[:].bitcast(F32),
                                        ALU.subtract).then_inc(s_ctx_lo, 1)

            def d_stats(i):
                dve.wait_ge(s_proj, i + 1)
                stats("d", psD[:], i)

            def add(k, y, i, hop):
                dve.wait_ge(norms[k]["s_out"], i + 1)
                nc.vector.tensor_tensor(x[:, i, :], x[:, i, :], y, ALU.add).then_inc(s_sum, 1)
                dve.wait_ge(s_sum, sums_after(hop, i))
                stats(next_norm[hop], x[:, i, :], i)

            def d_add(i):
                add("d", yd[:], i, "d_add")

            def f_max(i):
                dve.wait_ge(s_logit, i + 1)
                nc.vector.max(mx8[:], psL[:, 0:E0]).then_inc(s_mx8, 1)
                dve.wait_ge(s_mx8, i + 1)
                nc.vector.tensor_scalar(nmx[:, i, :], mx8[:, 0:1], -1.0, None, ALU.mult).then_inc(s_nmx, 1)

            def f_choose(i):
                dve.wait_ge(s_exp, i + 1)
                nc.vector.reciprocal(rs[:, i, :], sm[:, i, :]).then_inc(s_rs, 1)
                dve.wait_ge(s_rs, i + 1)
                nc.vector.tensor_scalar(pn[:], ex[:], rs[:, i, :], None, ALU.mult).then_inc(s_pn, 1)
                dve.wait_ge(s_pn, i + 1)
                nc.vector.max(top8[:], pn[:]).then_inc(s_top8, 1)
                dve.wait_ge(s_top8, i + 1)
                nc.vector.match_replace(pr[:], top8[:], pn[:], 0.0).then_inc(s_pr, 1)
                nc.vector.reduce_sum(wsum[:, i, :], top8[:], AX.X).then_inc(s_wsum, 1)
                dve.wait_ge(s_pr, i + 1)
                if i >= 1:
                    dve.wait_ge(s_wTp, i)
                nc.vector.tensor_tensor(w[:], pn[:], pr[:], ALU.subtract).then_inc(s_w, 1)

            def f_sum(i):
                n = norms["f"]
                dve.wait_ge(s_wsum, i + 1)
                dve.wait_ge(n["s_rstd"], i + 1)
                nc.vector.tensor_tensor(rw_scale[:, i, :], n["rstd"][:, i, :], wsum[:, i, :],
                                        ALU.mult).then_inc(s_scale, 1)
                dve.wait_ge(s_scale, i + 1)
                if i >= 1:
                    dve.wait_ge(s_sum, sums_after("g_add", i - 1))
                nc.vector.tensor_scalar(o0[:], x[:, i, :], n["mv"][:, i, 0:1], rw_scale[:, i, :], ALU.subtract,
                                        ALU.mult).then_inc(s_h2, 1)
                dve.wait_ge(s_h2, i + 1)
                dve.wait_ge(s_mix, i + 1)
                nc.vector.tensor_tensor(o0[:], psM[:], o0[:], ALU.add).then_inc(s_o0, 1)
                dve.wait_ge(s_o0, i + 1)
                stats("g", o0[:], i)

            def g_add(i):
                add("g", o0[:], i, "g_add")

            def first_stats(i):
                dve.wait_ge(s_x[i], 16)
                stats("a", x[:, i, :], i)

            def a_low(i):
                dve.wait_ge(s_n_hi, i + 1)
                if i >= 1:
                    dve.wait_ge(s_qkv, i)
                nc.vector.tensor_tensor(n_lo[:], psT[:], n_hi[:].bitcast(F32), ALU.subtract).then_inc(s_n_lo, 1)

            def a_rope(i):
                dve.wait_ge(s_qkv, i + 1)
                qk = psQ[:, 0:QW + KW].rearrange("p (h d) -> p h d", d=HD)
                if i >= 1:
                    dve.wait_ge(s_qr, i)
                for half in range(2):
                    lo, hi = half * HD // 2, (half + 1) * HD // 2
                    nc.vector.tensor_tensor(rs_[:, :, lo:hi], qk[:, :, HD // 2 - lo:HD - lo],
                                            sin[:, i:i + 1, lo:hi].to_broadcast([P, QK_HEADS, HD // 2]),
                                            ALU.mult).then_inc(s_rc, 1)
                nc.vector.tensor_tensor(rc[:], qk, cos[:, i:i + 1, :].to_broadcast([P, QK_HEADS, HD]),
                                        ALU.mult).then_inc(s_rc, 1)
                dve.wait_ge(s_rc, 3 * i + 3)
                if i >= 1:
                    dve.wait_ge(s_high, 3 * i)
                    dve.wait_ge(s_r1, i)
                nc.vector.tensor_tensor(qr[:], rc[:], rs_[:], ALU.add).then_inc(s_qr, 1)

            def s_rest(i):
                dve.wait_ge(s_high, 3 * i + 3)
                if i >= 1:
                    dve.wait_ge(s_low, 2 * i)
                nc.vector.tensor_tensor(rest[:], qr[:], stack[i % 2][:, :, 0, :], ALU.subtract).then_inc(s_r1, 1)

            def s_rest2(i):
                dve.wait_ge(s_mid, 2 * i + 2)
                nc.vector.tensor_tensor(rest[:], rest[:], stack[i % 2][:, :, 3, :], ALU.subtract).then_inc(s_r2, 1)

            def take(i, u):
                dve.wait_ge(s_stp, i * (QK_HEADS // 8) + u + 1)
                if u < NH // 8:
                    dst, src = attn["q"][0:STACK, 8 * u:8 * u + 8, i * P:(i + 1) * P], psS[u % 2][0:STACK, :, :]
                else:
                    dst, src = attn["k"][0:STACK, :, i * P:(i + 1) * P], psK[0:STACK, :, :]
                nc.vector.tensor_copy(dst, src).then_inc(s_ste_dve, 1)

            def m_low(i):
                dve.wait_ge(s_mhi, i + 1)
                nc.vector.tensor_tensor(moe["lo"][:, :, i * P:(i + 1) * P], yT[:],
                                        moe["hi"][:, :, i * P:(i + 1) * P].bitcast(F32),
                                        ALU.subtract).then_inc(s_mlo, 1)

            def m_choose(i):
                dve.wait_ge(s_ge, i + 1)
                nc.vector.tensor_scalar(gd[:], ge[:], 1.0, None, ALU.add).then_inc(s_gd, 1)
                dve.wait_ge(s_gd, i + 1)
                nc.vector.reciprocal(sg[:], gd[:]).then_inc(s_sg, 1)
                dve.wait_ge(s_sg, i + 1)
                nc.vector.tensor_tensor(s20[:, 0:E1], sg[:], gb[:], ALU.add).then_inc(s_s20, 1)
                dve.wait_ge(s_s20, i + 1)
                nc.vector.max(g8[:], s20[:]).then_inc(s_g8, 1)
                dve.wait_ge(s_g8, i + 1)
                nc.vector.tensor_copy(rep8[:, 0:TOP1], g8[:, 0:TOP1]).then_inc(s_rep, 1)
                nc.vector.reduce_sum(gsum[:, i, :], g8[:, 0:TOP1], AX.X).then_inc(s_gsum, 1)
                dve.wait_ge(s_rep, i + 1)
                nc.vector.match_replace(g20[:], rep8[:], s20[:], -3e38).then_inc(s_g20, 1)
                dve.wait_ge(s_gsum, i + 1)
                nc.vector.tensor_scalar(gden[:, i, :], gsum[:, i, :], 1e-20, None, ALU.add).then_inc(s_gden, 1)
                dve.wait_ge(s_g20, i + 1)
                nc.vector.tensor_scalar(gm[:, i, :], g20[:, 0:E1], -2e38, None, ALU.is_le).then_inc(s_gm, 1)
                dve.wait_ge(s_gden, i + 1)
                nc.vector.reciprocal(grec[:, i, :], gden[:, i, :]).then_inc(s_grec, 1)
                dve.wait_ge(s_gm, i + 1)
                nc.vector.tensor_tensor(moe["counts"][:, i + 1, :], moe["counts"][:, i, :], gm[:, i, :],
                                        ALU.add).then_inc(s_counts, 1)
                nc.vector.tensor_tensor(gc[:], gm[:, i, :], s20[:, 0:E1], ALU.mult).then_inc(s_gc, 1)
                dve.wait_ge(s_grec, i + 1)
                dve.wait_ge(s_gc, i + 1)
                nc.vector.tensor_scalar(cw[:, i, :], gc[:], grec[:, i, :], None, ALU.mult).then_inc(s_cw, 1)

            def m_slot(i):
                dve.wait_ge(s_pos, i + 1)
                nc.vector.tensor_tensor(place[:], psP[:], ebase[:], ALU.add).then_inc(s_place, 1)
                dve.wait_ge(s_place, i + 1)
                if i >= 1:
                    dve.wait_ge(s_wk, TOP1 * i)
                nc.vector.tensor_tensor(chosen[:], place[:], gm[:, i, :], ALU.mult).then_inc(s_chosen, 1)
                dve.wait_ge(s_chosen, i + 1)
                nc.vector.max(slot8[:, i, :], chosen[:]).then_inc(s_slot8, 1)
                dve.wait_ge(s_slot8, i + 1)
                nc.vector.tensor_scalar(moe["slot"][:, TOP1 * i:TOP1 * (i + 1)], slot8[:, i, 0:TOP1], -1.0, None,
                                        ALU.add).then_inc(s_slot, 1)
                dve.wait_ge(s_cw, i + 1)
                for k in range(TOP1):
                    nc.vector.scalar_tensor_tensor(
                        out=picked[:, k, :], in0=chosen[:], scalar=slot8[:, i, k:k + 1], in1=cw[:, i, :],
                        op0=ALU.is_equal, op1=ALU.mult,
                        accum_out=moe["w"][:, TOP1 * i + k:TOP1 * i + k + 1]).then_inc(s_wk, 1)

            if after is not None:
                dve.wait_ge(s_den, 16)
                nc.vector.reciprocal(rden, den).then_inc(s_rden, 1)
            for n in range(n_first):
                split(n)
            dve.wait_ge(s_load, 16 * len(loads))
            if moe is not None:
                dve.wait_ge(s_pre, 6)
            plan.run(dict(d_divide=d_divide, d_low=d_low, d_stats=d_stats, d_add=d_add, f_max=f_max,
                          f_choose=f_choose, f_sum=f_sum, g_add=g_add, first_stats=first_stats,
                          a_low=a_low, a_rope=a_rope, s_rest=s_rest, s_rest2=s_rest2, s_take01=lambda i: take(i, 0),
                          s_take23=lambda i: take(i, 2), s_take_k=lambda i: take(i, 4), m_exp=m_low,
                          m_choose=m_choose, m_slot=m_slot),
                     [(split_slot[n] + 1, lambda n=n: split(n)) for n in range(n_first, len(splits))])

        @block.tensor
        def _(pe):
            def split_product(out, a_hi, a_lo, w_hi, w_lo, chunks, open_group=True):
                for k in chunks:
                    for m, (a, wt) in enumerate(((a_hi, w_hi), (a_hi, w_lo), (a_lo, w_hi))):
                        last = nc.tensor.matmul(out, a[:, k, :], wt[:, k, :], start=open_group and k == 0 and m == 0,
                                                stop=(k == KC - 1 and m == 2))
                return last

            def transposed(out, src, signal):
                for k in range(KC):
                    last = nc.tensor.transpose(out[:, k, :], src[:, k * P:(k + 1) * P], ident[:])
                last.then_inc(signal, 1)

            def d_project(i):
                if i == 0:
                    pe.wait_ge(s_w_lo, n_first)
                pe.wait_ge(s_ctx_lo, i + 1)
                if i >= 1:
                    pe.wait_ge(norms["d"]["s_out"], i)
                if after == 0:
                    nc.tensor.matmul(psD[:], ones_row[0:1, :], bd[:], start=True, stop=False)
                split_product(psD[:], ctx_hi, ctx_lo, wd_hi, wd_lo, range(KC // 2), after != 0)

            def d_project2(i):
                split_product(psD[:], ctx_hi, ctx_lo, wd_hi, wd_lo, range(KC // 2, KC)).then_inc(s_proj, 1)

            def f_turn(i):
                pe.wait_ge(norms["f"]["s_out"], i + 1)
                done = plan.before("f_turn", i, "a_turn")
                if done:
                    pe.wait_ge(s_n_lo, done)
                transposed(psT, yt["f"], s_hTp)

            def f_logits(i):
                pe.wait_ge(s_hT, i + 1)
                if i >= 1:
                    pe.wait_ge(s_exp, i)
                nc.tensor.matmul(psL[:, 0:E0], ones_row[0:1, :], rb[:], start=True, stop=False)
                for k in range(KC):
                    last = nc.tensor.matmul(psL[:, 0:E0], yT[:, k, :], rw[:, k, :], start=False,
                                            stop=(k == KC - 1))
                last.then_inc(s_logit, 1)

            def f_turn_w(i):
                pe.wait_ge(s_w, i + 1)
                if i >= 1:
                    pe.wait_ge(s_o0, i)
                nc.tensor.transpose(psM[0:E0, 0:P], w[:], ident[:]).then_inc(s_wTp, 1)

            def f_mix(i):
                pe.wait_ge(s_wT, i + 1)
                nc.tensor.matmul(psM[:], wT[:], eb[:], start=True, stop=True).then_inc(s_mix, 1)

            def a_turn(i):
                pe.wait_ge(norms["a"]["s_out"], i + 1)
                if i >= 1:
                    pe.wait_ge(s_n_lo, i)
                if ffn:
                    pe.wait_ge(s_hT, plan.before("a_turn", i, "f_turn"))
                transposed(psT, yt["a"], s_nTp)

            def a_project(i):
                if i == 0:
                    pe.wait_ge(s_w_lo, len(splits))
                pe.wait_ge(s_n_lo, i + 1)
                if i >= 1:
                    pe.wait_ge(s_v, i)
                project_columns(0, QW)

            def project_columns(c0, c1):
                if before == 0:
                    nc.tensor.matmul(psQ[:, c0:c1], ones_row[0:1, :], bq[:, c0:c1], start=True, stop=False)
                return split_product(psQ[:, c0:c1], n_hi, n_lo, wq_hi[:, :, c0:c1], wq_lo[:, :, c0:c1], range(KC),
                                     before != 0)

            def a_project2(i):
                project_columns(QW, QKV).then_inc(s_qkv, 1)

            def turn_stack(i, u, out):
                for j in range(8):
                    last = nc.tensor.transpose(out[0:STACK, j, :],
                                               stack[i % 2][:, 8 * u + j, :, :].rearrange("p s d -> p (s d)"),
                                               identb[:])
                last.then_inc(s_stp, 1)

            def s_turn01(i):
                pe.wait_ge(s_low, 2 * i + 2)
                if i >= 1:
                    pe.wait_ge(s_ste_dve, 3 * i - 1)
                turn_stack(i, 0, psS[0])
                if i >= 1:
                    pe.wait_ge(s_ste_act, 2 * i)
                turn_stack(i, 1, psS[1])

            def s_turn23(i):
                pe.wait_ge(s_ste_dve, 3 * i + 1)
                turn_stack(i, 2, psS[0])
                pe.wait_ge(s_ste_act, 2 * i + 1)
                turn_stack(i, 3, psS[1])

            def s_turn_k(i):
                if i >= 1:
                    pe.wait_ge(s_ste_dve, 3 * i)
                elif after is not None:
                    assert plan.before("s_take23", 0, "d_apply") == NB
                    pe.wait_ge(norms["d"]["s_out"], NB)
                turn_stack(i, 4, psK)

            def m_turn(i):
                pe.wait_ge(norms["m"]["s_out"], i + 1)
                if i >= 1:
                    pe.wait_ge(s_mT, i)
                transposed(psT, yt["m"], s_mTp)

            def m_logits(i):
                pe.wait_ge(s_mT, i + 1)
                if i >= 1:
                    pe.wait_ge(s_ge, i)
                for k in range(KC):
                    last = nc.tensor.matmul(psG[:], yT[:, k, :], gw[:, k, :], start=(k == 0), stop=(k == KC - 1))
                last.then_inc(s_glog, 1)

            def m_count(i):
                pe.wait_ge(s_counts, i + 1)
                if i >= 1:
                    pe.wait_ge(s_place, i)
                nc.tensor.matmul(psP[:], tri[:], gm[:, i, :], start=True, stop=False)
                nc.tensor.matmul(psP[:], moe["ones"][:], moe["counts"][:, i, :], start=False, stop=True).then_inc(s_pos, 1)

            pe.wait_ge(s_load, 16 * len(loads))
            plan.run(dict(d_project=d_project, d_project2=d_project2, a_project2=a_project2, f_turn=f_turn, f_logits=f_logits, f_turn_w=f_turn_w, f_mix=f_mix,
                          a_turn=a_turn, a_project=a_project, s_turn01=s_turn01, s_turn23=s_turn23,
                          s_take23=s_turn_k, m_turn=m_turn, m_logits=m_logits, m_count=m_count))


STEPS = []
for _c in range(S // 512):
    _q0 = 512 * _c
    for _kb in range(0, 4 * _c, 2):
        STEPS.append((_c, [(_kb, _q0, 512, 0), (_kb + 1, _q0, 512, 512)]))
    _d = 4 * _c
    STEPS.append((_c, [(_d, _q0, 512, 0), (_d + 1, _q0 + 128, 384, 512), (_d + 3, _q0 + 384, 128, 896)]))
    STEPS.append((_c, [(_d + 2, _q0 + 256, 256, 0)]))
N_STEPS = len(STEPS)
FIRST_HALF = 2
UNITS = [(qb, k0, min(512, (qb + 1) * P - k0), k0 // 512) for qb in range(NB) for k0 in range(0, (qb + 1) * P, 512)]
N_UNITS = REP * len(UNITS)
UNITS_WITH_STEP = [11, 7, 8, 9, 9, 4]
TURN = 4
AHEAD = sum(UNITS_WITH_STEP[TURN:])
assert sum(UNITS_WITH_STEP) == N_UNITS and len(UNITS_WITH_STEP) == N_STEPS
P_BUFS = 3
assert N_STEPS % P_BUFS == 0
U_BUFS = 3
assert N_UNITS % U_BUFS == 0


def attention_phase(nc, name, layer, const, attn, io):
    scale = SCALES[layer]
    identb, mask = const["identb"], const["mask"]
    q, k, v = attn["q"], attn["k"], attn["v"]
    with ExitStack() as ctx:
        b = Buffers(nc, ctx, name)
        sem = b.sem
        vg = b.sb("vg", [P, NB, VW])
        pt = [b.sb(f"pt{n}", [P, REP, 1024]) for n in range(P_BUFS)]
        mraw = b.sb("mraw", [P, REP * NB, 2])
        nm, m_r1, m_r2 = (b.sb(n, [P, REP * NB]) for n in ("nm", "m_r1", "m_r2"))
        m3 = b.sb("m3", [P, MROWS, REP * NB], BF16)
        mT = b.sb("mT", [MROWS * REP * NB, P], BF16)
        ob = [b.sb(f"ob{n}", [P, 512]) for n in range(2)]
        psU = [b.ps(f"psU{n}", [P, 512]) for n in range(U_BUFS)]
        psE = [b.ps(f"psE{n}", [P, 1024]) for n in range(2)]
        psO = b.ps("psO", [P, 512])
        psX = psE[0][0:MROWS * REP * NB, 0:P // 2].bitcast(BF16)
        (s_ones, s_pre, s_vg, s_unit, s_max, s_nm, s_m, s_m3, s_mTp, s_mT, s_mrow, s_sc, s_p, s_causal, s_pv, s_ob) = map(
            sem, ("s_ones", "s_pre", "s_vg", "s_unit", "s_max", "s_nm", "s_m", "s_m3", "s_mTp", "s_mT", "s_mrow", "s_sc",
                  "s_p", "s_causal", "s_pv", "s_ob"))
        s_out = [sem("s_out0"), sem("s_out1")]
        block = ctx.enter_context(nc.Block())
        N_EXP = REP * N_STEPS
        OUT_DMAS = 2 * REP
        DIAG = [n for n, (c, tiles) in enumerate(STEPS) if tiles[0][0] >= 4 * c]
        SPOTS = {n: 2 if len(STEPS[n][1]) > 1 else 1 for n in DIAG}

        def over_groups(eng, prologue, body):
            prologue()
            body(0)
            with eng.Fori(1, NKV - 2) as g:
                body(g)
            body(NKV - 2)
            body(NKV - 1)

        def is_group(g):
            return not isinstance(g, int) or 0 <= g < NKV

        @block.sync
        def _(sp):
            def rows(gm):
                sp.wait_ge(s_mT, gm + 1)
                apart(sp)
                sp.dma_start(q[STACK:STACK + MROWS, bass.ds(gm * REP, REP), :], mT[:]).then_inc(s_mrow, 16)

            def store(g, c):
                sp.wait_ge(s_ob, 2 * g + c + 1)
                apart(sp)
                for j in range(REP):
                    at = slice(c * 512, (c + 1) * 512)
                    sp.dma_start(io["ctx_write"][bass.ds(g * (REP * HD) + j * HD, HD), at],
                                 ob[c][32 * j:32 * j + HD, :]).then_inc(s_out[c], 16)
                    sp.dma_start(io["den"][bass.ds(g * REP + j, 1), at],
                                 ob[c][32 * j + HD:32 * j + HD + 1, :]).then_inc(s_out[c], 16)

            def body(g):
                if is_group(g - 1):
                    store(g - 1, 1)
                store(g, 0)
                if is_group(g + 1):
                    rows(g + 1)

            over_groups(sp, lambda: rows(0), body)
            store(NKV - 1, 1)
            for c in range(2):
                sp.wait_ge(s_out[c], 16 * OUT_DMAS * NKV)

        @block.gpsimd
        def _(pool):
            def causal(g, n):
                pool.wait_ge(s_p, REP * (N_STEPS * g + n + 1))
                t = pt[n % P_BUFS]
                spots = [t[:, :, 0:1024].rearrange("p h (a w) -> p h a w", w=512)[:, :, :, 0:P], t[:, :, 896:1024]]
                if len(STEPS[n][1]) == 1:
                    spots = [t[:, :, 0:P]]
                for spot in spots:
                    rows = [[0, w] for w in spot.shape[1:-1]]
                    apart(pool)
                    nc.gpsimd.affine_select(out=spot, in_=spot, compare_op=ALU.is_ge, fill=0.0, base=0,
                                            pattern=rows + [[1, P]], channel_multiplier=-1).then_inc(s_causal, 1)

            def split_maxima(gm):
                pool.wait_ge(s_nm, gm + 1)
                if is_group(gm - 1):
                    pool.wait_ge(s_mTp, gm)
                apart(pool)
                nc.gpsimd.tensor_copy(m3[:, 0, :], nm[:]).then_inc(s_m, 1)
                pool.wait_ge(s_m, 4 * gm + 1)
                nc.gpsimd.tensor_tensor(m_r1[:], nm[:], m3[:, 0, :], ALU.subtract).then_inc(s_m, 1)
                pool.wait_ge(s_m, 4 * gm + 2)
                apart(pool)
                nc.gpsimd.tensor_copy(m3[:, 1, :], m_r1[:]).then_inc(s_m, 1)
                pool.wait_ge(s_m, 4 * gm + 3)
                nc.gpsimd.tensor_tensor(m_r2[:], m_r1[:], m3[:, 1, :], ALU.subtract).then_inc(s_m, 1)
                pool.wait_ge(s_m, 4 * gm + 4)
                apart(pool)
                nc.gpsimd.tensor_copy(m3[:, 2, :], m_r2[:]).then_inc(s_m3, 1)

            def body(g):
                if is_group(g - 1):
                    pool.wait_ge(s_pv, N_STEPS * g)
                apart(pool)
                nc.gpsimd.tensor_copy(vg[:, :, 0:HD], v[:, :, bass.ds(g, 1), :].rearrange("p b a w -> p b (a w)")
                                      ).then_inc(s_vg, 1)
                for n in DIAG:
                    if n >= TURN and n - 1 < TURN and is_group(g + 1):
                        split_maxima(g + 1)
                    causal(g, n)

            nc.gpsimd.memset(vg[:], 1.0).then_inc(s_ones, 1)
            pool.wait_ge(s_ones, 1)
            over_groups(pool, lambda: split_maxima(0), body)

        @block.scalar
        def _(act):
            def take_rows(gm):
                act.wait_ge(s_mTp, gm + 1)
                nc.scalar.copy(mT[:], psX).then_inc(s_mT, 1)

            def take_output(g, c):
                act.wait_ge(s_pv, N_STEPS * g + (N_STEPS if c else FIRST_HALF))
                if is_group(g - 1):
                    act.wait_ge(s_out[c], 16 * OUT_DMAS * g)
                nc.scalar.copy(ob[c][:], psO[:]).then_inc(s_ob, 1)

            def body(g):
                for n, (c, tiles) in enumerate(STEPS):
                    width = max(col + w for _, _, w, col in tiles)
                    for j in range(REP):
                        u = REP * n + j
                        act.wait_ge(s_sc, N_EXP * g + u + 1)
                        if j == 0 and (n >= P_BUFS or is_group(g - 1)):
                            act.wait_ge(s_pv, N_STEPS * g + n - P_BUFS + 1)
                        nc.scalar.activation(pt[n % P_BUFS][:, j, 0:width], psE[u % 2][:, 0:width], ACT.Exp,
                                             scale=scale).then_inc(s_p, 1)
                        if n == 0 and j == 0 and is_group(g - 1):
                            take_output(g - 1, 1)
                        if n == FIRST_HALF + 1 and j == 0:
                            take_output(g, 0)
                    if n == TURN and is_group(g + 1):
                        take_rows(g + 1)

            over_groups(act, lambda: take_rows(0), body)
            take_output(NKV - 1, 1)

        @block.vector
        def _(dve):
            def maxima(gm):
                for u in range(N_UNITS):
                    qb, k0, nk, slot = UNITS[u % len(UNITS)]
                    dve.wait_ge(s_unit, N_UNITS * gm + u + 1)
                    nc.vector.tensor_reduce(mraw[:, (u // len(UNITS)) * NB + qb, slot:slot + 1], psU[u % U_BUFS][:, 0:nk],
                                            AX.X, ALU.max).then_inc(s_max, 1)
                dve.wait_ge(s_max, N_UNITS * (gm + 1))
                if is_group(gm - 1):
                    dve.wait_ge(s_m3, gm)
                nc.vector.tensor_reduce(nm[:], mraw[:], AX.X, ALU.max, negate=True).then_inc(s_nm, 1)
                dve.wait_ge(s_nm, gm + 1)

            nc.vector.memset(mraw[:], -3e38).then_inc(s_pre, 1)
            dve.wait_ge(s_pre, 1)
            maxima(0)
            with dve.Fori(1, NKV) as gm:
                maxima(gm)

        @block.tensor
        def _(pe):
            def unit(gm, u):
                j, (qb, k0, nk, _) = u // len(UNITS), UNITS[u % len(UNITS)]
                if not isinstance(gm, int) or N_UNITS * gm + u >= U_BUFS:
                    pe.wait_ge(s_max, N_UNITS * gm + u - U_BUFS + 1)
                out = psU[u % U_BUFS]
                diagonal = k0 + nk == (qb + 1) * P
                last = nc.tensor.matmul(out[:, 0:nk], head(gm, j, qb * P, P), keys(gm, k0, nk), start=True,
                                        stop=not diagonal)
                if diagonal:
                    last = nc.tensor.matmul(out[:, nk - P:nk], identb[:], mask[:], start=False, stop=True)
                last.then_inc(s_unit, 1)

            def head(g, j, q0, n, rows=STACK):
                return q[0:rows, bass.ds(g * REP + j, 1), q0:q0 + n].rearrange("p a w -> p (a w)")

            def keys(g, k0, n, rows=STACK):
                return k[0:rows, bass.ds(g, 1), k0:k0 + n].rearrange("p a w -> p (a w)")

            def scores(g, n, j):
                u = REP * n + j
                if u >= 2 or is_group(g - 1):
                    pe.wait_ge(s_p, N_EXP * g + u - 1)
                if u == REP * (TURN + 1) and is_group(g + 1):
                    pe.wait_ge(s_mT, g + 2)
                for kb, q0, w, col in STEPS[n][1]:
                    last = nc.tensor.matmul(psE[u % 2][:, col:col + w], keys(g, kb * P, P, STACK + MROWS),
                                            head(g, j, q0, w, STACK + MROWS), start=True, stop=True)
                last.then_inc(s_sc, 1)

            def values(g, n, t):
                c, tiles = STEPS[n]
                if t == 0:
                    if n == 0:
                        pe.wait_ge(s_vg, g + 1)
                        if is_group(g - 1):
                            pe.wait_ge(s_ob, 2 * g)
                    if n == FIRST_HALF:
                        pe.wait_ge(s_ob, 2 * g + 1)
                    pe.wait_ge(s_p, REP * (N_STEPS * g + n + 1))
                    if n in DIAG:
                        pe.wait_ge(s_causal, sum(SPOTS.values()) * g + sum(SPOTS[m] for m in DIAG if m <= n))
                kb, q0, w, col = tiles[t]
                for j in range(REP):
                    last = nc.tensor.matmul(psO[32 * j:32 * j + 32, q0 - 512 * c:q0 - 512 * c + w], vg[:, kb, :],
                                            pt[n % P_BUFS][:, j, col:col + w], start=(kb == 0),
                                            stop=(kb == 4 * c + 2))
                if t == len(tiles) - 1:
                    last.then_inc(s_pv, 1)

            def turn_rows(gm):
                pe.wait_ge(s_m3, gm + 1)
                if is_group(gm - 1):
                    pe.wait_ge(s_p, N_EXP * (gm - 1) + REP * TURN + REP - 1)
                nc.tensor.transpose(psX, m3[:].rearrange("p a n -> p (a n)"), identb[:]).then_inc(s_mTp, 1)

            def prologue():
                for u in range(N_UNITS):
                    unit(0, u)
                for u in range(AHEAD // 2):
                    unit(1, u)
                turn_rows(0)
                for u in range(AHEAD // 2, AHEAD):
                    unit(1, u)

            def body(g):
                pe.wait_ge(s_mrow, 16 * g + 16)
                for n in range(N_STEPS):
                    work = [lambda n=n, j=j: scores(g, n, j) for j in range(REP)]
                    if n >= 1:
                        tiles = [lambda n=n, t=t: values(g, n - 1, t) for t in range(len(STEPS[n - 1][1]))]
                        if n - 1 in DIAG:
                            work += tiles
                        else:
                            work = work[0:2] + tiles[0:1] + work[2:3] + tiles[1:2] + work[3:4] + tiles[2:]
                    if n == TURN and is_group(g + 1):
                        assert n - 1 not in DIAG
                        work = work[0:2] + [work[3], work[2], work[5], lambda: turn_rows(g + 1), work[4]]
                    gm, first = (g + 1, AHEAD) if n < TURN else (g + 2, -sum(UNITS_WITH_STEP[:TURN]))
                    at = first + sum(UNITS_WITH_STEP[:n])
                    units = UNITS_WITH_STEP[n] if is_group(gm) else 0
                    for m, piece in enumerate(work):
                        piece()
                        for u in range(at + units * m // len(work), at + units * (m + 1) // len(work)):
                            unit(gm, u)
                for t in range(len(STEPS[-1][1])):
                    values(g, N_STEPS - 1, t)

            over_groups(pe, prologue, body)


def moe_phase(nc, name, const, moe, io, out):
    x, ident, neg_half = const["x"], const["ident"], const["neg_half"]
    with ExitStack() as ctx:
        b = Buffers(nc, ctx, name)
        sem = b.sem
        raw_gu = [b.sb(f"raw_gu{n}", [P, KC, 2 * I1]) for n in range(2)]
        raw_dn = [b.sb(f"raw_dn{n}", [P, 2, H]) for n in range(2)]
        gu_hi = [b.sb(f"gu_hi{n}", [P, KC, 2 * I1], F32R) for n in range(2)]
        gu_lo = [b.sb(f"gu_lo{n}", [P, KC, 2 * I1], F32R) for n in range(2)]
        dn_hi = [b.sb(f"dn_hi{n}", [P, 2, H], F32R) for n in range(2)]
        dn_lo = [b.sb(f"dn_lo{n}", [P, 2, H], F32R) for n in range(2)]
        yacc = b.sb("yacc", [P, NB, H])
        ids = [b.sb(f"ids{n}", [P, 2, 2], I32) for n in range(2)]
        ids_out = [b.sb(f"ids_out{n}", [P, 2, 2], I32) for n in range(2)]
        xg = [b.sb(f"xg{n}", [P, 2, H]) for n in range(2)]
        x_hi = [b.sb(f"x_hi{n}", [P, KC, WIDE], F32R) for n in range(2)]
        x_lo = [b.sb(f"x_lo{n}", [P, KC, WIDE], F32R) for n in range(2)]
        sil = [b.sb(f"sil{n}", [P, 2, WIDE]) for n in range(2)]
        z = [b.sb(f"z{n}", [P, 2, WIDE]) for n in range(2)]
        z_hi = [b.sb(f"z_hi{n}", [P, 2, WIDE], F32R) for n in range(2)]
        z_lo = [b.sb(f"z_lo{n}", [P, 2, WIDE], F32R) for n in range(2)]
        ysb = [b.sb(f"ysb{n}", [P, 2, H]) for n in range(2)]
        yg = [buf[:, 0:2, :] for buf in xg + ysb + raw_dn + raw_gu]
        stats, mv = b.sb("stats", [P, NB, 6]), b.sb("mv", [P, NB, 2])
        ve, rstd, shift = (b.sb(n, [P, NB, 1]) for n in ("ve", "rstd", "shift"))
        s_shift = sem("s_shift")
        uval, tri16 = b.sb("uval", [E1, MAX_TILES]), b.sb("tri16", [E1, E1])
        ones16 = b.sb("ones16", [E1, 1])
        cnt = b.sb("cnt", [E1, MAX_TILES])
        n_t = [b.sb(f"n_t{j}", [E1, MAX_TILES]) for j in range(S // WIDE)]
        flags = b.sb("flags", [E1, 3, MAX_TILES])
        row = b.sb("row", [1, 3, MAX_TILES])
        since, place, in_use = (b.sb(n, [1, MAX_TILES]) for n in ("since", "place", "in_use"))
        rounds_f = b.sb("rounds_f", [1, 1])
        table = b.sb("table", [1, 2 * MAX_TILES + 1], I32)
        psX = b.ps("psX", [P, KC, WIDE])
        psG = b.ps("psG", [P, 4, WIDE])
        psY = [b.ps(f"psY{n}", [P, H]) for n in range(2)]
        psC = b.ps("psC", [E1, 128])
        (s_plan, s_cnt, s_cntd, s_n, s_cum, s_flags, s_row, s_rowd, s_calc, s_table, s_guhi, s_gulo, s_dnhi, s_dnlo, s_xT,
         s_xhi, s_xlo, s_gu, s_sil, s_z, s_zhi, s_zlo, s_y, s_yc, s_sum, s_st, s_mv, s_ve, s_rstd, s_yn, s_fin,
         s_store, s_ones) = map(
            sem, ("s_plan", "s_cnt", "s_cntd", "s_n", "s_cum", "s_flags", "s_row", "s_rowd", "s_calc", "s_table", "s_guhi",
                  "s_gulo", "s_dnhi", "s_dnlo", "s_xT", "s_xhi", "s_xlo", "s_gu", "s_sil", "s_z", "s_zhi", "s_zlo",
                  "s_y", "s_yc", "s_sum", "s_st", "s_mv", "s_ve", "s_rstd", "s_yn", "s_fin", "s_store", "s_ones"))
        s_rg, s_rd, s_ids, s_ids_out, s_xg, s_ys = ([sem(f"{n}{m}") for m in range(2)] for n in
                                                    ("s_rg", "s_rd", "s_ids", "s_ids_out", "s_xg", "s_ys"))
        s_yg = [sem(f"s_yg{n}") for n in range(len(yg))]
        block = ctx.enter_context(nc.Block())
        PEELED = 3

        def rounds(eng):
            eng.wait_ge(s_table, 1)
            apart(eng)
            more = eng.value_load(table[0:1, 2 * MAX_TILES:], min_val=MIN_ROUNDS - PEELED,
                                  max_val=MAX_TILES // 2 - PEELED)
            return more + PEELED

        def over_tiles(eng, body):
            for v in range(N_SHARED):
                body(v, v % 2, 0, [v >= d for d in range(5)])
            last = rounds(eng)
            for v in range(N_SHARED, N_SHARED + 2 * PEELED):
                body(v, v % 2, (v - N_SHARED) // 2, [True] * 5)
            with eng.Fori(PEELED, last) as r:
                body(2 * r + N_SHARED, 0, r, [True] * 5)
                body(2 * r + N_SHARED + 1, 1, r, [True] * 5)
            for d in range(4):
                body(2 * last + N_SHARED + d, d % 2, last + d // 2, [n > d for n in range(5)])
            return last

        def shared(v):
            return isinstance(v, int) and v < N_SHARED

        def weight_set(v, par):
            return (0, 0) if shared(v) else (v - N_SHARED + 1, 1 - par)

        def slots_of(eng, v):
            at = eng.value_load(table[0:1, bass.ds(v - N_SHARED + MAX_TILES, 1)], min_val=0, max_val=SLOT_ROWS - WIDE)
            return io["slots"][bass.ds(at, WIDE), :].rearrange("(p c) a -> p c a", c=2)

        def scattered(v, par, rnd):
            return v - 4, par, rnd - 2

        def sum_of(i, k):
            return 2 * TOP1 * (i // 2) + 2 * k + i % 2 + 1

        @block.sync
        def _(sp):
            def body(v, par, rnd, exist):
                if exist[4] and not shared(v - 4):
                    w, n, w_rnd = scattered(v, par, rnd)
                    if not (isinstance(w_rnd, int) and w_rnd == 0):
                        sp.wait_ge(s_ys[n], 32 * w_rnd)
                    apart(sp)
                    sp.dma_start(ids_out[n][:], slots_of(sp, w)).then_inc(s_ids_out[n], 16)
                if exist[0] and not shared(v):
                    take_in(v, par, rnd)

            def take_in(v, par, rnd):
                g, n = weight_set(v, par)
                if not (isinstance(rnd, int) and rnd == 0):
                    sp.wait_ge(s_xg[par], 32 * rnd)
                apart(sp)
                sp.dma_start(ids[par][:], slots_of(sp, v)).then_inc(s_ids[par], 16)
                e = sp.value_load(table[0:1, bass.ds(v - N_SHARED, 1)], min_val=0, max_val=E1 - 1)
                if not (isinstance(v, int) and v == N_SHARED):
                    sp.wait_ge(s_gulo, KC * (g - 1))
                    apart(sp)
                sp.dma_start(raw_gu[n][:], io["gu"][bass.ds(e, 1)].rearrange("a p k n -> p (a k) n")).then_inc(s_rg[n], 16)
                if not (isinstance(v, int) and v == N_SHARED):
                    sp.wait_ge(s_dnlo, 2 * (g - 1))
                    apart(sp)
                sp.dma_start(raw_dn[n][:], io["dn"][bass.ds(e, 1)].rearrange("a p k n -> p (a k) n")).then_inc(s_rd[n], 16)

            sp.dma_start(uval[:], io["uval"]).then_inc(s_plan, 16)
            sp.dma_start(tri16[:], io["tri16"]).then_inc(s_plan, 16)
            sp.dma_start(raw_gu[0][:], io["gu"][E1]).then_inc(s_rg[0], 16)
            sp.dma_start(raw_dn[0][:], io["dn"][E1]).then_inc(s_rd[0], 16)
            sp.wait_ge(moe["s_scattered"], 16 * TOP1 * NB)
            last = over_tiles(sp, body)

            def result(i):
                sp.wait_ge(s_fin, i + 1)
                sp.dma_start(out[:, i, :], x[:, i, :]).then_inc(s_store, 16)

            for n in range(2):
                sp.wait_ge(s_ys[n], 32 * last)
            apart(sp)
            by_block = io["ys"].rearrange("(k b p) h -> b p k h", b=NB, p=P)
            for i in range(NB):
                for half in range(2):
                    u = 2 * i + half
                    if u >= len(yg):
                        sp.wait_ge(s_sum, sum_of(i - len(yg) // 2, 2 * half + 1))
                    sp.dma_start(yg[u % len(yg)], by_block[i][:, 2 * half:2 * half + 2, :]
                                 ).then_inc(s_yg[u % len(yg)], 16)
            for i in range(NB):
                result(i)
            sp.wait_ge(s_store, 16 * NB)

        @block.gpsimd
        def _(pool):
            def body(v, par, rnd, exist):
                if exist[0] and not shared(v):
                    gather(v, par, rnd)
                if exist[4] and not shared(v - 4):
                    w, n, w_rnd = scattered(v, par, rnd)
                    pool.wait_ge(s_ids_out[n], 16 * w_rnd + 16)
                    pool.wait_ge(s_yc, 2 * w + 2)
                    apart(pool)
                    for c in range(2):
                        nc.gpsimd.indirect_dma_start(
                            io["ys"], bass.IndirectOffsetOnAxis(ap=ids_out[n][:, c, 1:2], axis=0), ysb[n][:, c, :], None,
                            bounds_check=TOP1 * S - 1, oob_is_err=False).then_inc(s_ys[n], 16)

            def gather(v, par, rnd):
                pool.wait_ge(s_ids[par], 16 * rnd + 16)
                if not (isinstance(rnd, int) and rnd == 0):
                    pool.wait_ge(s_xT, v - N_SHARED - 1)
                apart(pool)
                for c in range(2):
                    nc.gpsimd.indirect_dma_start(xg[par][:, c, :], None, io["rows"],
                                                 bass.IndirectOffsetOnAxis(ap=ids[par][:, c, 0:1], axis=0)
                                                 ).then_inc(s_xg[par], 16)

            nc.gpsimd.memset(ones16[:], 1.0).then_inc(s_ones, 1)
            over_tiles(pool, body)
            for i in range(NB):
                pool.wait_ge(s_mv, i + 1)
                nc.gpsimd.tensor_scalar(ve[:, i, :], mv[:, i, 1:2], EPS, 1.0, ALU.add, ALU.mult).then_inc(s_ve, 1)
                pool.wait_ge(s_ve, i + 1)
                nc.gpsimd.tensor_tensor(rstd[:, i, :], ve[:, i, :], neg_half[:], ALU.pow).then_inc(s_rstd, 1)
                pool.wait_ge(s_rstd, i + 1)
                nc.gpsimd.tensor_scalar(shift[:, i, :], mv[:, i, 0:1], rstd[:, i, :], -1.0, ALU.mult,
                                        ALU.mult).then_inc(s_shift, 1)

        @block.scalar
        def _(act):
            def split_up(g, n, half_round):
                act.wait_ge(s_rg[n], 16 * half_round + 16)
                for c in range(KC):
                    nc.scalar.copy(gu_hi[n][:, c, :], raw_gu[n][:, c, :]).then_inc(s_guhi, 1)

            def split_down(g, n, half_round):
                act.wait_ge(s_rd[n], 16 * half_round + 16)
                for c in range(2):
                    nc.scalar.copy(dn_hi[n][:, c, :], raw_dn[n][:, c, :]).then_inc(s_dnhi, 1)

            def body(v, par, rnd, exist):
                new, mid, old = exist[:3]
                if new and not shared(v):
                    act.wait_ge(s_xT, v - N_SHARED + 1)
                    act.wait_ge(s_gu, v - 1)
                    nc.scalar.copy(x_hi[par][:], psX[:]).then_inc(s_xhi, 1)
                    split_up(*weight_set(v, par), rnd + par)
                if mid and not shared(v - 1):
                    act.wait_ge(s_y, 2 * v - 4)
                    split_down(*weight_set(v - 1, 1 - par), rnd)
                if mid:
                    act.wait_ge(s_gu, v)
                    nc.scalar.activation(sil[1 - par][:], psG[:, 0:2, :], ACT.Silu).then_inc(s_sil, 1)
                    act.wait_ge(s_z, v)
                    nc.scalar.copy(z_hi[1 - par][:], z[1 - par][:]).then_inc(s_zhi, 1)
                if old:
                    store = not shared(v - 2)
                    if store and not (isinstance(rnd, int) and rnd < 2):
                        act.wait_ge(s_ys[par], 32 * rnd - 32)
                    for c in range(2):
                        act.wait_ge(s_y, 2 * v - 4 + c + 1)
                        dst = ysb[par][:, c, :] if store else yacc[:, 2 * (v - 2) + c, :]
                        nc.scalar.copy(dst, psY[c][:]).then_inc(s_yc, 1)

            split_up(0, 0, 0)
            split_down(0, 0, 0)
            over_tiles(act, body)
            for i in range(NB):
                act.wait_ge(s_shift, i + 1)
                nc.scalar.activation(yacc[:, i, :], yacc[:, i, :], ACT.Identity, bias=shift[:, i, :],
                                     scale=rstd[:, i, :]).then_inc(s_yn, 1)

        @block.vector
        def _(dve):
            def split_up(g, n):
                for c in range(KC):
                    dve.wait_ge(s_guhi, KC * g + c + 1)
                    nc.vector.tensor_tensor(gu_lo[n][:, c, :], raw_gu[n][:, c, :], gu_hi[n][:, c, :].bitcast(F32),
                                            ALU.subtract).then_inc(s_gulo, 1)

            def split_down(g, n):
                for c in range(2):
                    dve.wait_ge(s_dnhi, 2 * g + c + 1)
                    nc.vector.tensor_tensor(dn_lo[n][:, c, :], raw_dn[n][:, c, :], dn_hi[n][:, c, :].bitcast(F32),
                                            ALU.subtract).then_inc(s_dnlo, 1)

            def plan_tiles():
                dve.wait_ge(s_plan, 32)
                dve.wait_ge(s_cnt, 1)
                nc.vector.tensor_copy(cnt[:], psC[:, 0:MAX_TILES]).then_inc(s_cntd, 1)
                dve.wait_ge(s_cntd, 1)
                nc.vector.tensor_scalar(n_t[0][:], cnt[:], 0.0, None, ALU.is_gt).then_inc(s_n, 1)
                for j in range(1, S // WIDE):
                    dve.wait_ge(s_n, j)
                    nc.vector.tensor_scalar(flags[:, j % 2, :], cnt[:], float(WIDE * j), None,
                                            ALU.is_gt).then_inc(s_calc, 1)
                    dve.wait_ge(s_calc, j)
                    nc.vector.tensor_tensor(n_t[j][:], n_t[j - 1][:], flags[:, j % 2, :], ALU.add).then_inc(s_n, 1)
                dve.wait_ge(s_n, S // WIDE)
                dve.wait_ge(s_cum, 1)
                nc.vector.tensor_tensor(flags[:, 0, :], psC[:, MAX_TILES:2 * MAX_TILES], uval[:],
                                        ALU.is_le).then_inc(s_flags, 1)
                dve.wait_ge(s_flags, 1)
                nc.vector.tensor_tensor(flags[:, 1, :], flags[:, 0, :], n_t[-1][:], ALU.mult).then_inc(s_flags, 1)
                nc.vector.tensor_copy(flags[:, 2, :], n_t[-1][:]).then_inc(s_flags, 1)
                dve.wait_ge(s_row, 1)
                nc.vector.tensor_copy(row[:], psC[0:1, 0:3 * MAX_TILES].rearrange("p (a u) -> p a u", a=3)
                                      ).then_inc(s_rowd, 1)
                dve.wait_ge(s_rowd, 1)
                nc.vector.tensor_scalar(table[:, 0:MAX_TILES], row[:, 0, :], float(E1 - 1), None,
                                        ALU.min).then_inc(s_rowd, 1)
                nc.vector.tensor_tensor(since[:], uval[0:1, :], row[:, 1, :], ALU.subtract).then_inc(s_rowd, 1)
                dve.wait_ge(s_rowd, 3)
                nc.vector.tensor_scalar(place[:], row[:, 0, :], float(S // WIDE), None, ALU.mult).then_inc(s_rowd, 1)
                dve.wait_ge(s_rowd, 4)
                nc.vector.tensor_tensor(in_use[:], place[:], since[:], ALU.add).then_inc(s_rowd, 1)
                dve.wait_ge(s_rowd, 5)
                nc.vector.tensor_scalar(table[:, MAX_TILES:2 * MAX_TILES], in_use[:], float(E1 * S // WIDE), float(WIDE),
                                        ALU.min, ALU.mult).then_inc(s_rowd, 1)
                dve.wait_ge(s_rowd, 6)
                nc.vector.tensor_tensor(since[:, 0:MAX_TILES // 2], uval[0:1, 0:MAX_TILES:2],
                                        row[:, 2, 0:MAX_TILES // 2], ALU.is_lt).then_inc(s_rowd, 1)
                dve.wait_ge(s_rowd, 7)
                nc.vector.reduce_sum(rounds_f[:], since[:, 0:MAX_TILES // 2], AX.X).then_inc(s_rowd, 1)
                dve.wait_ge(s_rowd, 8)
                nc.vector.tensor_scalar(table[:, 2 * MAX_TILES:], rounds_f[:], float(-PEELED), None,
                                        ALU.add).then_inc(s_table, 1)

            def body(v, par, rnd, exist):
                new, mid, old = exist[:3]
                if new and not shared(v):
                    dve.wait_ge(s_xhi, v - N_SHARED + 1)
                    nc.vector.tensor_tensor(x_lo[par][:], psX[:], x_hi[par][:].bitcast(F32),
                                            ALU.subtract).then_inc(s_xlo, 1)
                    split_up(*weight_set(v, par))
                if mid and not shared(v - 1):
                    split_down(*weight_set(v - 1, 1 - par))
                if mid:
                    dve.wait_ge(s_sil, v)
                    nc.vector.tensor_tensor(z[1 - par][:], sil[1 - par][:], psG[:, 2:4, :], ALU.mult).then_inc(s_z, 1)
                    dve.wait_ge(s_zhi, v)
                    nc.vector.tensor_tensor(z_lo[1 - par][:], z[1 - par][:], z_hi[1 - par][:].bitcast(F32),
                                            ALU.subtract).then_inc(s_zlo, 1)

            plan_tiles()
            split_up(0, 0)
            split_down(0, 0)
            over_tiles(dve, body)

            def add_choice(i, k):
                u, pair = TOP1 * i + k, (TOP1 * i + k) // 2
                dve.wait_ge(s_yg[pair % len(yg)], 16 * (pair // len(yg) + 1))
                if k >= 1:
                    dve.wait_ge(s_sum, sum_of(i, k - 1))
                nc.vector.scalar_tensor_tensor(out=yacc[:, i, :], in0=yg[pair % len(yg)][:, k % 2, :],
                                               scalar=moe["w"][:, u:u + 1], in1=yacc[:, i, :], op0=ALU.mult,
                                               op1=ALU.add).then_inc(s_sum, 1)

            def final_stats(i):
                dve.wait_ge(s_sum, sum_of(i, TOP1 - 1))
                nc.vector.bn_stats(stats[:, i, :], yacc[:, i, :]).then_inc(s_st, 1)
                dve.wait_ge(s_st, i + 1)
                nc.vector.bn_aggr(mv[:, i, :], stats[:, i, :]).then_inc(s_mv, 1)

            def final_add(i):
                dve.wait_ge(s_yn, i + 1)
                nc.vector.tensor_tensor(x[:, i, :], x[:, i, :], yacc[:, i, :], ALU.add).then_inc(s_fin, 1)

            dve.wait_ge(s_yc, 2 * N_SHARED)
            for i in range(0, NB, 2):
                for k in range(TOP1):
                    add_choice(i, k)
                    add_choice(i + 1, k)
                final_stats(i)
                final_stats(i + 1)
                if i >= 2:
                    final_add(i - 2)
                    final_add(i - 1)
            final_add(NB - 2)
            final_add(NB - 1)
            dve.wait_ge(s_fin, NB)

        @block.tensor
        def _(pe):
            def turn(v, par, rnd):
                pe.wait_ge(s_xg[par], 32 * rnd + 32)
                if not (isinstance(v, int) and v == N_SHARED):
                    pe.wait_ge(s_xlo, v - N_SHARED)
                for c in range(2):
                    for k in range(KC):
                        last = nc.tensor.transpose(psX[:, k, c * P:(c + 1) * P], xg[par][:, c, k * P:(k + 1) * P], ident[:])
                last.then_inc(s_xT, 1)

            def up(v, par):
                g, n = weight_set(v, par)
                pe.wait_ge(s_gulo, KC * g + KC)
                if shared(v):
                    hi, lo = (moe[part][:, :, v * WIDE:(v + 1) * WIDE] for part in ("hi", "lo"))
                else:
                    pe.wait_ge(s_xlo, v - N_SHARED + 1)
                    hi, lo = x_hi[par], x_lo[par]
                if not (isinstance(v, int) and v == 0):
                    pe.wait_ge(s_z, v)
                for m in range(4):
                    for k in range(KC):
                        for j, (wt, a) in enumerate(((gu_hi[n], hi), (gu_hi[n], lo), (gu_lo[n], hi))):
                            last = nc.tensor.matmul(psG[:, m, :], wt[:, k, m * P:(m + 1) * P], a[:, k, :],
                                                    start=(k == 0 and j == 0), stop=(k == KC - 1 and j == 2))
                last.then_inc(s_gu, 1)

            def down(v, par):
                g, n = weight_set(v, par)
                pe.wait_ge(s_dnlo, 2 * g + 2)
                pe.wait_ge(s_zlo, v + 1)
                if not (isinstance(v, int) and v == 0):
                    pe.wait_ge(s_yc, 2 * v)
                for c in range(2):
                    for k in range(2):
                        for j, (a, wt) in enumerate(((z_hi[par], dn_hi[n]), (z_hi[par], dn_lo[n]), (z_lo[par], dn_hi[n]))):
                            last = nc.tensor.matmul(psY[c][:], a[:, k, c * P:(c + 1) * P], wt[:, k, :],
                                                    start=(k == 0 and j == 0), stop=(k == 1 and j == 2))
                    last.then_inc(s_y, 1)

            def body(v, par, rnd, exist):
                new, mid, old = exist[:3]
                if new and not shared(v):
                    turn(v, par, rnd)
                if mid:
                    up(v - 1, 1 - par)
                if old:
                    down(v - 2, par)

            pe.wait_ge(s_plan, 32)
            pe.wait_ge(s_ones, 1)
            nc.tensor.matmul(psC[:, 0:MAX_TILES], moe["counts"][:, NB, :], moe["ones"][:, 0:MAX_TILES], start=True,
                             stop=True).then_inc(s_cnt, 1)
            pe.wait_ge(s_n, S // WIDE)
            nc.tensor.matmul(psC[:, MAX_TILES:2 * MAX_TILES], tri16[:], n_t[-1][:], start=True, stop=True).then_inc(s_cum, 1)
            pe.wait_ge(s_flags, 3)
            nc.tensor.matmul(psC[0:1, 0:3 * MAX_TILES], ones16[:], flags[:].rearrange("e a u -> e (a u)"), start=True,
                             stop=True).then_inc(s_row, 1)
            over_tiles(pe, body)


def sandwich(nc, io, out):
    with ExitStack() as ctx:
        b = Buffers(nc, ctx)
        const = {
            "x": b.sb("x", [P, NB, H]), "ident": b.sb("ident", [P, P]), "identb": b.sb("identb", [P, P], BF16),
            "mask": b.sb("mask", [P, P], BF16), "ones_row": b.sb("ones_row", [1, P]),
            "neg_half": b.sb("neg_half", [P, 1]),
        }
        s_base, s_const = b.sem("s_base"), b.sem("s_const")
        for k in ("den", "rden"):
            io[k + "_spread"] = io[k].rearrange("h (a t) -> (h a) t", t=NH * S // P)
        io["ctx_write"] = io["ctx"].rearrange("(h r) t -> (h r) t", r=HD)
        io["ctx_read"] = io["ctx"].rearrange("(k p) t -> p k t", p=P)
        with ExitStack() as attn_ctx:
            a = Buffers(nc, attn_ctx)
            attn = {"q": a.sb("q", [STACK + MROWS, NH, S], BF16), "k": a.sb("k", [STACK + MROWS, NKV, S], BF16),
                    "v": a.sb("v", [P, NB, NKV, HD])}
            with nc.Block() as block:
                @block.gpsimd
                def _(pool):
                    nc.gpsimd.memset(const["ident"][:], 0.0).then_inc(s_base, 1)
                    nc.gpsimd.memset(const["identb"][:], 0.0).then_inc(s_base, 1)
                    nc.gpsimd.memset(const["mask"][:], 0.0).then_inc(s_base, 1)
                    nc.gpsimd.memset(const["ones_row"][:], 1.0).then_inc(s_const, 1)
                    nc.gpsimd.memset(const["neg_half"][:], -0.5).then_inc(s_const, 1)
                    pool.wait_ge(s_base, 3)
                    for m in ("ident", "identb"):
                        nc.gpsimd.affine_select(out=const[m][:], in_=const[m][:], compare_op=ALU.not_equal, fill=1.0,
                                                base=0, pattern=[[-1, P]], channel_multiplier=1).then_inc(s_const, 1)
                    nc.gpsimd.affine_select(out=const["mask"][:], in_=const["mask"][:], compare_op=ALU.is_ge, fill=NEG,
                                            base=0, pattern=[[-1, P]], channel_multiplier=1).then_inc(s_const, 1)
                    pool.wait_ge(s_const, 5)
            row_phase(nc, "a0_", const, attn, io, before=0)
            attention_phase(nc, "b0_", 0, const, attn, io)
            row_phase(nc, "c0_", const, attn, io, after=0, ffn=True, before=1)
            attention_phase(nc, "b1_", 1, const, attn, io)
        m = Buffers(nc, ctx)
        moe = {"hi": m.sb("m_hi", [P, KC, S], F32R), "lo": m.sb("m_lo", [P, KC, S], F32R),
               "slot": m.sb("slot", [P, TOP1 * NB], I32), "w": m.sb("w", [P, TOP1 * NB]),
               "rows_of": m.sb("rows_of", [P, NB * TOP1, 2], I32), "s_scattered": m.sem("s_scattered"),
               "counts": m.sb("counts", [P, NB + 1, E1]), "ones": m.sb("ones", [P, P])}
        row_phase(nc, "c1_", const, None, io, after=1, moe=moe)
        moe_phase(nc, "m_", const, moe, io, out)


def rope_tables(base, interleaved=False):
    half = np.arange(0, HD, 2, dtype=np.float32) / np.float32(HD)
    inv_freq = (np.float32(1.0) / np.power(np.float32(base), half)).astype(np.float32)
    angle = (np.arange(S, dtype=np.float32)[:, None] * inv_freq[None, :]).astype(np.float32)
    cos, sin = np.cos(angle), np.sin(angle)
    tables = np.concatenate([cos, cos], 1), np.concatenate([-sin, sin], 1)
    return [np.ascontiguousarray(t.astype(np.float32).reshape(NB, P, HD).transpose(1, 0, 2)) for t in tables]


def by_chunk(w):
    return np.ascontiguousarray(w.reshape(-1, P, w.shape[1]).transpose(1, 0, 2))


def kernel(**inputs):
    import concourse.bacc as _bacc
    from concourse.bass_utils import run_bass_kernel_spmd as _run

    a = {k: np.asarray(v) for k, v in inputs.items()}

    def regroup(w):
        g = w.reshape((NKV, REP + 2, HD) + w.shape[1:])
        return np.concatenate([g[:, :REP].reshape((QW,) + w.shape[1:]), g[:, REP].reshape((KW,) + w.shape[1:]),
                               g[:, REP + 1].reshape((KW,) + w.shape[1:])], 0)

    halves = np.concatenate([np.arange(0, HD, 2), np.arange(1, HD, 2)])
    qk_order = (np.arange(QK_HEADS)[:, None] * HD + halves[None, :]).reshape(-1)
    order1 = np.concatenate([qk_order, np.arange(QW + KW, QKV)])
    cos0, sin0 = rope_tables(1000000.0)
    cos1, sin1 = rope_tables(10000.0)
    gates = np.concatenate([a["L1_ffn_Wg"], a["L1_ffn_Sg"][None]], 0)
    ups = np.concatenate([a["L1_ffn_Wu"], a["L1_ffn_Su"][None]], 0)
    downs = np.concatenate([a["L1_ffn_Wd"], a["L1_ffn_Sd"][None]], 0)
    gu = np.concatenate([gates, ups], 1).transpose(0, 2, 1)
    dn = downs.transpose(0, 2, 1)
    token = np.arange(S, dtype=np.int32).reshape(NB, P).T
    arrays = {
        "x": a["L0_attn_hidden_states"].reshape(NB, P, H).transpose(1, 0, 2),
        "wq0": by_chunk(regroup(a["L0_attn_w_qkv"]).T),
        "bq": regroup(a["L0_attn_b_qkv"])[None],
        "wd0": by_chunk(a["L0_attn_w_dense"].T),
        "bd": a["L0_attn_b_dense"][None],
        "rw": by_chunk(a["L0_ffn_router_weight"].T),
        "rb": a["L0_ffn_router_bias"][None],
        "eb": a["L0_ffn_expert_bias"],
        "wq1": by_chunk(a["L1_attn_w_qkv"][:, order1]),
        "wd1": by_chunk(a["L1_attn_w_o"]),
        "gw": by_chunk(a["L1_ffn_gate_w"].T),
        "gb": np.broadcast_to(a["L1_ffn_bias"][None], (P, E1)),
        "gu": gu.reshape(E1 + 1, KC, P, 2 * I1).transpose(0, 2, 1, 3),
        "dn": dn.reshape(E1 + 1, 2, P, H).transpose(0, 2, 1, 3),
        "tri": np.triu(np.ones((P, P), np.float32), 1),
        "tri16": np.triu(np.ones((E1, E1), np.float32)),
        "ebase": np.broadcast_to((np.arange(E1) * S + 1).astype(np.float32)[None], (P, E1)),
        "uval": np.broadcast_to(np.arange(MAX_TILES, dtype=np.float32)[None], (E1, MAX_TILES)),
        "rows_of": np.stack(np.broadcast_arrays(token[:, :, None], token[:, :, None] + S * np.arange(TOP1, dtype=np.int32)),
                            -1).reshape(P, NB * TOP1, 2),
        "cos0": cos0, "sin0": sin0, "cos1": cos1, "sin1": sin1,
    }
    arrays = {k: np.ascontiguousarray(v) for k, v in arrays.items()}
    nc = _bacc.Bacc("TRN2", target_bir_lowering=False, num_devices=1)
    io = {k: nc.dram_tensor(f"in_{k}", v.shape, mybir.dt.from_np(v.dtype), kind="ExternalInput").ap()
          for k, v in arrays.items()}
    for scratch, rows in (("ctx", QW), ("den", NH), ("rden", NH)):
        io[scratch] = nc.dram_tensor(scratch + "_scratch", [rows, S], F32).ap()
    io["rows"] = nc.dram_tensor("rows_scratch", [S, H], F32).ap()
    io["ys"] = nc.dram_tensor("ys_scratch", [TOP1 * S, H], F32).ap()
    io["slots"] = nc.dram_tensor("slots_scratch", [SLOT_ROWS, 2], I32).ap()
    out = nc.dram_tensor("out_0", [P, NB, H], F32, kind="ExternalOutput").ap()
    sandwich(nc, io, out)
    r = _run(nc, [{f"in_{k}": v for k, v in arrays.items()}], core_ids=[0])
    return r.results[0]["out_0"].transpose(1, 0, 2).reshape(1, S, H)
```
